# Optimizing a Trainium2 kernel written in Bass

```python
import numpy as np
import jax
import jax.numpy as jnp

def _softmax(x, axis=-1):
    return jax.nn.softmax(x, axis=axis)

def _gelu(x):
    return jax.nn.gelu(x, approximate=True)

def _silu(x):
    return jax.nn.silu(x)

def _sigmoid(x):
    return jax.nn.sigmoid(x)

def _layernorm(x, axis=-1, eps=1e-05):
    m = jnp.mean(x, axis=axis, keepdims=True)
    v = jnp.var(x, axis=axis, keepdims=True)
    return (x - m) / jnp.sqrt(v + eps)

def _scatter_add(tgt, idx, src, axis=0):
    return tgt.at[idx].add(src)

def _segment_sum(src, seg, n):
    return jax.ops.segment_sum(src, seg, n)
kernel_name = 'mk_decoder_preln_d2_seqx_r8_3a37de'

def setup_inputs(seed: int=0):
    np.random.seed(seed)
    _w = jnp.asarray

    def _rec_inputs():
        import jax
        import jax.numpy as jnp
        _rk = jax.random.key(seed)
        x = 7.22e-05 + 1 * jax.random.normal(jax.random.fold_in(_rk, 1), (4, 256, 256), jnp.float32)
        _lenS = 256 - jax.random.randint(jax.random.fold_in(_rk, 7), (4,), 0, max(1, 256 // 4) + 1, jnp.int32)
        _lenS2 = 256 - jax.random.randint(jax.random.fold_in(_rk, 8), (4,), 0, max(1, 256 // 4) + 1, jnp.int32)
        _ctx_1024P = jax.random.normal(jax.random.fold_in(_rk, 11), (4, 16, 128), jnp.float32)
        _ctx_1024c = jax.random.dirichlet(jax.random.fold_in(_rk, 511), 0.3 * jnp.ones((16,), jnp.float32), (4, 256))
        _ctx_1024t = jnp.einsum('bsk,bkd->bsd', _ctx_1024c, _ctx_1024P)
        _ctx_1024t = _ctx_1024t * jax.lax.rsqrt(jnp.mean(jnp.square(_ctx_1024t)) + 1e-12) * 0.953939
        ctx_1024 = -1.39393e-06 + 0.999914 * (_ctx_1024t + 0.3 * jax.random.normal(jax.random.fold_in(_rk, 611), (4, 256, 128), jnp.float32))
        fside_BxSx2_0 = jax.random.uniform(jax.random.fold_in(_rk, 12), (4, 256, 2), jnp.float32, 0.0, 0.999707)
        return (x, ctx_1024, fside_BxSx2_0)
    x, ctx_1024, fside_BxSx2_0 = _rec_inputs()

    def _L0_attn_setup():
        import jax, jax.numpy as jnp
        import numpy as np
        D_MODEL = 256
        D_STATE = 128
        D_CONV = 4
        EXPAND = 2
        HEADDIM = 64
        D_INNER = EXPAND * D_MODEL
        NHEADS = D_INNER // HEADDIM
        CONV_DIM = D_INNER + 2 * D_STATE
        IN_PROJ = 2 * D_INNER + 2 * D_STATE + NHEADS
        INTER = 704
        EPS = 1e-06
        CHUNK = 128

        def rmsnorm(x, w, eps=EPS):
            var = jnp.mean(jnp.square(x), axis=-1, keepdims=True)
            return x * jax.lax.rsqrt(var + eps) * w

        def dw_causal_conv(x, w, b):
            xt = jnp.transpose(x, (0, 2, 1))
            xt = jnp.pad(xt, ((0, 0), (0, 0), (D_CONV - 1, 0)))
            y = jax.lax.conv_general_dilated(xt, w[:, None, :], window_strides=(1,), padding='VALID', feature_group_count=w.shape[0], dimension_numbers=('NCH', 'OIH', 'NCH'))
            y = y + b[None, :, None]
            return jnp.transpose(y, (0, 2, 1))

        def segsum(x):
            T = x.shape[-1]
            xx = jnp.broadcast_to(x[..., None], (*x.shape, T))
            xx = jnp.where(jnp.tril(jnp.ones((T, T), bool), -1), xx, 0.0)
            s = jnp.cumsum(xx, axis=-2)
            return jnp.where(jnp.tril(jnp.ones((T, T), bool), 0), s, -jnp.inf)

        def ssd(x, dt, A, Bm, Cm):
            b, l, h, p = x.shape
            n = Bm.shape[-1]
            c = l // CHUNK
            xr = x.reshape(b, c, CHUNK, h, p)
            dtr = dt.reshape(b, c, CHUNK, h)
            Br = Bm.reshape(b, c, CHUNK, n)
            Cr = Cm.reshape(b, c, CHUNK, n)
            dA = jnp.transpose(dtr * A, (0, 3, 1, 2))
            A_cum = jnp.cumsum(dA, axis=-1)
            L = jnp.exp(segsum(dA))
            xdt = xr * dtr[..., None]
            Y_diag = jnp.einsum('bcln,bcsn,bhcls,bcshp->bclhp', Cr, Br, L, xdt)
            decay_states = jnp.exp(A_cum[..., -1:] - A_cum)
            states = jnp.einsum('bcln,bhcl,bclhp->bchpn', Br, decay_states, xdt)
            A_last = A_cum[..., -1]
            decay_chunk = jnp.exp(segsum(jnp.pad(A_last, ((0, 0), (0, 0), (1, 0)))))
            states_cat = jnp.concatenate([jnp.zeros_like(states[:, :1]), states], axis=1)
            new_states = jnp.einsum('bhzc,bchpn->bzhpn', decay_chunk, states_cat)
            prev = new_states[:, :-1]
            state_decay = jnp.exp(A_cum)
            Y_off = jnp.einsum('bcln,bchpn,bhcl->bclhp', Cr, prev, state_decay)
            return (Y_diag + Y_off).reshape(b, l, h, p)
        key = jax.random.key(seed)
        ks = jax.random.split(key, 10)
        B, L = (2, 256)
        s = 0.02
        return {'hidden_states': jax.random.normal(ks[0], (B, L, D_MODEL), jnp.float32), 'norm1_w': jnp.ones((D_MODEL,), jnp.float32), 'in_proj_w': jax.random.normal(ks[1], (D_MODEL, IN_PROJ), jnp.float32) * s, 'conv_w': jax.random.normal(ks[2], (CONV_DIM, D_CONV), jnp.float32) * 0.1, 'conv_b': jnp.zeros((CONV_DIM,), jnp.float32), 'dt_bias': jax.random.uniform(ks[3], (NHEADS,), jnp.float32, -4.0, -1.0), 'A_log': jnp.log(jnp.arange(1, NHEADS + 1, dtype=jnp.float32)), 'D_param': jnp.ones((NHEADS,), jnp.float32), 'mixer_norm_w': jnp.ones((D_INNER,), jnp.float32), 'out_proj_w': jax.random.normal(ks[4], (D_INNER, D_MODEL), jnp.float32) * s, 'norm2_w': jnp.ones((D_MODEL,), jnp.float32), 'gate_w': jax.random.normal(ks[5], (D_MODEL, INTER), jnp.float32) * s, 'up_w': jax.random.normal(ks[6], (D_MODEL, INTER), jnp.float32) * s, 'down_w': jax.random.normal(ks[7], (INTER, D_MODEL), jnp.float32) * s}
    _L0_attn_all = _L0_attn_setup()
    _L0_attn_in = {k: v for k, v in _L0_attn_all.items() if k in ('norm1_w', 'in_proj_w', 'conv_w', 'conv_b', 'dt_bias', 'A_log', 'D_param', 'mixer_norm_w', 'out_proj_w', 'norm2_w', 'gate_w', 'up_w', 'down_w')}
    del _L0_attn_all

    def _L0_xattn_setup():
        import jax, jax.numpy as jnp
        import numpy as np
        DIM = 256
        CTX_DIM = 128
        N_HEADS = 32
        HEAD_DIM = DIM // N_HEADS
        POS_DIM = 2
        B, N, CTXN = (2, 256, 256)
        ROPE_BASE = 10000.0

        def apply_axial_rope(x, pos):
            b, n, h, d = x.shape
            p = pos.shape[-1]
            dpa = d // p
            half = dpa // 2
            freqs = ROPE_BASE ** (-jnp.arange(half, dtype=x.dtype) / half)
            ang = pos[..., :, None] * freqs
            cos = jnp.cos(ang)[:, :, None, :, :]
            sin = jnp.sin(ang)[:, :, None, :, :]
            xr = x.reshape(b, n, h, p, half, 2)
            x1, x2 = (xr[..., 0], xr[..., 1])
            out = jnp.stack([x1 * cos - x2 * sin, x1 * sin + x2 * cos], axis=-1)
            return out.reshape(b, n, h, d)
        key = jax.random.key(seed)
        ks = jax.random.split(key, 8)
        x = jax.random.normal(ks[0], (B, N, DIM), jnp.float32)
        ctx = jax.random.normal(ks[1], (B, CTXN, CTX_DIM), jnp.float32)
        pos_map = jax.random.uniform(ks[2], (B, N, POS_DIM), jnp.float32)
        ctx_pos_map = jax.random.uniform(ks[3], (B, CTXN, POS_DIM), jnp.float32)
        Wq = jax.random.normal(ks[4], (DIM, DIM), jnp.float32) / np.sqrt(DIM)
        Wkv = jax.random.normal(ks[5], (CTX_DIM, 2 * DIM), jnp.float32) / np.sqrt(CTX_DIM)
        Wout = jax.random.normal(ks[6], (DIM, DIM), jnp.float32) / np.sqrt(DIM)
        bout = jnp.zeros((DIM,), jnp.float32)
        return {'x': x, 'ctx': ctx, 'pos_map': pos_map, 'ctx_pos_map': ctx_pos_map, 'Wq': Wq, 'Wkv': Wkv, 'Wout': Wout, 'bout': bout}
    _L0_xattn_all = _L0_xattn_setup()
    _L0_xattn_in = {k: v for k, v in _L0_xattn_all.items() if k in ('Wq', 'Wkv', 'Wout', 'bout')}
    del _L0_xattn_all

    def _L0_ffn_setup():
        import jax, jax.numpy as jnp
        import numpy as np
        IN_F, OUT_F = (256, 256)
        N_EXPERTS, RANK, TOP_K = (8, 128, 2)
        key = jax.random.key(seed)
        k_x, k_r, k_a, k_b = jax.random.split(key, 4)
        hidden_states = jax.random.normal(k_x, (4, 512, IN_F), dtype=jnp.float32)
        router_w = jax.random.normal(k_r, (IN_F, N_EXPERTS), dtype=jnp.float32) * IN_F ** (-0.5)
        Wa = jax.random.normal(k_a, (N_EXPERTS, IN_F, RANK), dtype=jnp.float32) * IN_F ** (-0.5)
        Wb = jax.random.normal(k_b, (N_EXPERTS, RANK, OUT_F), dtype=jnp.float32) * RANK ** (-0.5)
        return {'hidden_states': hidden_states, 'router_w': router_w, 'Wa': Wa, 'Wb': Wb}
    _L0_ffn_all = _L0_ffn_setup()
    _L0_ffn_in = {k: v for k, v in _L0_ffn_all.items() if k in ('router_w', 'Wa', 'Wb')}
    del _L0_ffn_all

    def _L1_attn_setup():
        import jax, jax.numpy as jnp
        import numpy as np
        H, D, R, S, K, EV = (8, 32, 6, 2, 2, 2)
        HID = 256
        DV = D * EV
        KEY_DIM = H * D
        VAL_DIM = KEY_DIM * EV
        key = jax.random.key(seed)
        ks = jax.random.split(key, 9)
        b, t = (2, 128)

        def lin(k, fan_in, shape):
            return jax.random.normal(k, shape, jnp.float32) * fan_in ** (-0.5)
        return {'hidden_states': jax.random.normal(ks[0], (b, t, HID), jnp.float32), 'Wq': lin(ks[1], HID, (HID, KEY_DIM)), 'Wk': lin(ks[2], HID, (HID, KEY_DIM)), 'Wv': lin(ks[3], HID, (HID, VAL_DIM)), 'Wq_exp': lin(ks[4], D, (H, D, D * R)), 'Wk_exp': lin(ks[5], D, (H, D, D * R)), 'Wgate': lin(ks[6], D, (D, R - S)), 'Wg': lin(ks[7], HID, (HID, VAL_DIM)), 'Wo': lin(ks[8], VAL_DIM, (VAL_DIM, HID))}
    _L1_attn_all = _L1_attn_setup()
    _L1_attn_in = {k: v for k, v in _L1_attn_all.items() if k in ('Wq', 'Wk', 'Wv', 'Wq_exp', 'Wk_exp', 'Wgate', 'Wg', 'Wo')}
    del _L1_attn_all

    def _L1_xattn_setup():
        import jax, jax.numpy as jnp
        import numpy as np
        key = jax.random.key(seed)
        ks = jax.random.split(key, 6)
        B, L, N, C, D = (8, 64, 256, 128, 128)
        return {'teacher_logits': jax.random.normal(ks[0], (B, L, N), dtype=jnp.float32), 'teacher_features': jax.random.normal(ks[1], (B, N, C), dtype=jnp.float32), 'Wq': jax.random.normal(ks[2], (D, C), dtype=jnp.float32) * (1.0 / np.sqrt(C)), 'bq': jnp.zeros((D,), dtype=jnp.float32), 'Wk': jax.random.normal(ks[3], (D, C), dtype=jnp.float32) * (1.0 / np.sqrt(C)), 'bk': jnp.zeros((D,), dtype=jnp.float32)}
    _L1_xattn_all = _L1_xattn_setup()
    _L1_xattn_in = {k: v for k, v in _L1_xattn_all.items() if k in ('Wq', 'bq', 'Wk', 'bk')}
    del _L1_xattn_all

    def _L1_ffn_setup():
        import jax, jax.numpy as jnp
        import numpy as np
        B, S, H = (2, 256, 256)
        E, G, TKG, K = (32, 8, 4, 8)
        I, SI = (128, 256)
        ROUTED_SCALE = 2.5

        def _moe_forward(hidden_states, router_w, router_bias, w_gate, w_up, w_down, sw_gate, sw_up, sw_down):
            x = hidden_states.reshape(-1, H)
            T = x.shape[0]
            logits = x.astype(jnp.float32) @ router_w.astype(jnp.float32)
            scores = jax.nn.sigmoid(logits)
            scores_grouped = (scores + router_bias).reshape(T, G, E // G)
            top2, _ = jax.lax.top_k(scores_grouped, 2)
            group_scores = top2.sum(-1)
            _, top_groups = jax.lax.top_k(group_scores, TKG)
            mask = jnp.ones((T, G), bool).at[jnp.arange(T)[:, None], top_groups].set(False)
            masked = jnp.where(mask[:, :, None], 0.0, scores_grouped).reshape(T, E)
            _, top_k_index = jax.lax.top_k(masked, K)
            tkw = jnp.take_along_axis(scores, top_k_index, axis=-1)
            tkw = tkw / tkw.sum(-1, keepdims=True)
            tkw = (tkw * ROUTED_SCALE).astype(hidden_states.dtype)
            flat_idx = top_k_index.reshape(-1)
            sort_idx = jnp.argsort(flat_idx)
            xs = jnp.repeat(x, K, axis=0)[sort_idx]
            group_sizes = jnp.bincount(flat_idx, length=E).astype(jnp.int32)
            gate = jax.lax.ragged_dot(xs, w_gate, group_sizes)
            up = jax.lax.ragged_dot(xs, w_up, group_sizes)
            down = jax.lax.ragged_dot(jax.nn.silu(gate) * up, w_down, group_sizes)
            unsort = jnp.argsort(sort_idx)
            routed = (down[unsort].reshape(T, K, H) * tkw[..., None]).sum(axis=1)
            shared = jax.nn.silu(x @ sw_gate) * (x @ sw_up) @ sw_down
            return (routed + shared).reshape(hidden_states.shape)
        key = jax.random.key(seed)
        ks = jax.random.split(key, 9)

        def w(k, shape, fan_in):
            return jax.random.normal(k, shape, jnp.float32) / np.float32(np.sqrt(fan_in))
        return dict(hidden_states=jax.random.normal(ks[0], (B, S, H), jnp.float32), router_w=w(ks[1], (H, E), H), router_bias=jnp.zeros((E,), jnp.float32), w_gate=w(ks[2], (E, H, I), H), w_up=w(ks[3], (E, H, I), H), w_down=w(ks[4], (E, I, H), I), sw_gate=w(ks[5], (H, SI), H), sw_up=w(ks[6], (H, SI), H), sw_down=w(ks[7], (SI, H), SI))
    _L1_ffn_all = _L1_ffn_setup()
    _L1_ffn_in = {k: v for k, v in _L1_ffn_all.items() if k in ('router_w', 'router_bias', 'w_gate', 'w_up', 'w_down', 'sw_gate', 'sw_up', 'sw_down')}
    del _L1_ffn_all
    return {'x': x, 'ctx_1024': ctx_1024, 'fside_BxSx2_0': fside_BxSx2_0, 'L0_attn_norm1_w': _L0_attn_in['norm1_w'], 'L0_attn_in_proj_w': _L0_attn_in['in_proj_w'], 'L0_attn_conv_w': _L0_attn_in['conv_w'], 'L0_attn_conv_b': _L0_attn_in['conv_b'], 'L0_attn_dt_bias': _L0_attn_in['dt_bias'], 'L0_attn_A_log': _L0_attn_in['A_log'], 'L0_attn_D_param': _L0_attn_in['D_param'], 'L0_attn_mixer_norm_w': _L0_attn_in['mixer_norm_w'], 'L0_attn_out_proj_w': _L0_attn_in['out_proj_w'], 'L0_attn_norm2_w': _L0_attn_in['norm2_w'], 'L0_attn_gate_w': _L0_attn_in['gate_w'], 'L0_attn_up_w': _L0_attn_in['up_w'], 'L0_attn_down_w': _L0_attn_in['down_w'], 'L0_xattn_Wq': _L0_xattn_in['Wq'], 'L0_xattn_Wkv': _L0_xattn_in['Wkv'], 'L0_xattn_Wout': _L0_xattn_in['Wout'], 'L0_xattn_bout': _L0_xattn_in['bout'], 'L0_ffn_router_w': _L0_ffn_in['router_w'], 'L0_ffn_Wa': _L0_ffn_in['Wa'], 'L0_ffn_Wb': _L0_ffn_in['Wb'], 'L1_attn_Wq': _L1_attn_in['Wq'], 'L1_attn_Wk': _L1_attn_in['Wk'], 'L1_attn_Wv': _L1_attn_in['Wv'], 'L1_attn_Wq_exp': _L1_attn_in['Wq_exp'], 'L1_attn_Wk_exp': _L1_attn_in['Wk_exp'], 'L1_attn_Wgate': _L1_attn_in['Wgate'], 'L1_attn_Wg': _L1_attn_in['Wg'], 'L1_attn_Wo': _L1_attn_in['Wo'], 'L1_xattn_Wq': _L1_xattn_in['Wq'], 'L1_xattn_bq': _L1_xattn_in['bq'], 'L1_xattn_Wk': _L1_xattn_in['Wk'], 'L1_xattn_bk': _L1_xattn_in['bk'], 'L1_ffn_router_w': _L1_ffn_in['router_w'], 'L1_ffn_router_bias': _L1_ffn_in['router_bias'], 'L1_ffn_w_gate': _L1_ffn_in['w_gate'], 'L1_ffn_w_up': _L1_ffn_in['w_up'], 'L1_ffn_w_down': _L1_ffn_in['w_down'], 'L1_ffn_sw_gate': _L1_ffn_in['sw_gate'], 'L1_ffn_sw_up': _L1_ffn_in['sw_up'], 'L1_ffn_sw_down': _L1_ffn_in['sw_down']}

def reference(x, ctx_1024, fside_BxSx2_0, L0_attn_norm1_w, L0_attn_in_proj_w, L0_attn_conv_w, L0_attn_conv_b, L0_attn_dt_bias, L0_attn_A_log, L0_attn_D_param, L0_attn_mixer_norm_w, L0_attn_out_proj_w, L0_attn_norm2_w, L0_attn_gate_w, L0_attn_up_w, L0_attn_down_w, L0_xattn_Wq, L0_xattn_Wkv, L0_xattn_Wout, L0_xattn_bout, L0_ffn_router_w, L0_ffn_Wa, L0_ffn_Wb, L1_attn_Wq, L1_attn_Wk, L1_attn_Wv, L1_attn_Wq_exp, L1_attn_Wk_exp, L1_attn_Wgate, L1_attn_Wg, L1_attn_Wo, L1_xattn_Wq, L1_xattn_bq, L1_xattn_Wk, L1_xattn_bk, L1_ffn_router_w, L1_ffn_router_bias, L1_ffn_w_gate, L1_ffn_w_up, L1_ffn_w_down, L1_ffn_sw_gate, L1_ffn_sw_up, L1_ffn_sw_down):
    import jax
    import jax.numpy as jnp

    def _L0_attn_ref(hidden_states, norm1_w, in_proj_w, conv_w, conv_b, dt_bias, A_log, D_param, mixer_norm_w, out_proj_w, norm2_w, gate_w, up_w, down_w):
        import jax, jax.numpy as jnp
        import numpy as np
        D_MODEL = 256
        D_STATE = 128
        D_CONV = 4
        EXPAND = 2
        HEADDIM = 64
        D_INNER = EXPAND * D_MODEL
        NHEADS = D_INNER // HEADDIM
        CONV_DIM = D_INNER + 2 * D_STATE
        IN_PROJ = 2 * D_INNER + 2 * D_STATE + NHEADS
        INTER = 704
        EPS = 1e-06
        CHUNK = 128

        def rmsnorm(x, w, eps=EPS):
            var = jnp.mean(jnp.square(x), axis=-1, keepdims=True)
            return x * jax.lax.rsqrt(var + eps) * w

        def dw_causal_conv(x, w, b):
            xt = jnp.transpose(x, (0, 2, 1))
            xt = jnp.pad(xt, ((0, 0), (0, 0), (D_CONV - 1, 0)))
            y = jax.lax.conv_general_dilated(xt, w[:, None, :], window_strides=(1,), padding='VALID', feature_group_count=w.shape[0], dimension_numbers=('NCH', 'OIH', 'NCH'))
            y = y + b[None, :, None]
            return jnp.transpose(y, (0, 2, 1))

        def segsum(x):
            T = x.shape[-1]
            xx = jnp.broadcast_to(x[..., None], (*x.shape, T))
            xx = jnp.where(jnp.tril(jnp.ones((T, T), bool), -1), xx, 0.0)
            s = jnp.cumsum(xx, axis=-2)
            return jnp.where(jnp.tril(jnp.ones((T, T), bool), 0), s, -jnp.inf)

        def ssd(x, dt, A, Bm, Cm):
            b, l, h, p = x.shape
            n = Bm.shape[-1]
            c = l // CHUNK
            xr = x.reshape(b, c, CHUNK, h, p)
            dtr = dt.reshape(b, c, CHUNK, h)
            Br = Bm.reshape(b, c, CHUNK, n)
            Cr = Cm.reshape(b, c, CHUNK, n)
            dA = jnp.transpose(dtr * A, (0, 3, 1, 2))
            A_cum = jnp.cumsum(dA, axis=-1)
            L = jnp.exp(segsum(dA))
            xdt = xr * dtr[..., None]
            Y_diag = jnp.einsum('bcln,bcsn,bhcls,bcshp->bclhp', Cr, Br, L, xdt)
            decay_states = jnp.exp(A_cum[..., -1:] - A_cum)
            states = jnp.einsum('bcln,bhcl,bclhp->bchpn', Br, decay_states, xdt)
            A_last = A_cum[..., -1]
            decay_chunk = jnp.exp(segsum(jnp.pad(A_last, ((0, 0), (0, 0), (1, 0)))))
            states_cat = jnp.concatenate([jnp.zeros_like(states[:, :1]), states], axis=1)
            new_states = jnp.einsum('bhzc,bchpn->bzhpn', decay_chunk, states_cat)
            prev = new_states[:, :-1]
            state_decay = jnp.exp(A_cum)
            Y_off = jnp.einsum('bcln,bchpn,bhcl->bclhp', Cr, prev, state_decay)
            return (Y_diag + Y_off).reshape(b, l, h, p)
        B, L, _ = hidden_states.shape
        res = hidden_states
        h = rmsnorm(hidden_states, norm1_w)
        zxbcdt = h @ in_proj_w
        z = zxbcdt[..., :D_INNER]
        xBC = zxbcdt[..., D_INNER:D_INNER + CONV_DIM]
        dt = jax.nn.softplus(zxbcdt[..., -NHEADS:] + dt_bias)
        xBC = jax.nn.silu(dw_causal_conv(xBC, conv_w, conv_b))
        xs = xBC[..., :D_INNER].reshape(B, L, NHEADS, HEADDIM)
        Bm = xBC[..., D_INNER:D_INNER + D_STATE]
        Cm = xBC[..., D_INNER + D_STATE:]
        A = -jnp.exp(A_log)
        y = ssd(xs, dt, A, Bm, Cm)
        y = y + D_param[None, None, :, None] * xs
        y = y.reshape(B, L, D_INNER)
        y = rmsnorm(y * jax.nn.silu(z), mixer_norm_w)
        h1 = res + y @ out_proj_w
        h2 = rmsnorm(h1, norm2_w)
        mlp = jax.nn.silu(h2 @ gate_w) * (h2 @ up_w) @ down_w
        return h1 + mlp

    def _L0_xattn_ref(x, ctx, pos_map, ctx_pos_map, Wq, Wkv, Wout, bout):
        import jax, jax.numpy as jnp
        import numpy as np
        DIM = 256
        CTX_DIM = 128
        N_HEADS = 32
        HEAD_DIM = DIM // N_HEADS
        POS_DIM = 2
        B, N, CTXN = (2, 256, 256)
        ROPE_BASE = 10000.0

        def apply_axial_rope(x, pos):
            b, n, h, d = x.shape
            p = pos.shape[-1]
            dpa = d // p
            half = dpa // 2
            freqs = ROPE_BASE ** (-jnp.arange(half, dtype=x.dtype) / half)
            ang = pos[..., :, None] * freqs
            cos = jnp.cos(ang)[:, :, None, :, :]
            sin = jnp.sin(ang)[:, :, None, :, :]
            xr = x.reshape(b, n, h, p, half, 2)
            x1, x2 = (xr[..., 0], xr[..., 1])
            out = jnp.stack([x1 * cos - x2 * sin, x1 * sin + x2 * cos], axis=-1)
            return out.reshape(b, n, h, d)
        b, n, _ = x.shape
        ctx_n = ctx.shape[1]
        q = (x @ Wq).reshape(b, n, N_HEADS, HEAD_DIM)
        k, v = jnp.split(ctx @ Wkv, 2, axis=-1)
        k = k.reshape(b, ctx_n, N_HEADS, HEAD_DIM)
        v = v.reshape(b, ctx_n, N_HEADS, HEAD_DIM)
        q = apply_axial_rope(q, pos_map)
        k = apply_axial_rope(k, ctx_pos_map)
        scale = 1.0 / np.sqrt(HEAD_DIM).astype(np.float32)
        logits = jnp.einsum('bqhd,bkhd->bhqk', q, k) * scale
        w = jax.nn.softmax(logits, axis=-1)
        attn = jnp.einsum('bhqk,bkhd->bqhd', w, v)
        attn = attn.reshape(b, n, N_HEADS * HEAD_DIM)
        return attn @ Wout + bout

    def _L0_ffn_ref(hidden_states, router_w, Wa, Wb):
        import jax, jax.numpy as jnp
        import numpy as np
        IN_F, OUT_F = (256, 256)
        N_EXPERTS, RANK, TOP_K = (8, 128, 2)
        B, S, D = hidden_states.shape
        x = hidden_states.reshape(-1, D)
        norm = jnp.maximum(jnp.linalg.norm(x, axis=-1, keepdims=True), 1e-12)
        router_logits = x / norm @ router_w
        routing_weights = jax.nn.softmax(router_logits.astype(jnp.float32), axis=-1)
        rw, selected_experts = jax.lax.top_k(routing_weights, TOP_K)
        rw = rw / jnp.sum(rw, axis=-1, keepdims=True)
        rw = rw.astype(hidden_states.dtype)
        combine = jnp.sum(jax.nn.one_hot(selected_experts, N_EXPERTS, dtype=rw.dtype) * rw[..., None], axis=1)
        out = jnp.zeros((x.shape[0], OUT_F), dtype=hidden_states.dtype)
        for e in range(N_EXPERTS):
            out = out + combine[:, e, None] * (x @ Wa[e] @ Wb[e])
        return out.reshape(B, S, OUT_F)

    def _L1_attn_ref(hidden_states, Wq, Wk, Wv, Wq_exp, Wk_exp, Wgate, Wg, Wo):
        import jax, jax.numpy as jnp
        import numpy as np
        H, D, R, S, K, EV = (8, 32, 6, 2, 2, 2)
        HID = 256
        DV = D * EV
        KEY_DIM = H * D
        VAL_DIM = KEY_DIM * EV
        b, t, _ = hidden_states.shape
        q = (hidden_states @ Wq).reshape(b, t, H, D).transpose(2, 0, 1, 3)
        k = (hidden_states @ Wk).reshape(b, t, H, D).transpose(2, 0, 1, 3)
        v = (hidden_states @ Wv).reshape(b, t, H, DV)
        logits = jnp.einsum('hbtd,dn->hbtn', q, Wgate)
        scores = jax.nn.softmax(logits.astype(jnp.float32), axis=-1)
        w, idx = jax.lax.top_k(scores, K)
        w = w / jnp.sum(w, axis=-1, keepdims=True)
        idx = idx + S
        full = jnp.sum(jax.nn.one_hot(idx, R, dtype=w.dtype) * w[..., None], axis=-2)
        full = full.at[..., :S].set(1.0 / S)
        full = full / jnp.sum(full, axis=-1, keepdims=True)
        rw = full.astype(hidden_states.dtype).transpose(3, 1, 2, 0)
        mask = (rw != 0).astype(hidden_states.dtype)
        qe = jnp.einsum('hbtd,hde->hbte', q, Wq_exp).reshape(H, b, t, R, D).transpose(3, 1, 2, 0, 4)
        ke = jnp.einsum('hbtd,hde->hbte', k, Wk_exp).reshape(H, b, t, R, D).transpose(3, 1, 2, 0, 4)
        ve = jnp.broadcast_to(v[None], (R, b, t, H, DV))
        qe = qe * mask[..., None]
        ke = ke * mask[..., None]
        ve = ve * mask[..., None]
        attn = jax.nn.softmax(jnp.einsum('rbqhd,rbkhd->rbhqk', qe, ke) / D ** 0.5, axis=-1)
        o = jnp.einsum('rbhqk,rbkhd->rbqhd', attn, ve)
        o = jnp.einsum('rbthd,rbth->bthd', o, rw)
        g = (hidden_states @ Wg).reshape(b, t, H, DV)
        o = o * jax.nn.silu(g)
        return o.reshape(b, t, VAL_DIM) @ Wo

    def _L1_xattn_ref(teacher_logits, teacher_features, Wq, bq, Wk, bk):
        import jax, jax.numpy as jnp
        import numpy as np
        query = jnp.einsum('bnc,dc->bnd', teacher_features, Wq) + bq
        key = jnp.einsum('bnc,dc->bnd', teacher_features, Wk) + bk
        energy = jnp.einsum('bnd,bmd->bnm', query, key)
        attention = jax.nn.softmax(energy, axis=-1)
        x_m = jnp.einsum('bln,bmn->blm', teacher_logits, attention)
        return x_m

    def _L1_ffn_ref(hidden_states, router_w, router_bias, w_gate, w_up, w_down, sw_gate, sw_up, sw_down):
        import jax, jax.numpy as jnp
        import numpy as np
        B, S, H = (2, 256, 256)
        E, G, TKG, K = (32, 8, 4, 8)
        I, SI = (128, 256)
        ROUTED_SCALE = 2.5

        def _moe_forward(hidden_states, router_w, router_bias, w_gate, w_up, w_down, sw_gate, sw_up, sw_down):
            x = hidden_states.reshape(-1, H)
            T = x.shape[0]
            logits = x.astype(jnp.float32) @ router_w.astype(jnp.float32)
            scores = jax.nn.sigmoid(logits)
            scores_grouped = (scores + router_bias).reshape(T, G, E // G)
            top2, _ = jax.lax.top_k(scores_grouped, 2)
            group_scores = top2.sum(-1)
            _, top_groups = jax.lax.top_k(group_scores, TKG)
            mask = jnp.ones((T, G), bool).at[jnp.arange(T)[:, None], top_groups].set(False)
            masked = jnp.where(mask[:, :, None], 0.0, scores_grouped).reshape(T, E)
            _, top_k_index = jax.lax.top_k(masked, K)
            tkw = jnp.take_along_axis(scores, top_k_index, axis=-1)
            tkw = tkw / tkw.sum(-1, keepdims=True)
            tkw = (tkw * ROUTED_SCALE).astype(hidden_states.dtype)
            flat_idx = top_k_index.reshape(-1)
            sort_idx = jnp.argsort(flat_idx)
            xs = jnp.repeat(x, K, axis=0)[sort_idx]
            group_sizes = jnp.bincount(flat_idx, length=E).astype(jnp.int32)
            gate = jax.lax.ragged_dot(xs, w_gate, group_sizes)
            up = jax.lax.ragged_dot(xs, w_up, group_sizes)
            down = jax.lax.ragged_dot(jax.nn.silu(gate) * up, w_down, group_sizes)
            unsort = jnp.argsort(sort_idx)
            routed = (down[unsort].reshape(T, K, H) * tkw[..., None]).sum(axis=1)
            shared = jax.nn.silu(x @ sw_gate) * (x @ sw_up) @ sw_down
            return (routed + shared).reshape(hidden_states.shape)
        return _moe_forward(hidden_states, router_w, router_bias, w_gate, w_up, w_down, sw_gate, sw_up, sw_down)
    x = x + _L0_attn_ref(_layernorm(x, axis=-1), L0_attn_norm1_w, L0_attn_in_proj_w, L0_attn_conv_w, L0_attn_conv_b, L0_attn_dt_bias, L0_attn_A_log, L0_attn_D_param, L0_attn_mixer_norm_w, L0_attn_out_proj_w, L0_attn_norm2_w, L0_attn_gate_w, L0_attn_up_w, L0_attn_down_w)
    x = x + _L0_xattn_ref(_layernorm(x, axis=-1), ctx_1024, fside_BxSx2_0, fside_BxSx2_0, L0_xattn_Wq, L0_xattn_Wkv, L0_xattn_Wout, L0_xattn_bout)
    x = x + _L0_ffn_ref(_layernorm(x, axis=-1), L0_ffn_router_w, L0_ffn_Wa, L0_ffn_Wb)
    x = x + _L1_attn_ref(_layernorm(x, axis=-1), L1_attn_Wq, L1_attn_Wk, L1_attn_Wv, L1_attn_Wq_exp, L1_attn_Wk_exp, L1_attn_Wgate, L1_attn_Wg, L1_attn_Wo)
    x = x + _L1_xattn_ref(_layernorm(x, axis=-1), ctx_1024, L1_xattn_Wq, L1_xattn_bq, L1_xattn_Wk, L1_xattn_bk)
    x = x + _L1_ffn_ref(_layernorm(x, axis=-1), L1_ffn_router_w, L1_ffn_router_bias, L1_ffn_w_gate, L1_ffn_w_up, L1_ffn_w_down, L1_ffn_sw_gate, L1_ffn_sw_up, L1_ffn_sw_down)
    return x

_drawn_inputs = setup_inputs


def setup_inputs(seed=0):
    import zlib

    import numpy as np

    out = dict(_drawn_inputs(seed))
    spreads = {'L0_attn_norm1_w': (1.0, 0.2),
     'L0_attn_conv_b': (0.0, 0.1),
     'L0_attn_D_param': (1.0, 0.2),
     'L0_attn_mixer_norm_w': (1.0, 0.2),
     'L0_attn_norm2_w': (1.0, 0.543),
     'L0_xattn_bout': (0.0, 0.1),
     'L1_xattn_bq': (0.0, 0.1),
     'L1_xattn_bk': (0.0, 2.0),
     'L1_ffn_router_bias': (0.0, 0.1)}
    factors = {'L0_attn_dt_bias': 33.328, 'L0_attn_A_log': 29.912, 'L1_attn_Wgate': 2.804}
    for name, (base, spread) in spreads.items():
        noise = np.random.default_rng([zlib.crc32(name.encode()), seed]).standard_normal(out[name].shape)
        drawn = base * np.exp(spread * noise) if base else spread * noise
        out[name] = jnp.asarray(drawn.astype(out[name].dtype))
    for name, factor in factors.items():
        out[name] = (out[name] * factor).astype(out[name].dtype)
    return out
```

```python
from contextlib import ExitStack

import concourse.bass as bass
from concourse import mybir

F32 = mybir.dt.float32
BF16 = mybir.dt.bfloat16
ALU = mybir.AluOpType
ACT = mybir.ActivationFunctionType
AX = mybir.AxisListType

P = 128
B, T, D = 4, 256, 256
NT = T // P
KD = D // P
CD = 128
STREAMS = 2
PAIRS = B // STREAMS
HALF_PI = 1.5707963267948966

MH, MP = 8, 64
DI = MH * MP
KI = DI // P
NS = 128
NCH = (DI + 2 * NS) // P
INTER = 704
KG = -(-INTER // P)
XH, XD = 32, 8
NPAIR = XH // 2
HT = 12
XT3 = -(-XH // HT)
SHIFT = 96
QSLOTS = 4
FE = 8
AH, AD, AR, AS = 8, 32, 6, 2
AV = 64
VW = AV + 1
RH = 3
ME, MG, MTK, MTG = 32, 8, 8, 4
MI = 128
MSH = 2
ROUTED_SCALE = 2.5




class Plan:

    def __init__(self):
        self.number, self.count, self.freed, self.bank, self.before, self.final = {}, {}, {}, {}, {}, False


class Keys:

    def __init__(self, s, turn, plan, did, psum):
        self.s, self.turn, self.plan, self.did, self.psum = s, turn, plan, did, psum[s]
        self.taken, self.holder, self.latest = {}, {}, 3

    def take(self, name, banks=(0, 1, 2, 3)):
        after = [n for n in banks if n > self.latest] if self.latest in banks else list(banks)
        b = after[0] if after else banks[0]
        if len(banks) > 1:
            self.latest = b
        before = self.holder.get(b)
        self.holder[b] = name
        self.plan.bank[name] = b
        if before is None:
            return self.psum[:, b, :], None
        return self.psum[:, b, :], self.ready(*self.plan.freed[before]) if self.plan.final else None

    def bank(self, name):
        return self.psum[:, self.plan.bank.get(name, 0), :]

    def step(self, engine, name=None, frees=None):
        n = self.taken[engine] = self.taken.get(engine, 0) + 1
        if name is not None:
            assert self.plan.number.setdefault((engine, name), n) == n, (engine, name)
        if frees is not None:
            self.plan.number[engine, "frees", frees] = n
            self.plan.freed[frees] = (engine, "frees", frees)
        if not self.plan.final:
            self.plan.count[engine] = max(self.plan.count.get(engine, 0), n)
        return self.did[engine][self.s], 1

    def name_last(self, engine, name):
        self.plan.number[engine, name] = self.taken[engine]

    def last(self, engine):
        return self.did[engine][self.s], self.taken[engine]

    def ready(self, engine, *name):
        if not self.plan.final:
            return self.did[engine][self.s], 1
        return self.did[engine][self.s], self.plan.number[(engine, *name)]


def build(nc, plan, io, out):
    with ExitStack() as ctx:
        xall = ctx.enter_context(nc.sbuf_tensor("xall", [P, PAIRS, STREAMS, NT * D], F32))
        ident = ctx.enter_context(nc.sbuf_tensor("ident", [P, P], F32))
        five_blocks(nc, plan, io, xall, ident)
        grouped_experts(nc, io, out, xall, ident)


def five_blocks(nc, plan, io, xall, ident):
    with ExitStack() as ctx:
        def sb(name, shape, dt=F32):
            return ctx.enter_context(nc.sbuf_tensor(name, shape, dt))

        def sem(name):
            return ctx.enter_context(nc.semaphore(name))

        w_in = sb("w_in", [P, KD, DI + NCH * P + MH])
        w_mo = sb("w_mo", [P, KI, D])
        w_gate = sb("w_gate", [P, KD, INTER])
        w_up = sb("w_up", [P, KD, INTER])
        w_down = sb("w_down", [P, KG, D])
        w_xq = sb("w_xq", [P, KD, D])
        w_xkv = sb("w_xkv", [P, 2 * D])
        w_xo = sb("w_xo", [P, KD, D])
        w_fr = sb("w_fr", [P, KD, FE])
        w_fa = sb("w_fa", [P, FE, KD, P])
        w_fb = sb("w_fb", [P, FE, D])
        w_aq = sb("w_aq", [P, KD, AH * AD])
        w_ak = sb("w_ak", [P, KD, AH * AD])
        w_av = sb("w_av", [P, KD, AH * AV])
        w_ag = sb("w_ag", [P, KD, AH * AV])
        w_aeq = sb("w_aeq", [P, KD, AR * AD])
        w_aek = sb("w_aek", [P, KD, AR * AD])
        w_al = sb("w_al", [P, 4, AR - AS])
        w_ao = sb("w_ao", [P, AH * AV // P, D])
        w_tq = sb("w_tq", [P, P])
        w_tk = sb("w_tk", [P, P])
        norm1 = sb("norm1", [P, KD])
        norm2 = sb("norm2", [P, KD])
        mixn = sb("mixn", [P, KI])
        cw = sb("cw", [P, NCH, 4])
        cb = sb("cb", [P, NCH])
        dtb = sb("dtb", [P, MH])
        aneg = sb("aneg", [P, MH])
        dpar = sb("dpar", [P, MH])
        bout = sb("bout", [P, D])
        bq = sb("bq", [P, 1])
        bk = sb("bk", [P, 1])
        le = sb("le", [P, P])
        gt = sb("gt", [P, P])
        head12 = sb("head12", [SHIFT, HT])
        mem3 = sb("mem3", [SHIFT, RH])
        below = sb("below", [P, 4, 4])
        spread = sb("spread", [AH * AR, AH * 2, RH * AD], BF16)
        sincos = sb("sincos", [P, PAIRS, STREAMS, NT * 8])
        pw = sb("pw", [P, 2])

        psum = [ctx.enter_context(nc.psum_tensor(f"psum{s}", [P, 4, 512], F32)) for s in range(STREAMS)]
        WORDS = 12840
        per = []
        for s in range(STREAMS):
            a = sb(f"arena{s}", [P, WORDS])
            d = {}
            for n, shape in dict(X=[P, NT, D], XN=[P, NT, D], H=[P, NT, D], AT=[P, KD, T], CT=[P, T],
                                 small=[P, 256]).items():
                d[n] = sb(f"{n}{s}", shape)
            per.append((a, d))

        did = {e: [sem(f"{e}_did{s}") for s in range(STREAMS)] for e in ("tensor", "vector", "scalar", "pool")}
        loaded = [sem(f"loaded{s}") for s in range(STREAMS)]
        arrived = sem("turn_ended")
        started = sem("turn_started")
        rowed = [sem(f"rowed{s}") for s in range(STREAMS)]
        slot_rows = [[sem(f"slot_rows{s}{k}") for k in range(QSLOTS)] for s in range(STREAMS)]
        w_loaded = {n: sem(f"w_{n}") for n in ("small", "mamba", "rot", "fexp", "mom", "feat")}
        s_const = sem("constants")
        s_fill = sem("filled_consts")
        s_pool = sem("pool_consts")
        s_ang = sem("angles")
        s_sin = sem("sines")
        s_half = sem("halved")
        s_exp = sem("negated")

        def view(s, at, shape, dt=F32):
            n = 1
            for m in shape[1:]:
                n *= m
            words = n if dt == F32 else n // 2
            assert at + words <= WORDS, (at, shape)
            v = per[s][0][0:shape[0], at:at + words]
            if dt != F32:
                v = v.bitcast(dt)
            if len(shape) == 3:
                v = v.rearrange("p (a b) -> p a b", b=shape[2])
            if len(shape) == 4:
                v = v.rearrange("p (a b c) -> p a b c", b=shape[2], c=shape[3])
            if len(shape) == 5:
                v = v.rearrange("p (a b c d) -> p a b c d", b=shape[2], c=shape[3], d=shape[4])
            return v

        class Bufs:
            pass

        bufs = []
        for s in range(STREAMS):
            b = Bufs()
            d = per[s][1]
            b.X, b.XN, b.H, b.AT, b.CT = d["X"], d["XN"], d["H"], d["AT"], d["CT"]
            sm = d["small"]
            b.bst = sm[:, 0:12].rearrange("p (i c) -> p i c", i=NT)
            b.mv = sm[:, 12:16].rearrange("p (i c) -> p i c", i=NT)
            b.ve, b.rstd, b.r2, b.rh = sm[:, 16:18], sm[:, 18:20], sm[:, 20:22], sm[:, 22:24]
            b.ss, b.rs, b.ss2, b.rs2 = sm[:, 24:26], sm[:, 26:28], sm[:, 28:30], sm[:, 30:32]
            b.raw, b.nab, b.u, b.z, b.z2, b.ser, b.dt, b.dA = (
                sm[:, 32 + 16 * k:48 + 16 * k].rearrange("p (i h) -> p i h", i=NT) for k in range(8))
            b.dcy = sm[:, 160:176]
            b.sc = sm[:, 176:192].rearrange("p (i c) -> p i c", i=NT)
            b.XBC = view(s, 0, [P, NCH, T])
            b.TH = view(s, 1536, [P, NCH, T])
            b.G = view(s, 3072, [P, NT, DI])
            b.E = [view(s, 4096 + 1024 * i, [P, MH, P]) for i in range(NT)]
            b.CB = view(s, 6144, [P, NT, P])
            b.XT = view(s, 6400, [P, NT, DI])
            b.XDT = view(s, 7424, [P, NT, DI])
            b.XDEC = view(s, 8448, [P, DI])
            b.ST = view(s, 8960, [P, DI])
            b.BT = view(s, 9472, [P, NS])
            b.H1 = view(s, 9600, [P, NT, D])
            b.SQ = view(s, 10112, [P, DI])
            b.YO = view(s, 10624, [P, DI])
            b.YT = view(s, 1536, [P, KI, T])
            b.MTH = view(s, 2560, [P, 2, T])
            b.MA = view(s, 0, [P, KG, T])
            b.QC = view(s, 0, [P, NT, D])
            b.QS = view(s, 512, [P, NT, D])
            b.KR = view(s, 1024, [P, NT, D])
            b.QR = view(s, 1536, [P, NT, D])
            b.V1 = view(s, 2048, [P, NT, XH, 32])
            b.KT = view(s, 4096, [SHIFT + 1, XT3, T])
            b.QT = view(s, 4864, [SHIFT, XT3, T])
            b.KTB = view(s, 5632, [SHIFT, XT3, T], BF16)
            b.QMB = [view(s, 6016 + 256 * k, [SHIFT, 2, T], BF16) for k in range(2)]
            b.MX = view(s, 6528, [P, NT, XH])
            b.NMT = view(s, 6592, [XH, T])
            b.QM = [view(s, 6848 + 512 * k, [SHIFT + 1, 2, T]) for k in range(QSLOTS)]
            b.PT = [view(s, 8896 + 1024 * k, [P, NT, 2, T]) for k in range(3)]
            b.OT = [view(s, 1024 + 512 * k, [P, 2, T]) for k in range(2)]
            b.RD = view(s, 11968, [P, 4, 4])
            b.O = view(s, 0, [P, NT, D])
            b.FH = [view(s, 512 * k, [P, 2, T]) for k in range(2)]
            b.SQF = view(s, 1024, [P, D])
            b.f = [view(s, 1280 + 16 * k, [P, NT, FE]) for k in range(10)]
            b.fs = [view(s, 1600 + 2 * k, [P, NT]) for k in range(8)]
            b.AQ = view(s, 0, [P, KD, T])
            b.AK = view(s, 512, [P, KD, T])
            b.AV = view(s, 1024, [P, NT, AH, VW])
            b.r3 = [view(s, 2064 + 256 * k, [P, NT * AH, 4, 4]) for k in range(3)]
            b.r2d = [view(s, 2832 + 64 * k, [P, NT * AH, 4]) for k in range(5)]
            b.r1 = [view(s, 3152 + 16 * k, [P, NT * AH]) for k in range(3)]
            b.RW = view(s, 3200, [P, NT, AH, AR])
            b.MK = view(s, 3296, [P, NT, AH, AR])
            b.MKT = view(s, 3392, [AH * AR, T], BF16)
            b.AO = view(s, 3520, [P, NT, AH * AV])
            b.QE = [view(s, 4544 + 1536 * k, [SHIFT + 1, 2, RH, T]) for k in range(2)]
            b.KE = [view(s, 7616 + 512 * k, [SHIFT + 1, 2, T]) for k in range(2)]
            b.QEB = view(s, 8640, [SHIFT, 2, RH, T], BF16)
            b.KEB = view(s, 9408, [SHIFT, 2, T], BF16)
            b.VM = [view(s, 9664 + 520 * k, [P, NT, 4, VW]) for k in range(2)]
            b.APT = [b.XN, view(s, 10704, [P, NT, T])]
            b.AOT = view(s, 11216, [VW, AR, T])
            b.MB = b.H[0:SHIFT, :, :]
            b.ANT = view(s, 2064, [AR, T])
            b.AMX = view(s, 2320, [P, NT, AR])
            b.CO = view(s, 2332, [P, AR])
            b.TMP = view(s, 2338, [P, AR, AV])
            b.AG = view(s, 4544, [P, NT, AH * AV])
            b.AYT = view(s, 5568, [P, AH * AV // P, T])
            b.TQ = view(s, 0, [P, T])
            b.TK = view(s, 256, [P, T])
            b.TP = view(s, 512, [P, NT, T])
            b.TPT = view(s, 1024, [P, NT, T])
            b.ts = [view(s, 1536 + 2 * k, [P, NT]) for k in range(4)]
            bufs.append(b)
        ang = view(0, 0, [P, B * NT, 8])
        posn = view(0, 64, [P, B * NT, 2])

        block = ctx.enter_context(nc.Block())

        CONSTS = 6
        N_SMALL, N_MAMBA, N_ROT, N_FEXP, N_MOM, N_FEAT = 10, 6, 3, 3, 15, 2

        def keys(turn):
            return [Keys(s, turn, plan, did, psum) for s in range(STREAMS)]

        def turn_end(engine, turn):
            for e, n in plan.count.items():
                for s in range(STREAMS):
                    engine.wait_ge(did[e][s], n)
            engine.nop().then_inc(arrived, 1)

        @block.sync
        def _(sp):
            sp.dma_start(dtb[:, :], io["L0_attn_dt_bias"].partition_broadcast(P)).then_inc(w_loaded["small"], 16)
            sp.dma_start(aneg[:, :], io["L0_attn_A_log"].partition_broadcast(P)).then_inc(w_loaded["small"], 16)
            sp.dma_start(dpar[:, :], io["L0_attn_D_param"].partition_broadcast(P)).then_inc(w_loaded["small"], 16)
            sp.dma_start(bout[:, :], io["L0_xattn_bout"].partition_broadcast(P)).then_inc(w_loaded["small"], 16)
            sp.dma_start(norm1[:, :], io["norm1"]).then_inc(w_loaded["small"], 16)
            sp.dma_start(norm2[:, :], io["norm2"]).then_inc(w_loaded["small"], 16)
            sp.dma_start(mixn[:, :], io["mixn"]).then_inc(w_loaded["small"], 16)
            sp.dma_start(cw[:, :, :], io["conv_w"]).then_inc(w_loaded["small"], 16)
            sp.dma_start(cb[:, :], io["conv_b"]).then_inc(w_loaded["small"], 16)
            sp.dma_start(posn[:, :, :], io["pos"]).then_inc(w_loaded["small"], 16)

            def load(K, b):
                sp.dma_start(b.X[:, :, :], io["x"][K.s][K.turn]).then_inc(loaded[K.s], 16)
                sp.dma_start(b.CT[:, :], io["ctx"][K.s][K.turn]).then_inc(loaded[K.s], 16)

            def rot_rows(K, b):
                sp.wait_ge(*K.ready("vector", "xnm"))
                for p in range(NPAIR):
                    if p >= QSLOTS:
                        sp.wait_ge(*K.ready("tensor", ("xt", p - QSLOTS, NT - 1)))
                    sp.dma_start(b.QM[p % QSLOTS][SHIFT:SHIFT + 1, :, :], b.NMT[2 * p:2 * p + 2, :]).then_inc(
                        slot_rows[K.s][p % QSLOTS], 16)

            def mom_rows(K, b):
                for h in range(AH):
                    sp.wait_ge(*K.ready("vector", f"anm{h}"))
                    sp.dma_start(b.QE[h % 2][SHIFT:SHIFT + 1, :, :, :].rearrange("p a g t -> p (a g) t"),
                                 b.ANT[:, :]).then_inc(rowed[K.s], 16)

            sp.dma_start(w_in[:, :, :], io["L0_attn_in_proj_w"].rearrange("(k p) n -> p k n", p=P)).then_inc(
                w_loaded["mamba"], 16)
            sp.dma_start(w_mo[:, :, :], io["L0_attn_out_proj_w"].rearrange("(k p) n -> p k n", p=P)).then_inc(
                w_loaded["mamba"], 16)
            sp.dma_start(w_gate[:, :, :], io["L0_attn_gate_w"].rearrange("(k p) n -> p k n", p=P)).then_inc(
                w_loaded["mamba"], 16)
            sp.dma_start(w_up[:, :, :], io["L0_attn_up_w"].rearrange("(k p) n -> p k n", p=P)).then_inc(
                w_loaded["mamba"], 16)
            full_rows = INTER // P * P
            sp.dma_start(w_down[:, 0:KG - 1, :], io["L0_attn_down_w"][0:full_rows, :].rearrange(
                "(k p) n -> p k n", p=P)).then_inc(w_loaded["mamba"], 16)
            sp.dma_start(w_down[0:INTER - full_rows, KG - 1, :], io["L0_attn_down_w"][full_rows:INTER, :]).then_inc(
                w_loaded["mamba"], 16)
            with sp.Fori(0, PAIRS) as turn:
                K2 = keys(turn)
                for K, b in zip(K2, bufs):
                    load(K, b)
                for stage in (rot_rows, mom_rows):
                    for K, b in zip(K2, bufs):
                        stage(K, b)
                turn_end(sp, turn)
                sp.wait_ge(arrived, 5)
                for c in [c for e in did.values() for c in e] + loaded + rowed + [c for s in slot_rows for c in s] + [
                        arrived]:
                    sp.sem_clear(c)
                sp.nop().then_inc(started, 1)

        @block.scalar
        def _(act):
            for n, t, src in (
                ("rot", w_xq[:, :, :], io["L0_xattn_Wq"].rearrange("(k p) n -> p k n", p=P)),
                ("rot", w_xkv[:, :], io["L0_xattn_Wkv"]),
                ("rot", w_xo[:, :, :], io["L0_xattn_Wout"].rearrange("(k p) n -> p k n", p=P)),
                ("fexp", w_fr[:, :, :], io["L0_ffn_router_w"].rearrange("(k p) n -> p k n", p=P)),
                ("fexp", w_fa[:, :, :, :], io["L0_ffn_Wa"].rearrange("e (k p) r -> p e k r", p=P)),
                ("fexp", w_fb[:, :, :], io["L0_ffn_Wb"].rearrange("e p n -> p e n")),
                ("mom", w_aq[:, :, :], io["L1_attn_Wq"].rearrange("(k p) n -> p k n", p=P)),
                ("mom", w_ak[:, :, :], io["L1_attn_Wk"].rearrange("(k p) n -> p k n", p=P)),
                ("mom", w_av[:, :, :], io["L1_attn_Wv"].rearrange("(k p) n -> p k n", p=P)),
                ("mom", w_ag[:, :, :], io["L1_attn_Wg"].rearrange("(k p) n -> p k n", p=P)),
                ("mom", w_ao[:, :, :], io["L1_attn_Wo"].rearrange("(k p) n -> p k n", p=P)),
                ("feat", w_tq[:, :], io["wq_t"]),
                ("feat", w_tk[:, :], io["wk_t"]),
                ("mom", bq[:, :], io["bq"]),
                ("mom", bk[:, :], io["bk"]),
            ):
                act.dma_start(t, src).then_inc(w_loaded[n], 16)
            for k in range(KD):
                act.dma_start(w_aeq[:, k, :], io["wq_exp"][k]).then_inc(w_loaded["mom"], 16)
                act.dma_start(w_aek[:, k, :], io["wk_exp"][k]).then_inc(w_loaded["mom"], 16)
            act.wait_ge(s_fill, 1)
            for a in range(4):
                act.dma_start(w_al[32 * a:32 * a + 32, a, :], io["L1_attn_Wgate"]).then_inc(w_loaded["mom"], 16)
            act.wait_ge(s_ang, 1)
            nc.scalar.activation(sincos[:, :, :, :].rearrange("p a b c -> p (a b c)"),
                                 ang[:, :, :].rearrange("p a b -> p (a b)"), ACT.Sin).then_inc(s_sin, 1)
            act.wait_ge(w_loaded["small"], 16 * N_SMALL)
            nc.scalar.activation(aneg[:, :], aneg[:, :], ACT.Exp).then_inc(s_exp, 1)


            def turned(K, b, name):
                act.wait_ge(*K.ready("tensor", name))
                nc.scalar.copy(b.AT[:, :, :].rearrange("p k t -> p (k t)"), K.bank(name)).then_inc(
                    *K.step("scalar", name, frees=name))

            def mamba_in(K, b):
                act.wait_ge(*K.ready("tensor", "hT"))
                for k in range(KD):
                    nc.scalar.activation(b.AT[:, k, :], K.bank("hT")[:, k * T:(k + 1) * T], ACT.Copy,
                                         scale=norm1[:, k:k + 1]).then_inc(*K.step("scalar", f"hT{k}", frees="hT"))
                for j in range(NCH // 2):
                    act.wait_ge(*K.ready("tensor", f"xbc{j}"))
                    for c in (2 * j, 2 * j + 1):
                        nc.scalar.activation(b.XBC[:, c, :], K.bank(f"xbc{j}")[:, (c % 2) * T:(c % 2 + 1) * T],
                                             ACT.Identity, bias=cb[:, c:c + 1], scale=cw[:, c, 3:4]).then_inc(
                                                 *K.step("scalar", f"tap{c}"))
                for i in range(NT):
                    act.wait_ge(*K.ready("tensor", f"z{i}"))
                    nc.scalar.activation(b.G[:, i, :], K.bank(f"z{i}"), ACT.Tanh, scale=0.5).then_inc(
                        *K.step("scalar", f"thz{i}"))
                for j in range(NCH // 2):
                    act.wait_ge(*K.ready("vector", f"conv{j}"))
                    nc.scalar.activation(b.TH[:, 2 * j:2 * j + 2, :], b.XBC[:, 2 * j:2 * j + 2, :],
                                         ACT.Tanh).then_inc(*K.step("scalar", f"th{j}"))
                act.wait_ge(*K.ready("vector", "dt_low"))
                nc.scalar.activation(b.u, b.nab, ACT.Exp).then_inc(*K.step("scalar", "dt_exp"))

            def mamba_ssd(K, b):
                act.wait_ge(*K.ready("tensor", "bT"))
                nc.scalar.copy(b.BT[:, :], K.bank("bT")[:, 0:NS]).then_inc(*K.step("scalar", "bT", frees="bT"))
                for i in range(NT):
                    act.wait_ge(*K.ready("tensor", f"xsT{i}"))
                    nc.scalar.copy(b.XT[:, i, :], K.bank(f"xsT{i}")).then_inc(*K.step("scalar", f"xs{i}"))
                act.wait_ge(*K.ready("tensor", "cum"))
                nc.scalar.activation(b.dcy, K.bank("cum")[:, 0:2 * MH], ACT.Exp).then_inc(
                    *K.step("scalar", "decay", frees="cum"))
                for i in range(NT):
                    for j in range(2):
                        act.wait_ge(*K.ready("tensor", f"seg{i}{j}"))
                        nc.scalar.activation(b.E[i][:, 4 * j:4 * j + 4, :].rearrange("p h l -> p (h l)"),
                                             K.bank(f"seg{i}{j}"), ACT.Exp).then_inc(
                                                 *K.step("scalar", f"L{i}{j}", frees=f"seg{i}{j}"))
                act.wait_ge(*K.ready("tensor", "state"))
                nc.scalar.copy(b.ST[:, :], K.bank("state")).then_inc(*K.step("scalar", "state", frees="state"))

            def mamba_out(K, b):
                for i in range(NT):
                    act.wait_ge(*K.ready("vector", f"gated{i}"))
                    nc.scalar.activation(b.SQ[:, :], b.XT[:, i, :], ACT.Square,
                                         accum_out=b.ss[:, i:i + 1]).then_inc(*K.step("scalar", f"y_square{i}"))
                    act.wait_ge(*K.last("scalar"))
                for j in range(2):
                    act.wait_ge(*K.ready("tensor", f"ynT{j}"))
                    for k in (2 * j, 2 * j + 1):
                        nc.scalar.activation(b.YT[:, k, :], K.bank(f"ynT{j}")[:, (k % 2) * T:(k % 2 + 1) * T], ACT.Copy,
                                             scale=mixn[:, k:k + 1]).then_inc(
                                                 *K.step("scalar", f"yT{k}", frees=f"ynT{j}"))
                for i in range(NT):
                    act.wait_ge(*K.ready("vector", f"h1{i}"))
                    nc.scalar.activation(b.SQ[:, 0:D], b.H1[:, i, :], ACT.Square,
                                         accum_out=b.ss2[:, i:i + 1]).then_inc(*K.step("scalar", f"h_square{i}"))
                    act.wait_ge(*K.last("scalar"))
                act.wait_ge(*K.ready("tensor", "h2T"))
                for k in range(KD):
                    nc.scalar.activation(b.AT[:, k, :], K.bank("h2T")[:, k * T:(k + 1) * T], ACT.Copy,
                                         scale=norm2[:, k:k + 1]).then_inc(*K.step("scalar", f"h2T{k}", frees="h2T"))
                for j in range(KG):
                    m = min(P, INTER - j * P)
                    act.wait_ge(*K.ready("tensor", f"gu{j}"))
                    if j >= 2:
                        act.wait_ge(*K.ready("vector", f"ma{j - 2}"))
                    nc.scalar.activation(b.MTH[0:m, j % 2, :], K.bank(f"gu{j}")[0:m, 0:T], ACT.Tanh,
                                         scale=0.5).then_inc(*K.step("scalar", f"thg{j}"))

            def rot_in(K, b):
                turned(K, b, "xT")
                act.wait_ge(*K.ready("pool", "v_pad"))
                act.wait_ge(*K.ready("tensor", "xv"))
                for i in range(NT):
                    nc.scalar.copy(b.V1[:, i, :, 0:XD], K.bank("xv")[:, i * D:(i + 1) * D].rearrange(
                        "p (h d) -> p h d", d=XD)).then_inc(*K.step("scalar", f"v{i}", frees="xv"))
                for n, t in (("xkT", b.KT), ("xqT", b.QT)):
                    for c in range(2):
                        act.wait_ge(*K.ready("tensor", f"{n}{c}"))
                        if c == 0:
                            nc.scalar.copy(t[0:SHIFT, 0:2, :].rearrange("p f t -> p (f t)"),
                                           K.bank(f"{n}0")[0:SHIFT, :]).then_inc(
                                               *K.step("scalar", f"{n}0", frees=f"{n}0"))
                        else:
                            m = D - 2 * SHIFT
                            nc.scalar.copy(t[0:m, 2, :], K.bank(f"{n}1")[0:m, 0:T]).then_inc(
                                *K.step("scalar", f"{n}1", frees=f"{n}1"))

            def masked_pair(K, b, p, out, name):
                for e in range(2):
                    h = 2 * p + e
                    nc.scalar.activation(out[0:SHIFT, e, :], b.QT[:, h // HT, :], ACT.Copy,
                                         scale=head12[:, h % HT:h % HT + 1]).then_inc(
                                             *K.step("scalar", (name, p) if e else None))

            def rot_max(K, b):
                act.wait_ge(*K.last("scalar"))
                act.wait_ge(*K.ready("pool", "k_pad"))
                for p in range(NPAIR):
                    if p >= 2:
                        act.wait_ge(*K.ready("tensor", ("xs", p - 2)))
                    masked_pair(K, b, p, b.QMB[p % 2], "q_low")

            def rot_heads(K, b):
                for p in range(QSLOTS - 1):
                    masked_pair(K, b, p, b.QM[p], "q_masked")
                for p in range(NPAIR):
                    if p + QSLOTS - 1 < NPAIR:
                        if p >= 1:
                            act.wait_ge(*K.ready("tensor", ("xt", p - 1, NT - 1)))
                        masked_pair(K, b, p + QSLOTS - 1, b.QM[(p + QSLOTS - 1) % QSLOTS], "q_masked")
                    if p >= 3:
                        act.wait_ge(*K.ready("tensor", ("weighed", p - 3)))
                    for k in range(NT):
                        act.wait_ge(*K.ready("tensor", ("xt", p, k)))
                        nc.scalar.activation(b.PT[p % 3][:, k, :, :].rearrange("p e t -> p (e t)"),
                                             K.bank(("xt", p, k)), ACT.Exp, scale=XD ** -0.5).then_inc(
                                                 *K.step("scalar", ("weights", p, k), frees=("xt", p, k)))
                    if p >= 4 and p % 4 == 0:
                        rot_values(K, b, p // 4 - 1)
                rot_values(K, b, NPAIR // 4 - 1)

            def rot_out(K, b):
                turned(K, b, "xoF")

            def rot_values(K, b, g):
                act.wait_ge(*K.ready("tensor", ("xo", g)))
                if g >= 2:
                    act.wait_ge(*K.ready("tensor", ("xoT", g - 2)))
                nc.scalar.copy(b.OT[g % 2][:, :, :].rearrange("p e t -> p (e t)"), K.bank(("xo", g))).then_inc(
                    *K.step("scalar", ("oT", g), frees=("xo", g)))

            def low_rank(K, b):
                for i in range(NT):
                    act.wait_ge(*K.ready("vector", f"xn3{i}"))
                    nc.scalar.activation(b.SQF[:, :], b.XN[:, i, :], ACT.Square,
                                         accum_out=b.ss[:, i:i + 1]).then_inc(*K.step("scalar", f"x_square{i}"))
                    act.wait_ge(*K.last("scalar"))
                turned(K, b, "fT")
                act.wait_ge(*K.ready("vector", "f_shifted"))
                nc.scalar.activation(b.f[2], b.f[1], ACT.Exp).then_inc(*K.step("scalar", "f_exp"))
                for j in range(FE // 2):
                    act.wait_ge(*K.ready("tensor", ("fa", j)))
                    if j >= 2:
                        act.wait_ge(*K.ready("tensor", ("fb", 2 * j - 3)))
                    nc.scalar.copy(b.FH[j % 2][:, :, :].rearrange("p e t -> p (e t)"), K.bank(("fa", j))).then_inc(
                        *K.step("scalar", ("fh", j), frees=("fa", j)))

            def mom_in(K, b):
                turned(K, b, "aT")
                for n, t in (("aq", b.AQ), ("ak", b.AK)):
                    act.wait_ge(*K.ready("tensor", n))
                    nc.scalar.copy(t[:, :, :].rearrange("p k t -> p (k t)"), K.bank(n)).then_inc(
                        *K.step("scalar", n, frees=n))
                for i in range(NT):
                    act.wait_ge(*K.ready("tensor", f"av{i}"))
                    nc.scalar.copy(b.AV[:, i, :, 0:AV], K.bank(f"av{i}").rearrange("p (h d) -> p h d", d=AV)).then_inc(
                        *K.step("scalar", f"av{i}", frees=f"av{i}"))
                act.wait_ge(*K.ready("vector", "a_shifted"))
                nc.scalar.activation(b.r2d[1], b.r2d[0], ACT.Exp).then_inc(*K.step("scalar", "a_exp"))
                act.wait_ge(*K.ready("tensor", "amT"))
                nc.scalar.copy(b.MKT[:, :], K.bank("amT")[0:AH * AR, 0:T]).then_inc(
                    *K.step("scalar", "mask_rows", frees="amT"))

            def mom_project(K, b, h):
                m = RH * AD
                act.wait_ge(*K.ready("tensor", ("aeq", h)))
                if h >= 2:
                    act.wait_ge(*K.ready("tensor", ("at", h - 2, AR - 1)))
                for g in range(RH):
                    nc.scalar.activation(b.QE[h % 2][0:m, :, g, :], K.bank(("aeq", h))[0:m, :].rearrange(
                        "p (e t) -> p e t", e=2), ACT.Copy, scale=mem3[:, g:g + 1]).then_inc(
                            *K.step("scalar", ("qe", h) if g == RH - 1 else None, frees=("aeq", h)))
                act.wait_ge(*K.ready("tensor", ("aem", h)))
                if h >= 1:
                    act.wait_ge(*K.ready("vector", ("ke", h - 1)))
                nc.scalar.copy(b.MB[:, :, :].rearrange("p e t -> p (e t)"), K.bank(("aem", h))[0:m, :]).then_inc(
                    *K.step("scalar", ("masks", h), frees=("aem", h)))

            def mom_heads(K, b):
                mom_project(K, b, 0)
                for h in range(AH):
                    if h + 1 < AH:
                        mom_project(K, b, h + 1)
                    for r in range(AR):
                        n = h * AR + r
                        act.wait_ge(*K.ready("tensor", ("at", h, r)))
                        if n >= 2:
                            act.wait_ge(*K.ready("tensor", ("weighed_a", n - 2)))
                        nc.scalar.activation(b.APT[n % 2][:, :, :].rearrange("p k t -> p (k t)"),
                                             K.bank(("at", h, r)), ACT.Exp, scale=AD ** -0.5).then_inc(
                                                 *K.step("scalar", ("weights_a", n), frees=("at", h, r)))
                        if r % 2 == 0 and r >= 2:
                            mom_values(K, b, h, r // 2 - 1)
                    mom_values(K, b, h, AR // 2 - 1)

            def mom_values(K, b, h, j):
                act.wait_ge(*K.ready("tensor", ("ao", h, j)))
                if h >= 1 and j == 0:
                    act.wait_ge(*K.ready("tensor", ("aoT", h - 1, NT - 1)))
                nc.scalar.copy(b.AOT[:, 2 * j:2 * j + 2, :].rearrange("p r t -> p (r t)"),
                               K.bank(("ao", h, j))[0:VW, :]).then_inc(
                                   *K.step("scalar", ("aoT", h, j), frees=("ao", h, j)))

            def mom_out(K, b):
                for i in range(NT):
                    act.wait_ge(*K.ready("tensor", f"ag{i}"))
                    nc.scalar.activation(b.AG[:, i, :], K.bank(f"ag{i}"), ACT.Tanh, scale=0.5).then_inc(
                        *K.step("scalar", f"thag{i}"))
                for j in range(2):
                    act.wait_ge(*K.ready("tensor", f"aoF{j}"))
                    nc.scalar.activation(b.AYT[:, 2 * j:2 * j + 2, :].rearrange("p k t -> p (k t)"),
                                         K.bank(f"aoF{j}"), ACT.Copy, scale=0.5).then_inc(
                                             *K.step("scalar", f"ayT{j}", frees=f"aoF{j}"))

            def feat(K, b):
                for n, t, bias in (("tq", b.TQ, bq), ("tk", b.TK, bk)):
                    act.wait_ge(*K.ready("tensor", n))
                    nc.scalar.activation(t[:, :], K.bank(n)[:, 0:T], ACT.Identity, bias=bias[:, 0:1]).then_inc(
                        *K.step("scalar", n, frees=n))
                act.wait_ge(*K.ready("vector", "t_max"))
                for i in range(NT):
                    nc.scalar.activation(b.TP[:, i, :], K.bank("te")[:, i * T:(i + 1) * T], ACT.Exp,
                                         bias=b.ts[1][:, i:i + 1], accum_out=b.ts[2][:, i:i + 1]).then_inc(
                                             *K.step("scalar", f"t_exp{i}", frees="te"))
                act.wait_ge(*K.ready("tensor", "tpT"))
                nc.scalar.copy(b.TPT[:, :, :].rearrange("p k t -> p (k t)"), K.bank("tpT")).then_inc(
                    *K.step("scalar", "tpT", frees="tpT"))
                turned(K, b, "tT")

            act.wait_ge(w_loaded["small"], 16 * N_SMALL)
            act.wait_ge(w_loaded["mom"], 16 * N_MOM)
            act.wait_ge(s_half, 2)
            act.wait_ge(s_const, CONSTS)
            with act.Fori(0, PAIRS) as turn:
                K2 = keys(turn)
                for stage in (mamba_in, mamba_ssd, mamba_out, rot_in, rot_max, rot_heads, rot_out,
                              low_rank, mom_in, mom_heads, mom_out, feat):
                    for K, b in zip(K2, bufs):
                        stage(K, b)
                turn_end(act, turn)
                act.wait_ge(started, turn + 1)

        @block.tensor
        def _(pe):
            def take(K, name, banks=(0, 1, 2, 3)):
                ps, wait = K.take(name, banks)
                if wait is not None:
                    pe.wait_ge(*wait)
                return ps

            def mm(out, lhsT, rhs, first, last):
                return nc.tensor.matmul(out, lhsT, rhs, start=first, stop=last)

            def turn_tiles(K, name, src, cols=KD, banks=(0, 1, 2, 3), c0=0):
                ps = take(K, name, banks)
                for k in range(cols):
                    for i in range(NT):
                        last = nc.tensor.transpose(ps[:, k * T + i * P:k * T + (i + 1) * P],
                                                   src[:, i, (c0 + k) * P:(c0 + k + 1) * P], ident[:, :])
                last.then_inc(*K.step("tensor", name))

            def mamba_in(K, b):
                pe.wait_ge(*K.ready("vector", "h_scaled"))
                turn_tiles(K, "hT", b.H)
                pe.wait_ge(*K.ready("scalar", "hT1"))
                for j in range(NCH // 2):
                    ps = take(K, f"xbc{j}")
                    for c in (2 * j, 2 * j + 1):
                        for k in range(KD):
                            last = mm(ps[:, (c % 2) * T:(c % 2 + 1) * T], w_in[:, k, DI + c * P:DI + (c + 1) * P],
                                      b.AT[:, k, :], k == 0, k == KD - 1)
                    last.then_inc(*K.step("tensor", f"xbc{j}"))
                ps = take(K, "dt")
                for i in range(NT):
                    for k in range(KD):
                        last = mm(ps[:, i * MH:(i + 1) * MH], b.AT[:, k, i * P:(i + 1) * P],
                                  w_in[:, k, DI + NCH * P:DI + NCH * P + MH], k == 0, k == KD - 1)
                last.then_inc(*K.step("tensor", "dt"))
                for i in range(NT):
                    ps = take(K, f"z{i}")
                    for k in range(KD):
                        last = mm(ps, b.AT[:, k, i * P:(i + 1) * P], w_in[:, k, 0:DI], k == 0, k == KD - 1)
                    last.then_inc(*K.step("tensor", f"z{i}"))

            def mamba_ssd(K, b):
                pe.wait_ge(*K.ready("vector", "xbc2"))
                ps = take(K, "cb")
                for i in range(NT):
                    last = mm(ps[:, i * P:(i + 1) * P], b.XBC[:, KI, i * P:(i + 1) * P],
                              b.XBC[:, KI + 1, i * P:(i + 1) * P], True, True)
                last.then_inc(*K.step("tensor", "cb"))
                ps = take(K, "bT")
                nc.tensor.transpose(ps[:, 0:NS], b.XBC[:, KI, 0:P], ident[:, :]).then_inc(*K.step("tensor", "bT"))
                for i in range(NT):
                    ps = take(K, f"xsT{i}")
                    for c in range(KI):
                        last = nc.tensor.transpose(ps[:, c * P:(c + 1) * P], b.XBC[:, c, i * P:(i + 1) * P],
                                                   ident[:, :])
                    last.then_inc(*K.step("tensor", f"xsT{i}"))
                pe.wait_ge(*K.ready("vector", "dA"))
                ps = take(K, "cum")
                mm(ps[:, 0:MH], gt[:, :], b.dA[:, 0, :], True, True)
                mm(ps[:, MH:2 * MH], le[:, :], b.dA[:, 1, :], True, True).then_inc(*K.step("tensor", "cum"))
                for i in range(NT):
                    pe.wait_ge(*K.ready("pool", f"dA_rows{i}"))
                    for j in range(2):
                        ps = take(K, f"seg{i}{j}")
                        mm(ps, gt[:, :], b.E[i][:, 4 * j:4 * j + 4, :].rearrange("p h l -> p (h l)"),
                           True, True).then_inc(*K.step("tensor", f"seg{i}{j}"))
                pe.wait_ge(*K.ready("pool", "x_decayed"))
                pe.wait_ge(*K.ready("scalar", "bT"))
                mm(take(K, "state"), b.BT[:, :], b.XDEC[:, :], True, True).then_inc(*K.step("tensor", "state"))
                for i in range(NT):
                    pe.wait_ge(*K.ready("vector", f"M{i}"))
                    ps = take(K, f"y{i}")
                    for h in range(MH):
                        last = mm(ps[:, h * MP:(h + 1) * MP], b.E[i][:, h, :], b.XDT[:, i, h * MP:(h + 1) * MP],
                                  True, True)
                    last.then_inc(*K.step("tensor", f"y{i}"))
                pe.wait_ge(*K.ready("scalar", "state"))
                mm(take(K, "yoff"), b.XBC[:, KI + 1, P:2 * P], b.ST[:, :], True, True).then_inc(
                    *K.step("tensor", "yoff"))

            def mamba_out(K, b):
                pe.wait_ge(*K.ready("vector", "gated1"))
                for j in range(2):
                    turn_tiles(K, f"ynT{j}", b.XT, c0=2 * j)
                pe.wait_ge(*K.ready("scalar", "yT3"))
                ps = take(K, "mo")
                for i in range(NT):
                    for k in range(KI):
                        last = mm(ps[:, i * D:(i + 1) * D], b.YT[:, k, i * P:(i + 1) * P], w_mo[:, k, :],
                                  k == 0, k == KI - 1)
                last.then_inc(*K.step("tensor", "mo"))
                pe.wait_ge(*K.ready("vector", "h2"))
                turn_tiles(K, "h2T", b.H)
                pe.wait_ge(*K.ready("scalar", "h2T1"))
                for j in range(KG):
                    m = min(P, INTER - j * P)
                    ps = take(K, f"gu{j}")
                    for n, w in enumerate((w_gate, w_up)):
                        for k in range(KD):
                            last = mm(ps[0:m, n * T:(n + 1) * T], w[:, k, j * P:j * P + m], b.AT[:, k, :],
                                      k == 0, k == KD - 1)
                    last.then_inc(*K.step("tensor", f"gu{j}"))
                pe.wait_ge(*K.ready("vector", f"ma{KG - 1}"))
                ps = take(K, "down")
                for i in range(NT):
                    for j in range(KG):
                        m = min(P, INTER - j * P)
                        last = mm(ps[:, i * D:(i + 1) * D], b.MA[0:m, j, i * P:(i + 1) * P], w_down[0:m, j, :],
                                  j == 0, j == KG - 1)
                last.then_inc(*K.step("tensor", "down"))

            def turn_heads(K, name, src):
                for c in range(2):
                    ps = take(K, f"{name}{c}")
                    for n in range(2 if c == 0 else 1):
                        c0 = (2 * c + n) * SHIFT
                        m = min(SHIFT, D - c0)
                        for i in range(NT):
                            last = nc.tensor.transpose(ps[0:m, n * T + i * P:n * T + (i + 1) * P],
                                                       src[:, i, c0:c0 + m], ident[:, :])
                    last.then_inc(*K.step("tensor", f"{name}{c}"))

            def rot_in(K, b):
                for n, c in (("xk", 0), ("xv", D)):
                    ps = take(K, n)
                    for i in range(NT):
                        last = mm(ps[:, i * D:(i + 1) * D], b.CT[:, i * P:(i + 1) * P], w_xkv[:, c:c + D], True, True)
                    last.then_inc(*K.step("tensor", n))
                pe.wait_ge(*K.ready("vector", "k_turned"))
                turn_heads(K, "xkT", b.KR)
                pe.wait_ge(*K.ready("vector", "xn21"))
                turn_tiles(K, "xT", b.XN)
                pe.wait_ge(*K.ready("scalar", "xT"))
                ps = take(K, "xq")
                for i in range(NT):
                    for k in range(KD):
                        last = mm(ps[:, i * D:(i + 1) * D], b.AT[:, k, i * P:(i + 1) * P], w_xq[:, k, :],
                                  k == 0, k == KD - 1)
                last.then_inc(*K.step("tensor", "xq"))
                pe.wait_ge(*K.ready("vector", "q_turned"))
                turn_heads(K, "xqT", b.QR)

            def rot_max(K, b):
                pe.wait_ge(*K.ready("pool", "k_low"))
                for p in range(NPAIR):
                    pe.wait_ge(*K.ready("scalar", ("q_low", p)))
                    for i in range(NT):
                        ps = take(K, ("xs", p, i), (0, 1, 2))
                        for e in range(2):
                            last = mm(ps[:, e * T:(e + 1) * T], b.QMB[p % 2][:, e, i * P:(i + 1) * P],
                                      b.KTB[:, (2 * p + e) // HT, :], True, True)
                        last.then_inc(*K.step("tensor", ("xs", p, i)))
                    K.name_last("tensor", ("xs", p))
                pe.wait_ge(*K.ready("vector", "x_max"))
                ps = take(K, "xm", (0, 1, 2))
                for i in range(NT):
                    last = nc.tensor.transpose(ps[0:XH, i * P:(i + 1) * P], b.MX[:, i, :], ident[:, :])
                last.then_inc(*K.step("tensor", "xm"))

            def rot_heads(K, b):
                for p in range(NPAIR + 1):
                    if p < NPAIR:
                        pe.wait_ge(*K.ready("scalar", ("q_masked", p)))
                        pe.wait_ge(slot_rows[K.s][p % QSLOTS], 16 * (p // QSLOTS + 1))
                        for k in range(NT):
                            ps = take(K, ("xt", p, k), (0, 1, 2))
                            mm(ps, b.KT[:, 2 * p // HT, k * P:(k + 1) * P],
                               b.QM[p % QSLOTS][:, :, :].rearrange("p e t -> p (e t)"), True, True).then_inc(
                                   *K.step("tensor", ("xt", p, k)))
                    if p >= 1:
                        weigh(K, b, p - 1)

            def weigh(K, b, p):
                g = p % 4
                if p % 4 == 0:
                    take(K, ("xo", p // 4), (3,))
                ps = K.bank(("xo", p // 4))
                pe.wait_ge(*K.ready("scalar", ("weights", p, 1)))
                for e in range(2):
                    for k in range(NT):
                        last = mm(ps[32 * g:32 * g + 32, e * T:(e + 1) * T], b.V1[:, k, 2 * p + e, :],
                                  b.PT[p % 3][:, k, e, :], k == 0, k == NT - 1)
                last.then_inc(*K.step("tensor", ("weighed", p)))
                if p % 4 == 3:
                    g4 = p // 4
                    K.name_last("tensor", ("xo", g4))
                    pe.wait_ge(*K.ready("scalar", ("oT", g4)))
                    ps = take(K, ("xoT", g4), (0, 1, 2))
                    for e in range(2):
                        for i in range(NT):
                            last = nc.tensor.transpose(ps[:, (2 * e + i) * P:(2 * e + i + 1) * P],
                                                       b.OT[g4 % 2][:, e, i * P:(i + 1) * P], ident[:, :])
                    last.then_inc(*K.step("tensor", ("xoT", g4)))

            def rot_out(K, b):
                pe.wait_ge(*K.ready("vector", "x_heads3"))
                turn_tiles(K, "xoF", b.O)
                pe.wait_ge(*K.ready("scalar", "xoF"))
                ps = take(K, "xout")
                for i in range(NT):
                    for k in range(KD):
                        last = mm(ps[:, i * D:(i + 1) * D], b.AT[:, k, i * P:(i + 1) * P], w_xo[:, k, :],
                                  k == 0, k == KD - 1)
                last.then_inc(*K.step("tensor", "xout"))

            def low_rank(K, b):
                pe.wait_ge(*K.ready("vector", "xn31"))
                turn_tiles(K, "fT", b.XN)
                pe.wait_ge(*K.ready("scalar", "fT"))
                ps = take(K, "fr")
                for i in range(NT):
                    for k in range(KD):
                        last = mm(ps[:, i * FE:(i + 1) * FE], b.AT[:, k, i * P:(i + 1) * P], w_fr[:, k, :],
                                  k == 0, k == KD - 1)
                last.then_inc(*K.step("tensor", "fr"))
                for j in range(FE // 2 + 1):
                    if j < FE // 2:
                        ps = take(K, ("fa", j))
                        for e in range(2):
                            for k in range(KD):
                                last = mm(ps[:, e * T:(e + 1) * T], w_fa[:, 2 * j + e, k, :], b.AT[:, k, :],
                                          k == 0, k == KD - 1)
                        last.then_inc(*K.step("tensor", ("fa", j)))
                    if j >= 1:
                        pe.wait_ge(*K.ready("scalar", ("fh", j - 1)))
                        for e in range(2):
                            x = 2 * (j - 1) + e
                            ps = take(K, ("fb", x))
                            for i in range(NT):
                                last = mm(ps[:, i * D:(i + 1) * D], b.FH[(j - 1) % 2][:, e, i * P:(i + 1) * P],
                                          w_fb[:, x, :], True, True)
                            last.then_inc(*K.step("tensor", ("fb", x)))

            def mom_in(K, b):
                pe.wait_ge(*K.ready("vector", "xn41"))
                turn_tiles(K, "aT", b.XN)
                pe.wait_ge(*K.ready("scalar", "aT"))
                for n, w in (("aq", w_aq), ("ak", w_ak)):
                    ps = take(K, n)
                    for m in range(KD):
                        for k in range(KD):
                            last = mm(ps[:, m * T:(m + 1) * T], w[:, k, m * P:(m + 1) * P], b.AT[:, k, :],
                                      k == 0, k == KD - 1)
                    last.then_inc(*K.step("tensor", n))
                for i in range(NT):
                    ps = take(K, f"av{i}")
                    for k in range(KD):
                        last = mm(ps, b.AT[:, k, i * P:(i + 1) * P], w_av[:, k, :], k == 0, k == KD - 1)
                    last.then_inc(*K.step("tensor", f"av{i}"))
                pe.wait_ge(*K.ready("scalar", "aq"))
                ps = take(K, "al")
                for i in range(NT):
                    for k in range(KD):
                        c = 32 * i + 16 * k
                        last = mm(ps[:, c:c + 16], b.AQ[:, k, i * P:(i + 1) * P],
                                  w_al[:, :, :].rearrange("p a n -> p (a n)"), True, True)
                last.then_inc(*K.step("tensor", "al"))
                pe.wait_ge(*K.ready("vector", "a_mask"))
                ps = take(K, "amT")
                for i in range(NT):
                    last = nc.tensor.transpose(ps[0:AH * AR, i * P:(i + 1) * P],
                                               b.MK[:, i, :, :].rearrange("p h r -> p (h r)"), ident[:, :])
                last.then_inc(*K.step("tensor", "amT"))

            def mom_project(K, b, h):
                a, kk, m = h % 4, h // 4, RH * AD
                r = slice(32 * a, 32 * a + 32)
                for n, w, src in (("aeq", w_aeq, b.AQ), ("aek", w_aek, b.AK)):
                    pe.wait_ge(*K.ready("scalar", "ak"))
                    ps = take(K, (n, h), (0, 1, 2))
                    for rh in range(2):
                        last = mm(ps[0:m, rh * T:(rh + 1) * T], w[r, kk, rh * m:(rh + 1) * m], src[r, kk, :],
                                  True, True)
                    last.then_inc(*K.step("tensor", (n, h)))
                pe.wait_ge(*K.ready("scalar", "mask_rows"))
                ps = take(K, ("aem", h), (0, 1, 2))
                for rh in range(2):
                    last = mm(ps[0:m, rh * T:(rh + 1) * T], spread[:, 2 * h + rh, :], b.MKT[:, :], True, True)
                last.then_inc(*K.step("tensor", ("aem", h)))

            def mom_max(K, b, h):
                pe.wait_ge(*K.ready("pool", ("ke_low", h)))
                for q in range(AR):
                    rh, g = q // RH, q % RH
                    ps = take(K, ("as", h, q), (0, 1, 2))
                    for i in range(NT):
                        last = mm(ps[:, i * T:(i + 1) * T], b.QEB[:, rh, g, i * P:(i + 1) * P],
                                  b.KEB[:, rh, :], True, True)
                    last.then_inc(*K.step("tensor", ("as", h, q)))

            def mom_turn_max(K, b, h):
                pe.wait_ge(*K.ready("vector", ("a_max", h)))
                ps = take(K, ("am", h), (0, 1, 2))
                for i in range(NT):
                    last = nc.tensor.transpose(ps[0:AR, i * P:(i + 1) * P], b.AMX[:, i, :], ident[:, :])
                last.then_inc(*K.step("tensor", ("am", h)))

            def mom_heads(K, b):
                for h in range(-1, AH):
                    if h + 1 < AH:
                        mom_project(K, b, h + 1)
                        mom_max(K, b, h + 1)
                    if h >= 0:
                        pe.wait_ge(rowed[K.s], 16 * (h + 1))
                        for q in range(AR + 1):
                            if q < AR:
                                rh, g = q // RH, q % RH
                                ps = take(K, ("at", h, q), (0, 1, 2))
                                for k in range(NT):
                                    last = mm(ps[:, k * T:(k + 1) * T], b.KE[h % 2][:, rh, k * P:(k + 1) * P],
                                              b.QE[h % 2][:, rh, g, :], True, True)
                                last.then_inc(*K.step("tensor", ("at", h, q)))
                            if q >= 1:
                                mom_weigh(K, b, h, q - 1)
                        for i in range(NT):
                            pe.wait_ge(*K.ready("scalar", ("aoT", h, AR // 2 - 1)))
                            ps = take(K, ("aoT", h, i), (0, 1, 2))
                            for q in range(AR):
                                last = nc.tensor.transpose(ps[:, q * VW:(q + 1) * VW], b.AOT[:, q, i * P:(i + 1) * P],
                                                           ident[0:VW, 0:VW])
                            last.then_inc(*K.step("tensor", ("aoT", h, i)))
                    if h + 1 < AH:
                        mom_turn_max(K, b, h + 1)

            def mom_weigh(K, b, h, q):
                n = h * AR + q
                if q % 2 == 0:
                    take(K, ("ao", h, q // 2), (3,))
                ps = K.bank(("ao", h, q // 2))
                if q == 2:
                    pe.wait_ge(*K.ready("vector", ("vm", h)))
                pe.wait_ge(*K.ready("scalar", ("weights_a", n)))
                for k in range(NT):
                    v = b.AV[:, k, h, :] if q < AS else b.VM[h % 2][:, k, q - AS, :]
                    last = mm(ps[0:VW, (q % 2) * T:(q % 2 + 1) * T], v, b.APT[n % 2][:, k, :], k == 0, k == NT - 1)
                last.then_inc(*K.step("tensor", ("weighed_a", n)))
                if q % 2 == 1:
                    K.name_last("tensor", ("ao", h, q // 2))

            def mom_out(K, b):
                for i in range(NT):
                    ps = take(K, f"ag{i}")
                    for k in range(KD):
                        last = mm(ps, b.AT[:, k, i * P:(i + 1) * P], w_ag[:, k, :], k == 0, k == KD - 1)
                    last.then_inc(*K.step("tensor", f"ag{i}"))
                pe.wait_ge(*K.ready("vector", "a_gated1"))
                for j in range(2):
                    turn_tiles(K, f"aoF{j}", b.AO, c0=2 * j)
                pe.wait_ge(*K.ready("scalar", "ayT1"))
                ps = take(K, "aout")
                for i in range(NT):
                    for k in range(AH * AV // P):
                        last = mm(ps[:, i * D:(i + 1) * D], b.AYT[:, k, i * P:(i + 1) * P], w_ao[:, k, :],
                                  k == 0, k == AH * AV // P - 1)
                last.then_inc(*K.step("tensor", "aout"))

            def feat(K, b):
                for n, w in (("tq", w_tq), ("tk", w_tk)):
                    mm(take(K, n)[:, 0:T], w[:, :], b.CT[:, :], True, True).then_inc(*K.step("tensor", n))
                pe.wait_ge(*K.ready("scalar", "tk"))
                ps = take(K, "te")
                for i in range(NT):
                    last = mm(ps[:, i * T:(i + 1) * T], b.TQ[:, i * P:(i + 1) * P], b.TK[:, :], True, True)
                last.then_inc(*K.step("tensor", "te"))
                pe.wait_ge(*K.ready("vector", "t_norm1"))
                turn_tiles(K, "tpT", b.TP)
                pe.wait_ge(*K.ready("vector", "xn51"))
                turn_tiles(K, "tT", b.XN)
                pe.wait_ge(*K.ready("scalar", "tT"))
                ps = take(K, "tout")
                for i in range(NT):
                    for k in range(KD):
                        last = mm(ps[:, i * D:(i + 1) * D], b.AT[:, k, i * P:(i + 1) * P], b.TPT[:, k, :],
                                  k == 0, k == KD - 1)
                last.then_inc(*K.step("tensor", "tout"))

            pe.wait_ge(s_const, CONSTS)
            for n, c in (("mamba", N_MAMBA), ("rot", N_ROT), ("fexp", N_FEXP), ("mom", N_MOM), ("feat", N_FEAT)):
                pe.wait_ge(w_loaded[n], 16 * c)
            with pe.Fori(0, PAIRS) as turn:
                K2 = keys(turn)
                for stage in (mamba_in, mamba_ssd, mamba_out, rot_in, rot_max, rot_heads, rot_out, low_rank, mom_in,
                              mom_heads, mom_out, feat):
                    for K, b in zip(K2, bufs):
                        stage(K, b)
                turn_end(pe, turn)
                pe.wait_ge(started, turn + 1)

        @block.vector
        def _(dve):
            def statistics(K, b, q):
                for i in range(NT):
                    nc.vector.bn_stats(b.bst[:, i, :], b.X[:, i, :]).then_inc(*K.step("vector"))
                dve.wait_ge(*K.last("vector"))
                for i in range(NT):
                    nc.vector.bn_aggr(b.mv[:, i, :], b.bst[:, i, :]).then_inc(*K.step("vector", f"stat{q}{i}"))

            def normalised(K, b, q):
                statistics(K, b, q)
                dve.wait_ge(*K.last("vector"))
                dve.wait_ge(*K.ready("pool", f"rstd{q}"))
                for i in range(NT):
                    nc.vector.tensor_scalar(b.XN[:, i, :], b.X[:, i, :], b.mv[:, i, 0:1], b.rstd[:, i:i + 1],
                                            ALU.subtract, ALU.mult).then_inc(*K.step("vector", f"xn{q}{i}"))

            def heads_in(t, n):
                return t.unsqueeze(2).broadcast_to([P, MH, n])

            def mamba_in(K, b):
                dve.wait_ge(loaded[K.s], 32)
                normalised(K, b, 1)
                dve.wait_ge(*K.ready("pool", "h_scale"))
                for i in range(NT):
                    nc.vector.tensor_scalar(b.H[:, i, :], b.X[:, i, :], b.mv[:, i, 0:1], b.rh[:, i:i + 1],
                                            ALU.subtract, ALU.mult).then_inc(*K.step("vector"))
                K.name_last("vector", "h_scaled")
                for j in range(NCH // 2):
                    ps = K.bank(f"xbc{j}")
                    dve.wait_ge(*K.ready("tensor", f"xbc{j}"))
                    for n in range(1, 4):
                        for c in (2 * j, 2 * j + 1):
                            if n == 1:
                                dve.wait_ge(*K.ready("scalar", f"tap{2 * j + 1}"))
                            elif c == 2 * j:
                                dve.wait_ge(*K.last("vector"))
                            t0 = (c % 2) * T
                            nc.vector.scalar_tensor_tensor(
                                out=b.XBC[:, c, n:T], in0=ps[:, t0:t0 + T - n], scalar=cw[:, c, 3 - n:4 - n],
                                in1=b.XBC[:, c, n:T], op0=ALU.mult, op1=ALU.add).then_inc(
                                    *K.step("vector", f"conv{j}" if (n, c) == (3, 2 * j + 1) else None,
                                            frees=f"xbc{j}" if (n, c) == (3, 2 * j + 1) else None))
                dve.wait_ge(*K.ready("tensor", "dt"))
                nc.vector.tensor_tensor(b.raw, K.bank("dt")[:, 0:NT * MH].rearrange("p (i h) -> p i h", i=NT),
                                        dtb[:, :].unsqueeze(1).broadcast_to([P, NT, MH]), ALU.add).then_inc(
                                            *K.step("vector", frees="dt"))
                dve.wait_ge(*K.last("vector"))
                nc.vector.scalar_tensor_tensor(out=b.nab, in0=b.raw, scalar=-1.0, in1=b.raw, op0=ALU.mult,
                                               op1=ALU.min).then_inc(*K.step("vector", "dt_low"))
                for i in range(NT):
                    dve.wait_ge(*K.ready("scalar", f"thz{i}"))
                    nc.vector.scalar_tensor_tensor(out=b.G[:, i, :], in0=b.G[:, i, :], scalar=1.0,
                                                   in1=K.bank(f"z{i}"), op0=ALU.add, op1=ALU.mult).then_inc(
                                                       *K.step("vector", f"z_gate{i}", frees=f"z{i}"))
                for j in range(NCH // 2):
                    dve.wait_ge(*K.ready("scalar", f"th{j}"))
                    nc.vector.scalar_tensor_tensor(out=b.XBC[:, 2 * j:2 * j + 2, :], in0=b.TH[:, 2 * j:2 * j + 2, :],
                                                   scalar=1.0, in1=b.XBC[:, 2 * j:2 * j + 2, :], op0=ALU.add,
                                                   op1=ALU.mult).then_inc(*K.step("vector", f"xbc{j}"))
                dve.wait_ge(*K.ready("scalar", "dt_exp"))
                nc.vector.tensor_scalar(b.z2, b.u, 2.0, None, ALU.add).then_inc(*K.step("vector"))
                dve.wait_ge(*K.last("vector"))
                nc.vector.reciprocal(b.z, b.z2).then_inc(*K.step("vector"))
                dve.wait_ge(*K.last("vector"))
                nc.vector.tensor_tensor(b.z, b.z, b.u, ALU.mult).then_inc(*K.step("vector"))
                dve.wait_ge(*K.last("vector"))
                nc.vector.tensor_tensor(b.z2, b.z, b.z, ALU.mult).then_inc(*K.step("vector"))
                dve.wait_ge(*K.last("vector"))
                nc.vector.tensor_scalar(b.ser, b.z2, 1.0 / 17, None, ALU.mult).then_inc(*K.step("vector"))
                for n in range(15, 1, -2):
                    dve.wait_ge(*K.last("vector"))
                    nc.vector.scalar_tensor_tensor(out=b.ser, in0=b.ser, scalar=1.0 / n, in1=b.z2, op0=ALU.add,
                                                   op1=ALU.mult).then_inc(*K.step("vector"))
                dve.wait_ge(*K.last("vector"))
                nc.vector.scalar_tensor_tensor(out=b.ser, in0=b.ser, scalar=1.0, in1=b.z, op0=ALU.add,
                                               op1=ALU.mult).then_inc(*K.step("vector"))
                nc.vector.tensor_scalar(b.raw, b.raw, 0.0, None, ALU.max).then_inc(*K.step("vector"))
                dve.wait_ge(*K.last("vector"))
                nc.vector.scalar_tensor_tensor(out=b.dt, in0=b.ser, scalar=2.0, in1=b.raw, op0=ALU.mult,
                                               op1=ALU.add).then_inc(*K.step("vector"))
                dve.wait_ge(*K.last("vector"))
                nc.vector.tensor_tensor(b.dA, b.dt, aneg[:, :].unsqueeze(1).broadcast_to([P, NT, MH]),
                                        ALU.mult).then_inc(*K.step("vector", "dA"))

            def mamba_ssd(K, b):
                dve.wait_ge(*K.ready("tensor", "cb"))
                for i in range(NT):
                    nc.vector.tensor_tensor(b.CB[:, i, :], K.bank("cb")[:, i * P:(i + 1) * P], le[:, :],
                                            ALU.mult).then_inc(*K.step("vector", frees="cb"))
                for i in range(NT):
                    dve.wait_ge(*K.ready("scalar", f"xs{i}"))
                    nc.vector.tensor_tensor(b.XDT[:, i, :].rearrange("p (h d) -> p h d", h=MH),
                                            K.bank(f"xsT{i}").rearrange("p (h d) -> p h d", h=MH),
                                            heads_in(b.dt[:, i, :], MP), ALU.mult).then_inc(
                                                *K.step("vector", f"x_dt{i}", frees=f"xsT{i}"))
                for i in range(NT):
                    dve.wait_ge(*K.ready("scalar", f"L{i}1"))
                    nc.vector.tensor_tensor(b.E[i][:, :, :], b.E[i][:, :, :],
                                            b.CB[:, i, :].unsqueeze(1).broadcast_to([P, MH, P]), ALU.mult).then_inc(
                                                *K.step("vector", f"M{i}"))

            def mamba_out(K, b):
                dve.wait_ge(*K.ready("tensor", "yoff"))
                nc.vector.tensor_tensor(b.YO[:, :].rearrange("p (h d) -> p h d", h=MH),
                                        K.bank("yoff").rearrange("p (h d) -> p h d", h=MH),
                                        heads_in(b.dcy[:, MH:2 * MH], MP), ALU.mult).then_inc(
                                            *K.step("vector", frees="yoff"))
                for i in range(NT):
                    dve.wait_ge(*K.ready("pool", f"x_skip{i}"))
                    dve.wait_ge(*K.ready("tensor", f"y{i}"))
                    nc.vector.tensor_tensor(b.XT[:, i, :], K.bank(f"y{i}"), b.XT[:, i, :], ALU.add).then_inc(
                        *K.step("vector", frees=f"y{i}"))
                dve.wait_ge(*K.last("vector"))
                nc.vector.tensor_tensor(b.XT[:, 1, :], b.XT[:, 1, :], b.YO[:, :], ALU.add).then_inc(*K.step("vector"))
                dve.wait_ge(*K.last("vector"))
                for i in range(NT):
                    nc.vector.tensor_tensor(b.XT[:, i, :], b.XT[:, i, :], b.G[:, i, :], ALU.mult).then_inc(
                        *K.step("vector", f"gated{i}"))
                dve.wait_ge(*K.ready("tensor", "mo"))
                dve.wait_ge(*K.ready("pool", "y_scale"))
                for i in range(NT):
                    nc.vector.scalar_tensor_tensor(out=b.H1[:, i, :], in0=K.bank("mo")[:, i * D:(i + 1) * D],
                                                   scalar=b.rs[:, i:i + 1], in1=b.XN[:, i, :], op0=ALU.mult,
                                                   op1=ALU.add).then_inc(*K.step("vector", f"h1{i}", frees="mo"))
                dve.wait_ge(*K.ready("pool", "h1_scale"))
                for i in range(NT):
                    nc.vector.tensor_scalar(b.H[:, i, :], b.H1[:, i, :], b.rs2[:, i:i + 1], None, ALU.mult).then_inc(
                        *K.step("vector"))
                K.name_last("vector", "h2")
                for j in range(KG):
                    m = min(P, INTER - j * P)
                    ps = K.bank(f"gu{j}")
                    dve.wait_ge(*K.ready("scalar", f"thg{j}"))
                    nc.vector.scalar_tensor_tensor(out=b.MA[0:m, j, :], in0=b.MTH[0:m, j % 2, :], scalar=1.0,
                                                   in1=ps[0:m, 0:T], op0=ALU.add, op1=ALU.mult).then_inc(
                                                       *K.step("vector"))
                    dve.wait_ge(*K.last("vector"))
                    nc.vector.tensor_tensor(b.MA[0:m, j, :], b.MA[0:m, j, :], ps[0:m, T:2 * T], ALU.mult).then_inc(
                        *K.step("vector", f"ma{j}", frees=f"gu{j}"))
                dve.wait_ge(*K.ready("tensor", "down"))
                dve.wait_ge(*K.ready("pool", "x_h1"))
                for i in range(NT):
                    nc.vector.scalar_tensor_tensor(out=b.X[:, i, :], in0=K.bank("down")[:, i * D:(i + 1) * D],
                                                   scalar=0.5, in1=b.X[:, i, :], op0=ALU.mult,
                                                   op1=ALU.add).then_inc(*K.step("vector", frees="down"))
                dve.wait_ge(*K.last("vector"))

            def rotate(K, b, group, out, name):
                ps = K.bank(group)
                sc = b.sc
                dve.wait_ge(*K.ready("tensor", group))
                for i in range(NT):
                    x = ps[:, i * D:(i + 1) * D].rearrange("p (h f e) -> p h f e", f=4, e=2)
                    for t, c in ((b.QS, 0), (b.QC, 4)):
                        for e in range(2):
                            nc.vector.tensor_tensor(
                                t[:, i, :].rearrange("p (h f e) -> p h f e", f=4, e=2)[:, :, :, e], x[:, :, :, e],
                                sc[:, i, c:c + 4].unsqueeze(1).broadcast_to([P, XH, 4]), ALU.mult).then_inc(
                                    *K.step("vector", frees=group))
                dve.wait_ge(*K.last("vector"))
                qs, qc, o = (t[:, :, :].rearrange("p i (n e) -> p i n e", e=2) for t in (b.QS, b.QC, out))
                nc.vector.tensor_tensor(o[:, :, :, 0], qc[:, :, :, 0], qs[:, :, :, 1], ALU.subtract).then_inc(
                    *K.step("vector"))
                nc.vector.tensor_tensor(o[:, :, :, 1], qs[:, :, :, 0], qc[:, :, :, 1], ALU.add).then_inc(
                    *K.step("vector", name))
                dve.wait_ge(*K.last("vector"))

            def rot_in(K, b):
                nc.vector.tensor_copy(b.sc.rearrange("p i c -> p (i c)"), sincos[:, K.turn, K.s, :]).then_inc(
                    *K.step("vector"))
                dve.wait_ge(*K.last("vector"))
                rotate(K, b, "xk", b.KR, "k_turned")
                normalised(K, b, 2)
                rotate(K, b, "xq", b.QR, "q_turned")

            def rot_max(K, b):
                for p in range(NPAIR):
                    h0 = 2 * p
                    for i in range(NT):
                        dve.wait_ge(*K.ready("tensor", ("xs", p, i)))
                        nc.vector.tensor_reduce(b.MX[:, i, h0:h0 + 2],
                                                K.bank(("xs", p, i)).rearrange("p (e t) -> p e t", e=2), AX.X, ALU.max,
                                                ).then_inc(*K.step("vector", frees=("xs", p, i)))
                dve.wait_ge(*K.last("vector"))
                nc.vector.tensor_scalar(b.MX[:, :, :], b.MX[:, :, :], -1.0, None, ALU.mult).then_inc(
                    *K.step("vector", "x_max"))
                dve.wait_ge(*K.ready("tensor", "xm"))
                nc.vector.tensor_copy(b.NMT[:, :], K.bank("xm")[0:XH, 0:T]).then_inc(
                    *K.step("vector", "xnm", frees="xm"))

            def rot_heads(K, b):
                for g4 in range(NPAIR // 4):
                    dve.wait_ge(*K.ready("tensor", ("xoT", g4)))
                    ps = K.bank(("xoT", g4)).rearrange("p (n c d) -> p n c d", n=4, d=32)
                    if g4:
                        dve.wait_ge(*K.last("vector"))
                    nc.vector.reciprocal(b.RD[:, :, :], ps[:, :, :, XD]).then_inc(*K.step("vector"))
                    dve.wait_ge(*K.last("vector"))
                    for e in range(2):
                        for i in range(NT):
                            o = b.O[:, i, :].rearrange("p (h d) -> p h d", d=XD)[:, 8 * g4 + e:8 * g4 + 8:2, :]
                            nc.vector.tensor_tensor(o, ps[:, 2 * e + i, :, 0:XD],
                                                    b.RD[:, 2 * e + i, :].unsqueeze(2).broadcast_to([P, 4, XD]),
                                                    ALU.mult).then_inc(*K.step("vector", frees=("xoT", g4)))
                    K.name_last("vector", f"x_heads{g4}")

            def add_block(K, b, name, wait=None):
                dve.wait_ge(*K.ready("tensor", name))
                nc.vector.tensor_tensor(b.X[:, :, :].rearrange("p i d -> p (i d)"), K.bank(name),
                                        b.X[:, :, :].rearrange("p i d -> p (i d)"), ALU.add).then_inc(
                                            *K.step("vector", frees=name))
                dve.wait_ge(*K.last("vector"))

            def rot_out(K, b):
                dve.wait_ge(*K.ready("pool", "x_bias"))
                add_block(K, b, "xout")

            def low_rank(K, b):
                normalised(K, b, 3)
                lg, lo, ex, v8, gt_, eq, cum, sel = b.f[0], b.f[1], b.f[2], b.f[3], b.f[4], b.f[5], b.f[6], b.f[7]
                comb = b.f[8]
                need, tot = b.fs[0], b.fs[1]
                dve.wait_ge(*K.ready("tensor", "fr"))
                dve.wait_ge(*K.ready("pool", "f_inverse"))
                for i in range(NT):
                    nc.vector.tensor_scalar(lg[:, i, :], K.bank("fr")[:, i * FE:(i + 1) * FE], b.rs[:, i:i + 1], None,
                                            ALU.mult).then_inc(*K.step("vector", frees="fr"))
                dve.wait_ge(*K.last("vector"))
                for i in range(NT):
                    nc.vector.max(v8[:, i, :], lg[:, i, :]).then_inc(*K.step("vector"))
                dve.wait_ge(*K.last("vector"))
                nc.vector.tensor_tensor(lo, lg, v8[:, :, 0:1].broadcast_to([P, NT, FE]), ALU.subtract).then_inc(
                    *K.step("vector", "f_shifted"))
                second = v8[:, :, 1:2].broadcast_to([P, NT, FE])
                nc.vector.tensor_tensor(gt_, lg, second, ALU.is_gt).then_inc(*K.step("vector"))
                nc.vector.tensor_tensor(eq, lg, second, ALU.is_equal).then_inc(*K.step("vector"))
                dve.wait_ge(*K.last("vector"))
                nc.vector.tensor_reduce(need, gt_, AX.X, ALU.add).then_inc(*K.step("vector"))
                for i in range(NT):
                    nc.vector.tensor_tensor_scan(cum[:, i, :], eq[:, i, :], eq[:, i, :], 0.0, ALU.add,
                                                 ALU.max).then_inc(*K.step("vector"))
                dve.wait_ge(*K.last("vector"))
                nc.vector.tensor_tensor(cum, cum, need.unsqueeze(2).broadcast_to([P, NT, FE]), ALU.add).then_inc(
                    *K.step("vector"))
                dve.wait_ge(*K.last("vector"))
                nc.vector.scalar_tensor_tensor(out=eq, in0=cum, scalar=2.5, in1=eq, op0=ALU.is_lt,
                                               op1=ALU.mult).then_inc(*K.step("vector"))
                dve.wait_ge(*K.last("vector"))
                nc.vector.tensor_tensor(sel, gt_, eq, ALU.add).then_inc(*K.step("vector"))
                dve.wait_ge(*K.last("vector"))
                dve.wait_ge(*K.ready("scalar", "f_exp"))
                nc.vector.tensor_tensor(sel, sel, ex, ALU.mult).then_inc(*K.step("vector"))
                dve.wait_ge(*K.last("vector"))
                nc.vector.tensor_reduce(tot, sel, AX.X, ALU.add).then_inc(*K.step("vector"))
                dve.wait_ge(*K.last("vector"))
                nc.vector.reciprocal(need, tot).then_inc(*K.step("vector"))
                dve.wait_ge(*K.last("vector"))
                nc.vector.tensor_tensor(comb, sel, need.unsqueeze(2).broadcast_to([P, NT, FE]), ALU.mult).then_inc(
                    *K.step("vector"))
                dve.wait_ge(*K.last("vector"))
                for e in range(FE):
                    dve.wait_ge(*K.ready("tensor", ("fb", e)))
                    for i in range(NT):
                        nc.vector.scalar_tensor_tensor(out=b.X[:, i, :], in0=K.bank(("fb", e))[:, i * D:(i + 1) * D],
                                                       scalar=comb[:, i, e:e + 1], in1=b.X[:, i, :], op0=ALU.mult,
                                                       op1=ALU.add).then_inc(*K.step("vector", frees=("fb", e)))
                    dve.wait_ge(*K.last("vector"))

            def mom_in(K, b):
                normalised(K, b, 4)
                G = NT * AH
                for i in range(NT):
                    nc.vector.memset(b.AV[:, i, :, AV:VW], 1.0).then_inc(*K.step("vector"))
                lo, pr, sel, rk = b.r2d[0], b.r2d[1], b.r2d[2], b.r2d[3]
                mx, tot, inv = b.r1
                above, same, _ = b.r3
                dve.wait_ge(*K.ready("tensor", "al"))
                lg = K.bank("al")[:, 0:4 * G].rearrange("p (g n) -> p g n", n=4)
                nc.vector.tensor_reduce(mx, lg, AX.X, ALU.max).then_inc(*K.step("vector"))
                dve.wait_ge(*K.last("vector"))
                nc.vector.tensor_tensor(lo, lg, mx.unsqueeze(2).broadcast_to([P, G, 4]), ALU.subtract).then_inc(
                    *K.step("vector", "a_shifted", frees="al"))
                dve.wait_ge(*K.ready("scalar", "a_exp"))
                mine = pr.unsqueeze(3).broadcast_to([P, G, 4, 4])
                other = pr.unsqueeze(2).broadcast_to([P, G, 4, 4])
                nc.vector.tensor_tensor(above, other, mine, ALU.is_gt).then_inc(*K.step("vector"))
                nc.vector.tensor_tensor(same, other, mine, ALU.is_equal).then_inc(*K.step("vector"))
                dve.wait_ge(*K.last("vector"))
                nc.vector.tensor_tensor(same.rearrange("p g a b -> p g (a b)"), same.rearrange("p g a b -> p g (a b)"),
                                        below[:, :, :].rearrange("p a b -> p (a b)").unsqueeze(1).broadcast_to(
                                            [P, G, 16]), ALU.mult).then_inc(*K.step("vector"))
                dve.wait_ge(*K.last("vector"))
                nc.vector.tensor_tensor(above, above, same, ALU.add).then_inc(*K.step("vector"))
                dve.wait_ge(*K.last("vector"))
                nc.vector.tensor_reduce(rk, above, AX.X, ALU.add).then_inc(*K.step("vector"))
                dve.wait_ge(*K.last("vector"))
                nc.vector.scalar_tensor_tensor(out=sel, in0=rk, scalar=1.5, in1=pr, op0=ALU.is_lt,
                                               op1=ALU.mult).then_inc(*K.step("vector"))
                dve.wait_ge(*K.last("vector"))
                nc.vector.tensor_reduce(tot, sel, AX.X, ALU.add).then_inc(*K.step("vector"))
                dve.wait_ge(*K.last("vector"))
                nc.vector.reciprocal(inv, tot).then_inc(*K.step("vector"))
                dve.wait_ge(*K.last("vector"))
                nc.vector.tensor_tensor(sel, sel, inv.unsqueeze(2).broadcast_to([P, G, 4]), ALU.mult).then_inc(
                    *K.step("vector"))
                dve.wait_ge(*K.last("vector"))
                nc.vector.tensor_reduce(tot, sel, AX.X, ALU.add).then_inc(*K.step("vector"))
                dve.wait_ge(*K.last("vector"))
                nc.vector.tensor_scalar(tot, tot, 1.0, None, ALU.add).then_inc(*K.step("vector"))
                dve.wait_ge(*K.last("vector"))
                nc.vector.reciprocal(inv, tot).then_inc(*K.step("vector"))
                dve.wait_ge(*K.last("vector"))
                rw = b.RW[:, :, :, :].rearrange("p i h r -> p (i h) r")
                mk = b.MK[:, :, :, :].rearrange("p i h r -> p (i h) r")
                nc.vector.tensor_tensor(rw[:, :, AS:AR], sel, inv.unsqueeze(2).broadcast_to([P, G, AR - AS]),
                                        ALU.mult).then_inc(*K.step("vector"))
                nc.vector.tensor_scalar(rw[:, :, 0:AS], inv.unsqueeze(2).broadcast_to([P, G, AS]), 1.0 / AS, None,
                                        ALU.mult).then_inc(*K.step("vector"))
                dve.wait_ge(*K.last("vector"))
                nc.vector.tensor_scalar(mk, rw, 0.0, None, ALU.not_equal).then_inc(*K.step("vector", "a_mask"))

            def mom_project(K, b, h):
                m = RH * AD
                dve.wait_ge(*K.ready("tensor", ("aek", h)))
                dve.wait_ge(*K.ready("scalar", ("masks", h)))
                if h >= 2:
                    dve.wait_ge(*K.ready("tensor", ("at", h - 2, AR - 1)))
                nc.vector.tensor_tensor(b.KE[h % 2][0:m, :, :].rearrange("p e t -> p (e t)"), K.bank(("aek", h))[0:m, :],
                                        b.MB[:, :, :].rearrange("p e t -> p (e t)"), ALU.mult).then_inc(
                                            *K.step("vector", ("ke", h), frees=("aek", h)))
                for q in range(AR):
                    dve.wait_ge(*K.ready("tensor", ("as", h, q)))
                    nc.vector.tensor_reduce(b.AMX[:, :, q:q + 1], K.bank(("as", h, q)).rearrange(
                        "p (i t) -> p i t", i=NT), AX.X, ALU.max).then_inc(*K.step("vector", frees=("as", h, q)))
                dve.wait_ge(*K.last("vector"))
                nc.vector.tensor_scalar(b.AMX[:, :, :], b.AMX[:, :, :], -1.0, None, ALU.mult).then_inc(
                    *K.step("vector", ("a_max", h)))

            def mom_rows_out(K, b, h):
                dve.wait_ge(*K.ready("tensor", ("am", h)))
                nc.vector.tensor_copy(b.ANT[:, :], K.bank(("am", h))[0:AR, 0:T]).then_inc(
                    *K.step("vector", f"anm{h}", frees=("am", h)))

            def mom_values(K, b, h):
                if h >= 2:
                    dve.wait_ge(*K.ready("tensor", ("weighed_a", (h - 1) * AR - 1)))
                for k in range(NT):
                    nc.vector.tensor_tensor(b.VM[h % 2][:, k, :, 0:AV],
                                            b.AV[:, k, h, 0:AV].unsqueeze(1).broadcast_to([P, AR - AS, AV]),
                                            b.MK[:, k, h, AS:AR].unsqueeze(2).broadcast_to([P, AR - AS, AV]),
                                            ALU.mult).then_inc(*K.step("vector"))
                    nc.vector.memset(b.VM[h % 2][:, k, :, AV:VW], 1.0).then_inc(*K.step("vector"))
                K.name_last("vector", ("vm", h))

            def mom_heads(K, b):
                dve.wait_ge(*K.ready("scalar", "av1"))
                mom_project(K, b, 0)
                mom_rows_out(K, b, 0)
                for h in range(AH):
                    mom_values(K, b, h)
                    if h + 1 < AH:
                        mom_project(K, b, h + 1)
                    for i in range(NT):
                        dve.wait_ge(*K.ready("tensor", ("aoT", h, i)))
                        ps = K.bank(("aoT", h, i))[:, 0:AR * VW].rearrange("p (r c) -> p r c", r=AR)
                        nc.vector.reciprocal(b.CO[:, :], ps[:, :, AV]).then_inc(*K.step("vector"))
                        dve.wait_ge(*K.last("vector"))
                        nc.vector.tensor_tensor(b.CO[:, :], b.CO[:, :], b.RW[:, i, h, :], ALU.mult).then_inc(
                            *K.step("vector"))
                        dve.wait_ge(*K.last("vector"))
                        nc.vector.tensor_tensor(b.TMP[:, :, :], ps[:, :, 0:AV],
                                                b.CO[:, :].unsqueeze(2).broadcast_to([P, AR, AV]), ALU.mult).then_inc(
                                                    *K.step("vector", frees=("aoT", h, i)))
                        dve.wait_ge(*K.last("vector"))
                        nc.vector.tensor_reduce(b.AO[:, i, h * AV:(h + 1) * AV],
                                                b.TMP[:, :, :].rearrange("p r c -> p c r"), AX.X, ALU.add).then_inc(
                                                    *K.step("vector"))
                    if h + 1 < AH:
                        mom_rows_out(K, b, h + 1)

            def mom_out(K, b):
                for i in range(NT):
                    dve.wait_ge(*K.ready("scalar", f"thag{i}"))
                    nc.vector.scalar_tensor_tensor(out=b.AG[:, i, :], in0=b.AG[:, i, :], scalar=1.0,
                                                   in1=K.bank(f"ag{i}"), op0=ALU.add, op1=ALU.mult).then_inc(
                                                       *K.step("vector", frees=f"ag{i}"))
                dve.wait_ge(*K.last("vector"))
                for i in range(NT):
                    nc.vector.tensor_tensor(b.AO[:, i, :], b.AO[:, i, :], b.AG[:, i, :], ALU.mult).then_inc(
                        *K.step("vector", f"a_gated{i}"))
                add_block(K, b, "aout")

            def feat(K, b):
                mx, neg, tot, inv = b.ts[0:4]
                dve.wait_ge(*K.ready("tensor", "te"))
                nc.vector.tensor_reduce(mx, K.bank("te").rearrange("p (i t) -> p i t", i=NT), AX.X, ALU.max).then_inc(
                    *K.step("vector"))
                dve.wait_ge(*K.last("vector"))
                nc.vector.tensor_scalar(neg, mx, -1.0, None, ALU.mult).then_inc(*K.step("vector", "t_max"))
                normalised(K, b, 5)
                dve.wait_ge(*K.ready("scalar", "t_exp1"))
                nc.vector.reciprocal(inv, tot).then_inc(*K.step("vector"))
                dve.wait_ge(*K.last("vector"))
                for i in range(NT):
                    nc.vector.tensor_scalar(b.TP[:, i, :], b.TP[:, i, :], inv[:, i:i + 1], None, ALU.mult).then_inc(
                        *K.step("vector", f"t_norm{i}"))
                add_block(K, b, "tout")
                nc.vector.tensor_copy(xall[:, K.turn, K.s, :], b.X[:, :, :].rearrange("p i d -> p (i d)")).then_inc(
                    *K.step("vector"))

            dve.wait_ge(w_loaded["small"], 16 * N_SMALL)
            for f in range(2):
                nc.vector.tensor_scalar(ang[:, :, f:4:2], posn[:, :, :], [1.0, 0.01][f], None, ALU.mult).then_inc(
                    s_half, 1)
            dve.wait_ge(s_half, 2)
            nc.vector.tensor_scalar(ang[:, :, 4:8], ang[:, :, 0:4], HALF_PI, None, ALU.add).then_inc(s_ang, 1)
            nc.vector.tensor_scalar(cw[:, :, :], cw[:, :, :], 0.5, None, ALU.mult).then_inc(s_half, 1)
            nc.vector.tensor_scalar(cb[:, :], cb[:, :], 0.5, None, ALU.mult).then_inc(s_half, 1)
            dve.wait_ge(s_exp, 1)
            nc.vector.tensor_scalar(aneg[:, :], aneg[:, :], -1.0, None, ALU.mult).then_inc(s_half, 1)
            dve.wait_ge(s_half, 5)
            dve.wait_ge(s_const, CONSTS)
            dve.wait_ge(s_sin, 1)
            with dve.Fori(0, PAIRS) as turn:
                K2 = keys(turn)
                for stage in (mamba_in, mamba_ssd, mamba_out, rot_in, rot_max, rot_heads, rot_out, low_rank, mom_in,
                              mom_heads, mom_out, feat):
                    for K, b in zip(K2, bufs):
                        stage(K, b)
                turn_end(dve, turn)
                dve.wait_ge(started, turn + 1)

        @block.gpsimd
        def _(pool):
            def power(K, out, base, name):
                pool.wait_ge(*K.last("pool"))
                nc.gpsimd.tensor_tensor(out, base, pw[:, :], ALU.pow).then_inc(*K.step("pool", name))

            def inverse_deviation(K, b, q):
                pool.wait_ge(*K.ready("vector", f"stat{q}1"))
                if K.taken.get("pool"):
                    pool.wait_ge(*K.last("pool"))
                nc.gpsimd.tensor_scalar(b.ve, b.mv[:, :, 1], 1e-5, None, ALU.add).then_inc(*K.step("pool"))
                power(K, b.rstd, b.ve, f"rstd{q}")

            def mamba_in(K, b):
                inverse_deviation(K, b, 1)
                pool.wait_ge(*K.last("pool"))
                nc.gpsimd.tensor_tensor(b.r2, b.rstd, b.rstd, ALU.mult).then_inc(*K.step("pool"))
                pool.wait_ge(*K.last("pool"))
                nc.gpsimd.tensor_tensor(b.r2, b.r2, b.mv[:, :, 1], ALU.mult).then_inc(*K.step("pool"))
                pool.wait_ge(*K.last("pool"))
                nc.gpsimd.tensor_scalar(b.r2, b.r2, 1e-6, None, ALU.add).then_inc(*K.step("pool"))
                power(K, b.rh, b.r2, None)
                pool.wait_ge(*K.last("pool"))
                nc.gpsimd.tensor_tensor(b.rh, b.rh, b.rstd, ALU.mult).then_inc(*K.step("pool", "h_scale"))

            def mamba_ssd(K, b):
                pool.wait_ge(*K.ready("vector", "dA"))
                for i in range(NT):
                    nc.gpsimd.tensor_tensor(b.E[i][:, :, :], le[:, :].unsqueeze(1).broadcast_to([P, MH, P]),
                                            b.dA[:, i, :].unsqueeze(2).broadcast_to([P, MH, P]), ALU.mult).then_inc(
                                                *K.step("pool", f"dA_rows{i}"))
                pool.wait_ge(*K.ready("scalar", "decay"))
                pool.wait_ge(*K.ready("vector", "x_dt0"))
                nc.gpsimd.tensor_tensor(b.XDEC[:, :].rearrange("p (h d) -> p h d", h=MH),
                                        b.XDT[:, 0, :].rearrange("p (h d) -> p h d", h=MH),
                                        b.dcy[:, 0:MH].unsqueeze(2).broadcast_to([P, MH, MP]), ALU.mult).then_inc(
                                            *K.step("pool", "x_decayed"))
                for i in range(NT):
                    pool.wait_ge(*K.ready("scalar", f"xs{i}"))
                    nc.gpsimd.tensor_tensor(b.XT[:, i, :].rearrange("p (h d) -> p h d", h=MH),
                                            b.XT[:, i, :].rearrange("p (h d) -> p h d", h=MH),
                                            dpar[:, :].unsqueeze(2).broadcast_to([P, MH, MP]), ALU.mult).then_inc(
                                                *K.step("pool", f"x_skip{i}"))

            def mamba_out(K, b):
                pool.wait_ge(*K.ready("scalar", "y_square1"))
                nc.gpsimd.tensor_scalar(b.ss, b.ss, 1.0 / DI, 4e-6, ALU.mult, ALU.add).then_inc(*K.step("pool"))
                power(K, b.rs, b.ss, "y_scale")
                pool.wait_ge(*K.ready("scalar", "h_square1"))
                nc.gpsimd.tensor_scalar(b.ss2, b.ss2, 1.0 / D, 1e-6, ALU.mult, ALU.add).then_inc(*K.step("pool"))
                power(K, b.rs2, b.ss2, "h1_scale")
                nc.gpsimd.tensor_tensor(b.X[:, :, :], b.X[:, :, :], b.H1[:, :, :], ALU.add).then_inc(
                    *K.step("pool", "x_h1"))

            def rot_in(K, b):
                pool.wait_ge(*K.ready("tensor", "down"))
                nc.gpsimd.memset(b.V1[:, :, :, :].rearrange("p i h d -> p (i h) d")[:, :, XD:XD + 1], 1.0).then_inc(
                    *K.step("pool"))
                nc.gpsimd.memset(b.V1[:, :, :, :].rearrange("p i h d -> p (i h) d")[:, :, XD + 1:32], 0.0).then_inc(
                    *K.step("pool", "v_pad"))
                inverse_deviation(K, b, 2)
                m = D - 2 * SHIFT
                pool.wait_ge(*K.last("pool"))
                nc.gpsimd.memset(b.QT[m:SHIFT, 2, :], 0.0).then_inc(*K.step("pool"))
                nc.gpsimd.memset(b.KT[m:SHIFT, 2, :], 0.0).then_inc(*K.step("pool"))
                pool.wait_ge(*K.last("pool"))
                nc.gpsimd.memset(b.KT[SHIFT:SHIFT + 1, :, :], 1.0).then_inc(*K.step("pool", "k_pad"))
                pool.wait_ge(*K.ready("scalar", "xkT1"))
                pool.wait_ge(*K.last("pool"))
                nc.gpsimd.tensor_copy(b.KTB[:, :, :], b.KT[0:SHIFT, :, :]).then_inc(*K.step("pool", "k_low"))
                pool.wait_ge(*K.last("pool"))

            def rot_out(K, b):
                pool.wait_ge(*K.ready("vector", "xn21"))
                pool.wait_ge(*K.last("pool"))
                nc.gpsimd.tensor_tensor(b.X[:, :, :], b.X[:, :, :],
                                        bout[:, :].unsqueeze(1).broadcast_to([P, NT, D]), ALU.add).then_inc(
                                            *K.step("pool", "x_bias"))

            def low_rank(K, b):
                inverse_deviation(K, b, 3)
                pool.wait_ge(*K.ready("scalar", "x_square1"))
                power(K, b.rs, b.ss, None)
                pool.wait_ge(*K.last("pool"))
                nc.gpsimd.tensor_scalar(b.rs, b.rs, 1e12, None, ALU.min).then_inc(*K.step("pool", "f_inverse"))

            def mom_in(K, b):
                inverse_deviation(K, b, 4)
                pool.wait_ge(*K.last("pool"))
                for k in range(2):
                    nc.gpsimd.memset(b.KE[k][SHIFT:SHIFT + 1, :, :], 1.0).then_inc(*K.step("pool"))
                pool.wait_ge(*K.last("pool"))

            def mom_heads(K, b):
                for h in range(AH):
                    pool.wait_ge(*K.ready("vector", ("ke", h)))
                    pool.wait_ge(*K.ready("scalar", ("qe", h)))
                    if h >= 1:
                        pool.wait_ge(*K.ready("tensor", ("as", h - 1, AR - 1)))
                    pool.wait_ge(*K.last("pool"))
                    nc.gpsimd.tensor_copy(b.KEB[:, :, :], b.KE[h % 2][0:SHIFT, :, :]).then_inc(*K.step("pool"))
                    nc.gpsimd.tensor_copy(b.QEB[:, :, :, :].rearrange("p a g t -> p (a g t)"),
                                          b.QE[h % 2][0:SHIFT, :, :, :].rearrange("p a g t -> p (a g t)")).then_inc(
                                              *K.step("pool", ("ke_low", h)))
                pool.wait_ge(*K.last("pool"))

            def feat(K, b):
                inverse_deviation(K, b, 5)

            s_c, n = s_pool, 0
            for t, v in ((ident, 0.0), (le, 1.0), (gt, 1.0), (head12, 1.0), (mem3, 1.0), (below, 1.0), (pw, -0.5)):
                nc.gpsimd.memset(t[tuple(slice(None) for _ in t.shape)], v).then_inc(s_c, 1)
                n += 1
            nc.gpsimd.memset(spread[:, :, :], 0.0).then_inc(s_c, 1)
            nc.gpsimd.memset(w_al[:, :, :], 0.0).then_inc(s_fill, 1)
            pool.wait_ge(s_c, n + 1)
            nc.gpsimd.affine_select(out=ident[:, :], in_=ident[:, :], compare_op=ALU.not_equal, fill=1.0, base=0,
                                    pattern=[[-1, P]], channel_multiplier=1).then_inc(s_const, 1)
            nc.gpsimd.affine_select(out=le[:, :], in_=le[:, :], compare_op=ALU.is_ge, fill=0.0, base=0,
                                    pattern=[[1, P]], channel_multiplier=-1).then_inc(s_c, 1)
            nc.gpsimd.affine_select(out=gt[:, :], in_=gt[:, :], compare_op=ALU.is_gt, fill=0.0, base=0,
                                    pattern=[[-1, P]], channel_multiplier=1).then_inc(s_const, 1)
            nc.gpsimd.affine_select(out=below[:, :, :], in_=below[:, :, :], compare_op=ALU.is_gt, fill=0.0, base=0,
                                    pattern=[[1, 4], [-1, 4]], channel_multiplier=0).then_inc(s_const, 1)
            nc.gpsimd.affine_select(out=spread[:, :, :], in_=spread[:, :, :], compare_op=ALU.not_equal, fill=1.0,
                                    base=0, pattern=[[-3, 2 * AH], [-1, RH], [0, AD]],
                                    channel_multiplier=1).then_inc(s_const, 1)
            for t, m, c in ((head12, XD, HT), (mem3, AD, RH)):
                nc.gpsimd.affine_select(out=t[:, :], in_=t[:, :], compare_op=ALU.is_ge, fill=0.0, base=0,
                                        pattern=[[-m, c]], channel_multiplier=1).then_inc(s_c, 1)
            pool.wait_ge(s_c, n + 4)
            for t, m, c in ((head12, XD, HT), (mem3, AD, RH)):
                nc.gpsimd.affine_select(out=t[:, :], in_=t[:, :], compare_op=ALU.is_ge, fill=0.0, base=m - 1,
                                        pattern=[[m, c]], channel_multiplier=-1).then_inc(s_const, 1)
            pool.wait_ge(w_loaded["small"], 16 * N_SMALL)
            pool.wait_ge(s_const, CONSTS)
            with pool.Fori(0, PAIRS) as turn:
                K2 = keys(turn)
                for stage in (mamba_in, mamba_ssd, mamba_out, rot_in, rot_out, low_rank, mom_in, mom_heads, feat):
                    for K, b in zip(K2, bufs):
                        stage(K, b)
                turn_end(pool, turn)
                pool.wait_ge(started, turn + 1)


def grouped_experts(nc, io, out, xall, ident):
    TT = B * NT
    CH = 512
    GS = ME // MG
    SLOTS = 4
    TURNS = ME // SLOTS
    with ExitStack() as ctx:
        def sb(name, shape, dt=F32):
            return ctx.enter_context(nc.sbuf_tensor(name, shape, dt))

        def sem(name):
            return ctx.enter_context(nc.semaphore(name))

        X = xall[:, :, :, :].rearrange("p a b (i d) -> p (a b i) d", d=D)
        XN = sb("g_xn", [P, TT, D])
        XT = sb("g_xT", [P, KD, B * T])
        wr = sb("g_wr", [P, KD, ME])
        rbias = sb("g_rbias", [P, ME])
        wg = sb("g_wg", [P, SLOTS, KD, MI])
        wu = sb("g_wu", [P, SLOTS, KD, MI])
        wd = sb("g_wd", [P, SLOTS, D])
        TH = sb("g_th", [P, 2, CH])
        HH = sb("g_hh", [P, 2, CH])
        bst = sb("g_bst", [P, TT, 6])
        mv = sb("g_mv", [P, TT, 2])
        rstd = sb("g_rstd", [P, TT])
        pw8 = sb("g_pw8", [P, TT])
        sc = sb("g_sc", [P, TT, ME])
        bi = sb("g_bi", [P, TT, ME])
        ta = sb("g_ta", [P, TT, ME])
        tb = sb("g_tb", [P, TT, ME])
        td = sb("g_td", [P, TT, ME])
        comb = sb("g_comb", [P, TT, ME])
        g4 = [sb(f"g_g{n}", [P, TT * MG]) for n in range(6)]
        ga = sb("g_ga", [P, TT, MG, MG])
        gb = sb("g_gb", [P, TT, MG, MG])
        lower = sb("g_lower", [P, MG, MG])
        v8 = sb("g_v8", [P, TT, 8])
        need = sb("g_need", [P, TT])
        tot = sb("g_tot", [P, TT])
        share = sb("g_share", [P, SLOTS, TT])
        psum = ctx.enter_context(nc.psum_tensor("g_psum", [P, 8, 512], F32))

        s_router = sem("g_router_in")
        s_slot = [sem(f"g_slot{j}") for j in range(SLOTS)]
        s_lower = sem("g_lower_made")
        s_stat = sem("g_stat")
        s_rstd = sem("g_rstd_made")
        s_xn = sem("g_xn_made")
        s_turn = sem("g_turned")
        s_xT = sem("g_xT_made")
        s_logit = sem("g_logits")
        s_sig = sem("g_exp")
        s_seq = sem("g_vector_seq")
        s_comb = sem("g_comb_made")
        s_gu = sem("g_gate_up")
        s_th = sem("g_tanh")
        s_half = sem("g_half")
        s_hh = sem("g_hidden")
        s_down = sem("g_down")
        s_acc = sem("g_added")
        s_out = sem("g_out")

        block = ctx.enter_context(nc.Block())


        @block.sync
        def _(sp):
            sp.dma_start(wr[:, :, :], io["L1_ffn_router_w"].rearrange("(k p) n -> p k n", p=P)).then_inc(s_router, 16)
            sp.dma_start(rbias[:, :], io["L1_ffn_router_bias"].partition_broadcast(P)).then_inc(s_router, 16)
            for m in range(MSH):
                j = SLOTS - MSH + m
                c = slice(m * MI, (m + 1) * MI)
                sp.dma_start(wg[:, j, :, :], io["L1_ffn_sw_gate"][:, c].rearrange("(k p) n -> p k n", p=P)).then_inc(
                    s_slot[j], 16)
                sp.dma_start(wu[:, j, :, :], io["L1_ffn_sw_up"][:, c].rearrange("(k p) n -> p k n", p=P)).then_inc(
                    s_slot[j], 16)
                sp.dma_start(wd[:, j, :], io["L1_ffn_sw_down"][c, :]).then_inc(s_slot[j], 16)

            def load(e, j):
                sp.dma_start(wg[:, j, :, :], io["w_gate_tiles"][e]).then_inc(s_slot[j], 16)
                sp.dma_start(wu[:, j, :, :], io["w_up_tiles"][e]).then_inc(s_slot[j], 16)
                sp.dma_start(wd[:, j, :], io["L1_ffn_w_down"][e]).then_inc(s_slot[j], 16)

            for j in range(SLOTS):
                if j >= SLOTS - MSH:
                    sp.wait_ge(s_down, 4 * (MSH + j - SLOTS + 1))
                load(j, j)
            with sp.Fori(1, TURNS) as turn:
                for j in range(SLOTS):
                    sp.wait_ge(s_down, turn * 4 * SLOTS + 4 * (MSH + j - SLOTS + 1))
                    load(turn * SLOTS + j, j)
            sp.wait_ge(s_acc, 4 * (MSH + ME))
            for b in range(B):
                sp.dma_start(out[b].rearrange("(i p) d -> p i d", p=P), X[:, NT * b:NT * (b + 1), :]).then_inc(
                    s_out, 16)
            sp.wait_ge(s_out, 16 * B)

        def program(turn):
            return [(j, turn * 2 * SLOTS + 2 * (MSH + j)) for j in range(SLOTS)]

        SHARED = [(SLOTS - MSH + m, 2 * m) for m in range(MSH)]

        @block.scalar
        def _(act):
            for q in range(TT // 2):
                act.wait_ge(s_turn, q + 1)
                nc.scalar.copy(XT[:, :, 2 * P * q:2 * P * (q + 1)], psum[:, q, :].rearrange("p (k t) -> p k t", k=KD)
                               ).then_inc(s_xT, 1)
            act.wait_ge(s_logit, 1)
            nc.scalar.activation(sc[:, :, :].rearrange("p t e -> p (t e)"), psum[:, 4, 0:TT * ME], ACT.Exp,
                                 scale=-1.0).then_inc(s_sig, 1)

            def tanh(n, c, first=False):
                act.wait_ge(s_gu, n + 1)
                if not first:
                    act.wait_ge(s_hh, n - 1)
                nc.scalar.activation(TH[:, c, :], psum[:, 2 * c, :], ACT.Tanh, scale=0.5).then_inc(s_th, 1)

            for j, n in SHARED:
                for c in range(2):
                    tanh(n + c, c, n == 0)
            with act.Fori(0, TURNS) as turn:
                for j, n in program(turn):
                    for c in range(2):
                        tanh(n + c, c)

        @block.tensor
        def _(pe):
            for q in range(TT // 2):
                pe.wait_ge(s_xn, 2 * q + 2)
                for k in range(KD):
                    for i in range(2):
                        last = nc.tensor.transpose(psum[:, q, (2 * k + i) * P:(2 * k + i + 1) * P],
                                                   XN[:, 2 * q + i, k * P:(k + 1) * P], ident[:, :])
                last.then_inc(s_turn, 1)
            pe.wait_ge(s_router, 32)
            pe.wait_ge(s_xT, TT // 2)
            for t in range(TT):
                for k in range(KD):
                    last = nc.tensor.matmul(psum[:, 4, t * ME:(t + 1) * ME], XT[:, k, t * P:(t + 1) * P], wr[:, k, :],
                                            start=(k == 0), stop=(k == KD - 1))
            last.then_inc(s_logit, 1)
            pe.wait_ge(s_sig, 1)

            def gate_up(j, n, c, first=False):
                if not first:
                    pe.wait_ge(s_hh, n - 1)
                for bank, w in ((2 * c, wg), (2 * c + 1, wu)):
                    for k in range(KD):
                        last = nc.tensor.matmul(psum[:, bank, :], w[:, j, k, :], XT[:, k, c * CH:(c + 1) * CH],
                                                start=(k == 0), stop=(k == KD - 1))
                last.then_inc(s_gu, 1)

            def down(j, n, c, first=False):
                pe.wait_ge(s_hh, n + 1)
                for q in range(2):
                    if not first:
                        pe.wait_ge(s_acc, 2 * n - 3 + q)
                    for i in range(2):
                        t = 2 * q + i
                        last = nc.tensor.matmul(psum[:, 4 + 2 * c + q, i * D:(i + 1) * D],
                                                HH[:, c, t * P:(t + 1) * P], wd[:, j, :], start=True, stop=True)
                    last.then_inc(s_down, 1)

            for j, n in SHARED:
                pe.wait_ge(s_slot[j], 48)
                gate_up(j, n, 0, n == 0)
                if n > 0:
                    down(j - 1, n - 1, 1, n - 1 == 1)
                gate_up(j, n + 1, 1, n == 0)
                down(j, n, 0, n == 0)
            with pe.Fori(0, TURNS) as turn:
                for j, n in program(turn):
                    pe.wait_ge(s_slot[j], turn * 48 + (96 if j >= SLOTS - MSH else 48))
                    gate_up(j, n, 0)
                    down((j - 1) % SLOTS, n - 1, 1)
                    gate_up(j, n + 1, 1)
                    down(j, n, 0)
            down(SLOTS - 1, 2 * (MSH + ME) - 1, 1)

        @block.gpsimd
        def _(pool):
            nc.gpsimd.memset(lower[:, :, :], 1.0).then_inc(s_lower, 1)
            nc.gpsimd.memset(pw8[:, :], -0.5).then_inc(s_lower, 1)
            pool.wait_ge(s_lower, 2)
            nc.gpsimd.affine_select(out=lower[:, :, :], in_=lower[:, :, :], compare_op=ALU.is_gt, fill=0.0, base=0,
                                    pattern=[[1, MG], [-1, MG]], channel_multiplier=0).then_inc(s_lower, 1)
            pool.wait_ge(s_stat, TT)
            nc.gpsimd.tensor_scalar(rstd[:, :], mv[:, :, 1], 1e-5, None, ALU.add).then_inc(s_rstd, 1)
            pool.wait_ge(s_rstd, 1)
            nc.gpsimd.tensor_tensor(rstd[:, :], rstd[:, :], pw8[:, :], ALU.pow).then_inc(s_rstd, 1)

        @block.vector
        def _(dve):
            seq = [0]

            def chain(instruction):
                seq[0] += 1
                instruction.then_inc(s_seq, 1)
                dve.wait_ge(s_seq, seq[0])

            for t in range(TT):
                nc.vector.bn_stats(bst[:, t, :], X[:, t, :]).then_inc(s_seq, 1)
                seq[0] += 1
            dve.wait_ge(s_seq, seq[0])
            for t in range(TT):
                nc.vector.bn_aggr(mv[:, t, :], bst[:, t, :]).then_inc(s_stat, 1)
            dve.wait_ge(s_stat, TT)
            dve.wait_ge(s_rstd, 2)
            for t in range(TT):
                nc.vector.tensor_scalar(XN[:, t, :], X[:, t, :], mv[:, t, 0:1], rstd[:, t:t + 1], ALU.subtract,
                                        ALU.mult).then_inc(s_xn, 1)
            dve.wait_ge(s_sig, 1)
            chain(nc.vector.tensor_scalar(sc[:, :, :], sc[:, :, :], 1.0, None, ALU.add))
            chain(nc.vector.reciprocal(sc[:, :, :], sc[:, :, :]))
            dve.wait_ge(s_router, 32)
            chain(nc.vector.tensor_tensor(bi[:, :, :], sc[:, :, :], rbias[:, :].unsqueeze(1).broadcast_to([P, TT, ME]),
                                          ALU.add))
            q = bi[:, :, :].rearrange("p t (g n) -> p (t g) n", n=GS)
            hi1, lo1, hi2, lo2, top, nxt = g4
            nc.vector.tensor_tensor(hi1[:, :], q[:, :, 0], q[:, :, 1], ALU.max)
            nc.vector.tensor_tensor(lo1[:, :], q[:, :, 0], q[:, :, 1], ALU.min)
            nc.vector.tensor_tensor(hi2[:, :], q[:, :, 2], q[:, :, 3], ALU.max)
            chain(nc.vector.tensor_tensor(lo2[:, :], q[:, :, 2], q[:, :, 3], ALU.min))
            nc.vector.tensor_tensor(top[:, :], hi1[:, :], hi2[:, :], ALU.max)
            nc.vector.tensor_tensor(nxt[:, :], hi1[:, :], hi2[:, :], ALU.min)
            chain(nc.vector.tensor_tensor(lo1[:, :], lo1[:, :], lo2[:, :], ALU.max))
            chain(nc.vector.tensor_tensor(nxt[:, :], nxt[:, :], lo1[:, :], ALU.max))
            chain(nc.vector.tensor_tensor(top[:, :], top[:, :], nxt[:, :], ALU.add))
            dve.wait_ge(s_lower, 3)
            score = top[:, :].rearrange("p (t g) -> p t g", g=MG)
            mine = score.unsqueeze(3).broadcast_to([P, TT, MG, MG])
            other = score.unsqueeze(2).broadcast_to([P, TT, MG, MG])
            nc.vector.tensor_tensor(ga[:, :, :, :], other, mine, ALU.is_gt)
            chain(nc.vector.tensor_tensor(gb[:, :, :, :], other, mine, ALU.is_equal))
            chain(nc.vector.tensor_tensor(gb[:, :, :, :].rearrange("p t a b -> p t (a b)"),
                                          gb[:, :, :, :].rearrange("p t a b -> p t (a b)"),
                                          lower[:, :, :].rearrange("p a b -> p (a b)").unsqueeze(1).broadcast_to(
                                              [P, TT, MG * MG]), ALU.mult))
            chain(nc.vector.tensor_tensor(ga[:, :, :, :], ga[:, :, :, :], gb[:, :, :, :], ALU.add))
            chain(nc.vector.tensor_reduce(hi1[:, :].rearrange("p (t g) -> p t g", g=MG), ga[:, :, :, :], AX.X, ALU.add))
            chain(nc.vector.tensor_scalar(hi1[:, :], hi1[:, :], MTG - 0.5, None, ALU.is_lt))
            chain(nc.vector.tensor_tensor(q, q, hi1[:, :].unsqueeze(2).broadcast_to([P, TT * MG, GS]), ALU.mult))
            for t in range(TT):
                nc.vector.max(v8[:, t, :], bi[:, t, :]).then_inc(s_seq, 1)
                seq[0] += 1
            dve.wait_ge(s_seq, seq[0])
            eighth = v8[:, :, 7:8].broadcast_to([P, TT, ME])
            nc.vector.tensor_tensor(ta[:, :, :], bi[:, :, :], eighth, ALU.is_gt)
            chain(nc.vector.tensor_tensor(tb[:, :, :], bi[:, :, :], eighth, ALU.is_equal))
            nc.vector.tensor_reduce(need[:, :], ta[:, :, :], AX.X, ALU.add).then_inc(s_seq, 1)
            seq[0] += 1
            for t in range(TT):
                nc.vector.tensor_tensor_scan(td[:, t, :], tb[:, t, :], tb[:, t, :], 0.0, ALU.add,
                                             ALU.max).then_inc(s_seq, 1)
                seq[0] += 1
            dve.wait_ge(s_seq, seq[0])
            chain(nc.vector.tensor_tensor(td[:, :, :], td[:, :, :], need[:, :].unsqueeze(2).broadcast_to([P, TT, ME]),
                                          ALU.add))
            chain(nc.vector.scalar_tensor_tensor(out=tb[:, :, :], in0=td[:, :, :], scalar=MTK + 0.5, in1=tb[:, :, :],
                                                 op0=ALU.is_lt, op1=ALU.mult))
            chain(nc.vector.tensor_tensor(ta[:, :, :], ta[:, :, :], tb[:, :, :], ALU.add))
            chain(nc.vector.tensor_tensor(ta[:, :, :], ta[:, :, :], sc[:, :, :], ALU.mult))
            chain(nc.vector.tensor_reduce(tot[:, :], ta[:, :, :], AX.X, ALU.add))
            chain(nc.vector.reciprocal(tot[:, :], tot[:, :]))
            chain(nc.vector.tensor_scalar(tot[:, :], tot[:, :], 0.5 * ROUTED_SCALE, None, ALU.mult))
            chain(nc.vector.tensor_tensor(comb[:, :, :], ta[:, :, :], tot[:, :].unsqueeze(2).broadcast_to([P, TT, ME]),
                                          ALU.mult))

            def hidden(n, c, first=False):
                dve.wait_ge(s_th, n + 1)
                if not first:
                    dve.wait_ge(s_down, 2 * n - 2)
                nc.vector.scalar_tensor_tensor(out=HH[:, c, :], in0=TH[:, c, :], scalar=1.0, in1=psum[:, 2 * c, :],
                                               op0=ALU.add, op1=ALU.mult).then_inc(s_half, 1)
                dve.wait_ge(s_half, n + 1)
                nc.vector.tensor_tensor(HH[:, c, :], HH[:, c, :], psum[:, 2 * c + 1, :], ALU.mult).then_inc(s_hh, 1)

            def add(n, c, scale):
                for q in range(2):
                    dve.wait_ge(s_down, 2 * n + 1 + q)
                    for i in range(2):
                        t = 4 * c + 2 * q + i
                        last = nc.vector.scalar_tensor_tensor(
                            out=X[:, t, :], in0=psum[:, 4 + 2 * c + q, i * D:(i + 1) * D],
                            scalar=0.5 if scale is None else share[:, scale, t:t + 1], in1=X[:, t, :], op0=ALU.mult,
                            op1=ALU.add)
                    last.then_inc(s_acc, 1)

            def shares(turn, j):
                nc.vector.tensor_copy(share[:, j, :], comb[:, :, turn * SLOTS + j])

            for j, n in SHARED:
                hidden(n, 0, n == 0)
                if n > 0:
                    add(n - 1, 1, None)
                hidden(n + 1, 1, n == 0)
                add(n, 0, None)
            nc.vector.memset(share[:, SLOTS - 1, :], 0.5)
            with dve.Fori(0, TURNS) as turn:
                for j, n in program(turn):
                    hidden(n, 0)
                    add(n - 1, 1, (j - 1) % SLOTS)
                    shares(turn, j)
                    hidden(n + 1, 1)
                    add(n, 0, j)
            add(2 * (MSH + ME) - 1, 1, SLOTS - 1)


def views(a):
    io = dict(a)
    io["x"] = a["x"].rearrange("(t s) (i p) d -> s t p i d", s=STREAMS, p=P)
    io["ctx"] = a["ctx_t"].rearrange("(t s) c n -> s t c n", s=STREAMS)
    io["pos"] = a["fside_BxSx2_0"].rearrange("b (i p) c -> p (b i) c", p=P)
    for n, m in (("wq_exp", "L1_attn_Wq_exp"), ("wk_exp", "L1_attn_Wk_exp")):
        io[n] = a[m].rearrange("(k a) d e -> k (a d) e", k=KD)
    for n, m in (("w_gate_tiles", "L1_ffn_w_gate"), ("w_up_tiles", "L1_ffn_w_up")):
        io[n] = a[m].rearrange("e (k p) n -> e p k n", p=P)
    return io


def declare(nc, shapes):
    a = {n: nc.dram_tensor(f"in_{n}_dram", s, F32, kind="ExternalInput").ap() for n, s in shapes.items()}
    return views(a), nc.dram_tensor("out_0_dram", (B, T, D), F32, kind="ExternalOutput").ap()


def program(nc, trial, shapes):
    plan = Plan()
    build(trial, plan, *declare(trial, shapes))
    plan.final = True
    build(nc, plan, *declare(nc, shapes))


def kernel(**inputs):
    import numpy as np
    import concourse.bacc as bacc
    from concourse.bass_utils import run_bass_kernel_spmd

    def columns(v, *rest):
        n = v.shape[0] // P
        return np.ascontiguousarray(np.moveaxis(v.reshape(n, P, *rest), 0, 1))

    a = {n: np.ascontiguousarray(v) for n, v in inputs.items()}
    a["ctx_t"] = np.ascontiguousarray(np.transpose(a.pop("ctx_1024"), (0, 2, 1)))
    a["norm1"] = columns(a.pop("L0_attn_norm1_w"))
    a["norm2"] = columns(a.pop("L0_attn_norm2_w"))
    a["mixn"] = columns(a.pop("L0_attn_mixer_norm_w"))
    a["conv_w"] = columns(a.pop("L0_attn_conv_w"), 4)
    a["conv_b"] = columns(a.pop("L0_attn_conv_b"))
    a["wq_t"] = np.ascontiguousarray(a.pop("L1_xattn_Wq").T)
    a["wk_t"] = np.ascontiguousarray(a.pop("L1_xattn_Wk").T)
    a["bq"] = a.pop("L1_xattn_bq").reshape(P, 1)
    a["bk"] = a.pop("L1_xattn_bk").reshape(P, 1)
    nc, trial = (bacc.Bacc("TRN2", target_bir_lowering=False, num_devices=1) for _ in range(2))
    program(nc, trial, {n: v.shape for n, v in a.items()})
    r = run_bass_kernel_spmd(nc, [{f"in_{n}_dram": v for n, v in a.items()}], core_ids=[0])
    return r.results[0]["out_0_dram"]
```

```python
from contextlib import ExitStack

import concourse.bass as bass
from concourse import mybir

F32 = mybir.dt.float32
BF16 = mybir.dt.bfloat16
ALU = mybir.AluOpType
ACT = mybir.ActivationFunctionType
AX = mybir.AxisListType

P = 128
B, T, D = 4, 256, 256
NT = T // P
KD = D // P
CD = 128
STREAMS = 2
PAIRS = B // STREAMS
HALF_PI = 1.5707963267948966

MH, MP = 8, 64
DI = MH * MP
KI = DI // P
NS = 128
NCH = (DI + 2 * NS) // P
INTER = 704
KG = -(-INTER // P)
XH, XD = 32, 8
NPAIR = XH // 2
HT = 12
XT3 = -(-XH // HT)
SHIFT = 96
QSLOTS = 4
FE = 8
AH, AD, AR, AS = 8, 32, 6, 2
AV = 64
VW = AV + 1
RH = 3
ME, MG, MTK, MTG = 32, 8, 8, 4
MI = 128
MSH = 2
ROUTED_SCALE = 2.5




class Plan:

    def __init__(self):
        self.number, self.count, self.freed, self.bank, self.final = {}, {}, {}, {}, False


class Keys:

    def __init__(self, s, turn, plan, did, psum):
        self.s, self.turn, self.plan, self.did, self.psum = s, turn, plan, did, psum[s]
        self.taken, self.holder, self.latest = {}, {}, 3

    def take(self, name, banks=(0, 1, 2, 3)):
        after = [n for n in banks if n > self.latest] if self.latest in banks else list(banks)
        b = after[0] if after else banks[0]
        if len(banks) > 1:
            self.latest = b
        before = self.holder.get(b)
        self.holder[b] = name
        self.plan.bank[name] = b
        if before is None:
            return self.psum[:, b, :], None
        return self.psum[:, b, :], self.ready(*self.plan.freed[before]) if self.plan.final else None

    def bank(self, name):
        return self.psum[:, self.plan.bank.get(name, 0), :]

    def step(self, engine, name=None, frees=None):
        n = self.taken[engine] = self.taken.get(engine, 0) + 1
        if name is not None:
            assert self.plan.number.setdefault((engine, name), n) == n, (engine, name)
        if frees is not None:
            self.plan.number[engine, "frees", frees] = n
            self.plan.freed[frees] = (engine, "frees", frees)
        if not self.plan.final:
            self.plan.count[engine] = max(self.plan.count.get(engine, 0), n)
        return self.did[engine][self.s], 1

    def name_last(self, engine, name):
        self.plan.number[engine, name] = self.taken[engine]

    def last(self, engine):
        return self.did[engine][self.s], self.taken[engine]

    def ready(self, engine, *name):
        if not self.plan.final:
            return self.did[engine][self.s], 1
        return self.did[engine][self.s], self.plan.number[(engine, *name)]


def build(nc, plan, io, out):
    with ExitStack() as ctx:
        xall = ctx.enter_context(nc.sbuf_tensor("xall", [P, PAIRS, STREAMS, NT * D], F32))
        ident = ctx.enter_context(nc.sbuf_tensor("ident", [P, P], F32))
        five_blocks(nc, plan, io, xall, ident)
        grouped_experts(nc, io, out, xall, ident)


def five_blocks(nc, plan, io, xall, ident):
    with ExitStack() as ctx:
        def sb(name, shape, dt=F32):
            return ctx.enter_context(nc.sbuf_tensor(name, shape, dt))

        def sem(name):
            return ctx.enter_context(nc.semaphore(name))

        w_in = sb("w_in", [P, KD, DI + NCH * P + MH])
        w_mo = sb("w_mo", [P, KI, D])
        w_gate = sb("w_gate", [P, KD, INTER])
        w_up = sb("w_up", [P, KD, INTER])
        w_down = sb("w_down", [P, KG, D])
        w_xq = sb("w_xq", [P, KD, D])
        w_xkv = sb("w_xkv", [P, 2 * D])
        w_xo = sb("w_xo", [P, KD, D])
        w_fr = sb("w_fr", [P, KD, FE])
        w_fa = sb("w_fa", [P, FE, KD, P])
        w_fb = sb("w_fb", [P, FE, D])
        w_aq = sb("w_aq", [P, KD, AH * AD])
        w_ak = sb("w_ak", [P, KD, AH * AD])
        w_av = sb("w_av", [P, KD, AH * AV])
        w_ag = sb("w_ag", [P, KD, AH * AV])
        w_aeq = sb("w_aeq", [P, KD, AR * AD])
        w_aek = sb("w_aek", [P, KD, AR * AD])
        w_al = sb("w_al", [P, 4, AR - AS])
        w_ao = sb("w_ao", [P, AH * AV // P, D])
        w_tq = sb("w_tq", [P, P])
        w_tk = sb("w_tk", [P, P])
        norm1 = sb("norm1", [P, KD])
        norm2 = sb("norm2", [P, KD])
        mixn = sb("mixn", [P, KI])
        cw = sb("cw", [P, NCH, 4])
        cb = sb("cb", [P, NCH])
        dtb = sb("dtb", [P, MH])
        aneg = sb("aneg", [P, MH])
        dpar = sb("dpar", [P, MH])
        bout = sb("bout", [P, D])
        bq = sb("bq", [P, 1])
        bk = sb("bk", [P, 1])
        le = sb("le", [P, P])
        gt = sb("gt", [P, P])
        head12 = sb("head12", [SHIFT, HT])
        mem3 = sb("mem3", [SHIFT, RH])
        below = sb("below", [P, 4, 4])
        spread = sb("spread", [AH * AR, AH * 2, RH * AD], BF16)
        sincos = sb("sincos", [P, PAIRS, STREAMS, NT * 8])
        pw = sb("pw", [P, 2])

        psum = [ctx.enter_context(nc.psum_tensor(f"psum{s}", [P, 4, 512], F32)) for s in range(STREAMS)]
        WORDS = 12840
        per = []
        for s in range(STREAMS):
            a = sb(f"arena{s}", [P, WORDS])
            d = {}
            for n, shape in dict(X=[P, NT, D], XN=[P, NT, D], H=[P, NT, D], AT=[P, KD, T], CT=[P, T],
                                 small=[P, 256]).items():
                d[n] = sb(f"{n}{s}", shape)
            per.append((a, d))

        did = {e: [sem(f"{e}_did{s}") for s in range(STREAMS)] for e in ("tensor", "vector", "scalar", "pool")}
        loaded = [sem(f"loaded{s}") for s in range(STREAMS)]
        arrived = sem("turn_ended")
        started = sem("turn_started")
        rowed = [sem(f"rowed{s}") for s in range(STREAMS)]
        slot_rows = [[sem(f"slot_rows{s}{k}") for k in range(QSLOTS)] for s in range(STREAMS)]
        w_loaded = {n: sem(f"w_{n}") for n in ("small", "in", "mamba", "rot", "fexp", "mom", "feat")}
        x_loaded = sem("x_loaded")
        s_ident = sem("ident_made")
        s_const = sem("constants")
        s_fill = sem("filled_consts")
        s_pool = sem("pool_consts")
        s_ang = sem("angles")
        s_sin = sem("sines")
        s_half = sem("halved")
        s_exp = sem("negated")

        def view(s, at, shape, dt=F32):
            n = 1
            for m in shape[1:]:
                n *= m
            words = n if dt == F32 else n // 2
            assert at + words <= WORDS, (at, shape)
            v = per[s][0][0:shape[0], at:at + words]
            if dt != F32:
                v = v.bitcast(dt)
            if len(shape) == 3:
                v = v.rearrange("p (a b) -> p a b", b=shape[2])
            if len(shape) == 4:
                v = v.rearrange("p (a b c) -> p a b c", b=shape[2], c=shape[3])
            if len(shape) == 5:
                v = v.rearrange("p (a b c d) -> p a b c d", b=shape[2], c=shape[3], d=shape[4])
            return v

        class Bufs:
            pass

        bufs = []
        for s in range(STREAMS):
            b = Bufs()
            d = per[s][1]
            b.X, b.XN, b.H, b.AT, b.CT = d["X"], d["XN"], d["H"], d["AT"], d["CT"]
            sm = d["small"]
            b.bst = sm[:, 0:12].rearrange("p (i c) -> p i c", i=NT)
            b.mv = sm[:, 12:16].rearrange("p (i c) -> p i c", i=NT)
            b.ve, b.rstd, b.r2, b.rh = sm[:, 16:18], sm[:, 18:20], sm[:, 20:22], sm[:, 22:24]
            b.ss, b.rs, b.ss2, b.rs2 = sm[:, 24:26], sm[:, 26:28], sm[:, 28:30], sm[:, 30:32]
            b.raw, b.nab, b.u, b.z, b.z2, b.ser, b.dt, b.dA = (
                sm[:, 32 + 16 * k:48 + 16 * k].rearrange("p (i h) -> p i h", i=NT) for k in range(8))
            b.dcy = sm[:, 160:176]
            b.sc = sm[:, 176:192].rearrange("p (i c) -> p i c", i=NT)
            b.XBC = view(s, 0, [P, NCH, T])
            b.TH = view(s, 1536, [P, NCH, T])
            b.G = view(s, 3072, [P, NT, DI])
            b.E = [view(s, 4096 + 1024 * i, [P, MH, P]) for i in range(NT)]
            b.CB = view(s, 6144, [P, NT, P])
            b.XT = view(s, 6400, [P, NT, DI])
            b.XDT = view(s, 7424, [P, NT, DI])
            b.XDEC = view(s, 8448, [P, DI])
            b.ST = view(s, 8960, [P, DI])
            b.BT = view(s, 9472, [P, NS])
            b.H1 = view(s, 9600, [P, NT, D])
            b.SQ = view(s, 10112, [P, DI])
            b.YO = view(s, 10624, [P, DI])
            b.YT = view(s, 1536, [P, KI, T])
            b.MTH = view(s, 2560, [P, 2, T])
            b.MA = view(s, 0, [P, KG, T])
            b.QC = view(s, 0, [P, NT, D])
            b.QS = view(s, 512, [P, NT, D])
            b.KR = view(s, 1024, [P, NT, D])
            b.QR = view(s, 1536, [P, NT, D])
            b.V1 = view(s, 2048, [P, NT, XH, 32])
            b.KT = view(s, 4096, [SHIFT + 1, XT3, T])
            b.QT = view(s, 4864, [SHIFT, XT3, T])
            b.KTB = view(s, 5632, [SHIFT, XT3, T], BF16)
            b.QMB = [view(s, 6016 + 256 * k, [SHIFT, 2, T], BF16) for k in range(2)]
            b.MX = view(s, 6528, [P, NT, XH])
            b.NMT = view(s, 6592, [XH, T])
            b.QM = [view(s, 6848 + 512 * k, [SHIFT + 1, 2, T]) for k in range(QSLOTS)]
            b.PT = [view(s, 8896 + 1024 * k, [P, NT, 2, T]) for k in range(3)]
            b.OT = [view(s, 1024 + 512 * k, [P, 2, T]) for k in range(2)]
            b.RD = view(s, 11968, [P, 4, 4])
            b.O = view(s, 0, [P, NT, D])
            b.FH = [view(s, 512 * k, [P, 2, T]) for k in range(2)]
            b.SQF = view(s, 1024, [P, D])
            b.f = [view(s, 1280 + 16 * k, [P, NT, FE]) for k in range(10)]
            b.fs = [view(s, 1600 + 2 * k, [P, NT]) for k in range(8)]
            b.AQ = view(s, 0, [P, KD, T])
            b.AK = view(s, 512, [P, KD, T])
            b.AV = view(s, 1024, [P, NT, AH, VW])
            b.r3 = [view(s, 2064 + 256 * k, [P, NT * AH, 4, 4]) for k in range(3)]
            b.r2d = [view(s, 2832 + 64 * k, [P, NT * AH, 4]) for k in range(5)]
            b.r1 = [view(s, 3152 + 16 * k, [P, NT * AH]) for k in range(3)]
            b.RW = view(s, 3200, [P, NT, AH, AR])
            b.MK = view(s, 3296, [P, NT, AH, AR])
            b.MKT = view(s, 3392, [AH * AR, T], BF16)
            b.AO = view(s, 3520, [P, NT, AH * AV])
            b.QE = [view(s, 4544 + 1536 * k, [SHIFT + 1, 2, RH, T]) for k in range(2)]
            b.KE = [view(s, 7616 + 512 * k, [SHIFT + 1, 2, T]) for k in range(2)]
            b.QEB = view(s, 8640, [SHIFT, 2, RH, T], BF16)
            b.KEB = view(s, 9408, [SHIFT, 2, T], BF16)
            b.VM = [view(s, 9664 + 520 * k, [P, NT, 4, VW]) for k in range(2)]
            b.APT = [b.XN, view(s, 10704, [P, NT, T])]
            b.AOT = view(s, 11216, [VW, AR, T])
            b.MB = b.H[0:SHIFT, :, :]
            b.ANT = view(s, 2064, [AR, T])
            b.AMX = view(s, 2320, [P, NT, AR])
            b.CO = view(s, 2332, [P, AR])
            b.TMP = view(s, 2338, [P, AR, AV])
            b.AG = view(s, 4544, [P, NT, AH * AV])
            b.AYT = view(s, 5568, [P, AH * AV // P, T])
            b.TQ = view(s, 0, [P, T])
            b.TK = view(s, 256, [P, T])
            b.TP = view(s, 512, [P, NT, T])
            b.TPT = view(s, 1024, [P, NT, T])
            b.ts = [view(s, 1536 + 2 * k, [P, NT]) for k in range(4)]
            bufs.append(b)
        ang = view(0, 0, [P, B * NT, 8])
        posn = view(0, 64, [P, B * NT, 2])

        block = ctx.enter_context(nc.Block())

        CONSTS = 5
        N_SMALL, N_IN, N_MAMBA, N_ROT, N_FEXP, N_MOM, N_FEAT = 10, 1, 5, 3, 3, 13, 4

        def keys(turn):
            return [Keys(s, turn, plan, did, psum) for s in range(STREAMS)]

        PARTS = dict(mamba_in=5, mamba_ssd=4, mamba_out=6, rot_in=4, rot_max=NPAIR + 1, rot_heads=NPAIR + 2,
                     rot_out=2, low_rank=3 + FE // 2, mom_in=4, mom_out=3, feat=5)

        def parts(s, *stages):
            return [(s, stage, n) for stage in stages for n in range(PARTS[stage])]

        def in_turns(one, other, lag=0):
            other = [None] * lag + other
            return [x for n in range(max(len(one), len(other))) for x in one[n:n + 1] + other[n:n + 1] if x]

        front = ("mamba_in", "mamba_ssd", "mamba_out", "rot_in")
        middle = ("rot_out", "low_rank", "mom_in")
        mid = [parts(s, *middle) for s in range(STREAMS)]
        BEFORE_MOM = (in_turns(parts(0, *front, "rot_max"), parts(1, *front), 1)
                      + in_turns(parts(1, "rot_max"), parts(0, "rot_heads"), 1) + parts(1, "rot_heads")
                      + in_turns(mid[0][:-1], mid[1][:-1], 1) + [mid[0][-1], mid[1][-1]])
        after = [in_turns(parts(s, "mom_out"), parts(s, "feat")[:3]) + parts(s, "feat")[3:] for s in range(STREAMS)]
        AFTER_MOM = in_turns(after[0][:-2], after[1][:-2]) + after[0][-2:] + after[1][-2:]

        def run(order, K2, **stages):
            begun = {}
            for s, name, n in order:
                if name in stages:
                    if n == 0:
                        begun[s, name] = stages[name](K2[s], bufs[s])
                    rest = next(begun[s, name], "end")
                    assert n + 1 < PARTS[name] or rest == "end", (name, n)

        UNITS = STREAMS * AH

        def units(K2, n):
            return K2[n % STREAMS], bufs[n % STREAMS], n // STREAMS

        def turn_end(engine, turn):
            for e, n in plan.count.items():
                for s in range(STREAMS):
                    engine.wait_ge(did[e][s], n)
            engine.nop().then_inc(arrived, 1)

        @block.sync
        def _(sp):
            def load_x(t):
                for s in range(STREAMS):
                    sp.dma_start(xall[:, t, s, :].rearrange("p (i d) -> p i d", i=NT), io["x"][s][t]).then_inc(
                        x_loaded, 16)

            load_x(0)
            sp.dma_start(posn[:, :, :], io["pos"]).then_inc(w_loaded["small"], 16)
            sp.dma_start(aneg[:, :], io["L0_attn_A_log"].partition_broadcast(P)).then_inc(w_loaded["small"], 16)
            sp.dma_start(dtb[:, :], io["L0_attn_dt_bias"].partition_broadcast(P)).then_inc(w_loaded["small"], 16)
            sp.dma_start(dpar[:, :], io["L0_attn_D_param"].partition_broadcast(P)).then_inc(w_loaded["small"], 16)
            sp.dma_start(bout[:, :], io["L0_xattn_bout"].partition_broadcast(P)).then_inc(w_loaded["small"], 16)
            for t in range(1, PAIRS):
                load_x(t)

            def load(K, b):
                sp.dma_start(b.CT[:, :], io["ctx"][K.s][K.turn]).then_inc(loaded[K.s], 16)

            def rot_rows(K, b):
                sp.wait_ge(*K.ready("vector", "xnm"))
                for p in range(NPAIR):
                    if p >= QSLOTS:
                        sp.wait_ge(*K.ready("tensor", ("xt", p - QSLOTS, NT - 1)))
                    sp.dma_start(b.QM[p % QSLOTS][SHIFT:SHIFT + 1, :, :], b.NMT[2 * p:2 * p + 2, :]).then_inc(
                        slot_rows[K.s][p % QSLOTS], 16)

            def mom_rows(K2):
                for n in range(UNITS):
                    K, b, h = units(K2, n)
                    sp.wait_ge(*K.ready("vector", f"anm{h}"))
                    sp.dma_start(b.QE[h % 2][SHIFT:SHIFT + 1, :, :, :].rearrange("p a g t -> p (a g) t"),
                                 b.ANT[:, :]).then_inc(rowed[K.s], 16)

            sp.dma_start(w_mo[:, :, :], io["L0_attn_out_proj_w"].rearrange("(k p) n -> p k n", p=P)).then_inc(
                w_loaded["mamba"], 16)
            sp.dma_start(w_gate[:, :, :], io["L0_attn_gate_w"].rearrange("(k p) n -> p k n", p=P)).then_inc(
                w_loaded["mamba"], 16)
            sp.dma_start(w_up[:, :, :], io["L0_attn_up_w"].rearrange("(k p) n -> p k n", p=P)).then_inc(
                w_loaded["mamba"], 16)
            full_rows = INTER // P * P
            sp.dma_start(w_down[:, 0:KG - 1, :], io["L0_attn_down_w"][0:full_rows, :].rearrange(
                "(k p) n -> p k n", p=P)).then_inc(w_loaded["mamba"], 16)
            sp.dma_start(w_down[0:INTER - full_rows, KG - 1, :], io["L0_attn_down_w"][full_rows:INTER, :]).then_inc(
                w_loaded["mamba"], 16)
            for n, t, src in (
                ("rot", w_xq[:, :, :], io["L0_xattn_Wq"].rearrange("(k p) n -> p k n", p=P)),
                ("rot", w_xkv[:, :], io["L0_xattn_Wkv"]),
                ("rot", w_xo[:, :, :], io["L0_xattn_Wout"].rearrange("(k p) n -> p k n", p=P)),
                ("fexp", w_fr[:, :, :], io["L0_ffn_router_w"].rearrange("(k p) n -> p k n", p=P)),
                ("fexp", w_fa[:, :, :, :], io["L0_ffn_Wa"].rearrange("e (k p) r -> p e k r", p=P)),
                ("fexp", w_fb[:, :, :], io["L0_ffn_Wb"].rearrange("e p n -> p e n")),
                ("mom", w_aq[:, :, :], io["L1_attn_Wq"].rearrange("(k p) n -> p k n", p=P)),
                ("mom", w_ak[:, :, :], io["L1_attn_Wk"].rearrange("(k p) n -> p k n", p=P)),
                ("mom", w_av[:, :, :], io["L1_attn_Wv"].rearrange("(k p) n -> p k n", p=P)),
                ("mom", w_ag[:, :, :], io["L1_attn_Wg"].rearrange("(k p) n -> p k n", p=P)),
                ("mom", w_ao[:, :, :], io["L1_attn_Wo"].rearrange("(k p) n -> p k n", p=P)),
                ("feat", w_tq[:, :], io["wq_t"]),
                ("feat", w_tk[:, :], io["wk_t"]),
                ("feat", bq[:, :], io["bq"]),
                ("feat", bk[:, :], io["bk"]),
            ):
                sp.dma_start(t, src).then_inc(w_loaded[n], 16)
            for k in range(KD):
                sp.dma_start(w_aeq[:, k, :], io["wq_exp"][k]).then_inc(w_loaded["mom"], 16)
                sp.dma_start(w_aek[:, k, :], io["wk_exp"][k]).then_inc(w_loaded["mom"], 16)
            sp.wait_ge(s_fill, 1)
            for a in range(4):
                sp.dma_start(w_al[32 * a:32 * a + 32, a, :], io["L1_attn_Wgate"]).then_inc(w_loaded["mom"], 16)
            with sp.Fori(0, PAIRS) as turn:
                K2 = keys(turn)
                for K, b in zip(K2, bufs):
                    load(K, b)
                for K, b in zip(K2, bufs):
                    rot_rows(K, b)
                mom_rows(K2)
                turn_end(sp, turn)
                sp.wait_ge(arrived, 5)
                for c in [c for e in did.values() for c in e] + loaded + rowed + [c for s in slot_rows for c in s] + [
                        arrived]:
                    sp.sem_clear(c)
                sp.nop().then_inc(started, 1)

        @block.scalar
        def _(act):
            act.dma_start(norm1[:, :], io["norm1"]).then_inc(w_loaded["small"], 16)
            act.dma_start(cw[:, :, :], io["conv_w"]).then_inc(w_loaded["small"], 16)
            act.dma_start(cb[:, :], io["conv_b"]).then_inc(w_loaded["small"], 16)
            act.dma_start(norm2[:, :], io["norm2"]).then_inc(w_loaded["small"], 16)
            act.dma_start(mixn[:, :], io["mixn"]).then_inc(w_loaded["small"], 16)
            act.dma_start(w_in[:, :, :], io["L0_attn_in_proj_w"].rearrange("(k p) n -> p k n", p=P)).then_inc(
                w_loaded["in"], 16)
            act.wait_ge(s_ang, 1)
            nc.scalar.activation(sincos[:, :, :, :].rearrange("p a b c -> p (a b c)"),
                                 ang[:, :, :].rearrange("p a b -> p (a b)"), ACT.Sin).then_inc(s_sin, 1)
            act.wait_ge(w_loaded["small"], 16 * N_SMALL)
            nc.scalar.activation(aneg[:, :], aneg[:, :], ACT.Exp).then_inc(s_exp, 1)


            def turned(K, b, name):
                act.wait_ge(*K.ready("tensor", name))
                nc.scalar.copy(b.AT[:, :, :].rearrange("p k t -> p (k t)"), K.bank(name)).then_inc(
                    *K.step("scalar", name, frees=name))

            def mamba_in(K, b):
                if K.s == 0:
                    act.wait_ge(x_loaded, (K.turn + 1) * (16 * STREAMS))
                nc.scalar.copy(b.X[:, :, :].rearrange("p i d -> p (i d)"), xall[:, K.turn, K.s, :]).then_inc(
                    *K.step("scalar", "x_in"))
                yield
                yield
                act.wait_ge(*K.ready("tensor", "hT"))
                for k in range(KD):
                    nc.scalar.activation(b.AT[:, k, :], K.bank("hT")[:, k * T:(k + 1) * T], ACT.Copy,
                                         scale=norm1[:, k:k + 1]).then_inc(*K.step("scalar", f"hT{k}", frees="hT"))
                yield
                for j in range(NCH // 2):
                    act.wait_ge(*K.ready("tensor", f"xbc{j}"))
                    for c in (2 * j, 2 * j + 1):
                        nc.scalar.activation(b.XBC[:, c, :], K.bank(f"xbc{j}")[:, (c % 2) * T:(c % 2 + 1) * T],
                                             ACT.Identity, bias=cb[:, c:c + 1], scale=cw[:, c, 3:4]).then_inc(
                                                 *K.step("scalar", f"tap{c}"))
                yield
                for j in (2, 0, 1):
                    act.wait_ge(*K.ready("vector", f"conv{j}"))
                    nc.scalar.activation(b.TH[:, 2 * j:2 * j + 2, :], b.XBC[:, 2 * j:2 * j + 2, :],
                                         ACT.Tanh).then_inc(*K.step("scalar", f"th{j}"))
                for i in range(NT):
                    act.wait_ge(*K.ready("tensor", f"z{i}"))
                    nc.scalar.activation(b.G[:, i, :], K.bank(f"z{i}"), ACT.Tanh, scale=0.5).then_inc(
                        *K.step("scalar", f"thz{i}"))
                act.wait_ge(*K.ready("vector", "dt_low"))
                nc.scalar.activation(b.u, b.nab, ACT.Exp).then_inc(*K.step("scalar", "dt_exp"))

            def mamba_ssd(K, b):
                act.wait_ge(*K.ready("tensor", "bT"))
                nc.scalar.copy(b.BT[:, :], K.bank("bT")[:, 0:NS]).then_inc(*K.step("scalar", "bT", frees="bT"))
                for i in range(NT):
                    act.wait_ge(*K.ready("tensor", f"xsT{i}"))
                    nc.scalar.copy(b.XT[:, i, :], K.bank(f"xsT{i}")).then_inc(*K.step("scalar", f"xs{i}"))
                yield
                act.wait_ge(*K.ready("tensor", "cum"))
                nc.scalar.activation(b.dcy, K.bank("cum")[:, 0:2 * MH], ACT.Exp).then_inc(
                    *K.step("scalar", "decay", frees="cum"))
                for i in range(NT):
                    for j in range(2):
                        act.wait_ge(*K.ready("tensor", f"seg{i}{j}"))
                        nc.scalar.activation(b.E[i][:, 4 * j:4 * j + 4, :].rearrange("p h l -> p (h l)"),
                                             K.bank(f"seg{i}{j}"), ACT.Exp).then_inc(
                                                 *K.step("scalar", f"L{i}{j}", frees=f"seg{i}{j}"))
                yield
                act.wait_ge(*K.ready("tensor", "state"))
                nc.scalar.copy(b.ST[:, :], K.bank("state")).then_inc(*K.step("scalar", "state", frees="state"))

            def mamba_out(K, b):
                for i in range(NT):
                    act.wait_ge(*K.ready("vector", f"gated{i}"))
                    nc.scalar.activation(b.SQ[:, :], b.XT[:, i, :], ACT.Square,
                                         accum_out=b.ss[:, i:i + 1]).then_inc(*K.step("scalar", f"y_square{i}"))
                    act.wait_ge(*K.last("scalar"))
                yield
                for j in range(2):
                    act.wait_ge(*K.ready("tensor", f"ynT{j}"))
                    for k in (2 * j, 2 * j + 1):
                        nc.scalar.activation(b.YT[:, k, :], K.bank(f"ynT{j}")[:, (k % 2) * T:(k % 2 + 1) * T], ACT.Copy,
                                             scale=mixn[:, k:k + 1]).then_inc(
                                                 *K.step("scalar", f"yT{k}", frees=f"ynT{j}"))
                yield
                for i in range(NT):
                    act.wait_ge(*K.ready("vector", f"h1{i}"))
                    nc.scalar.activation(b.SQ[:, 0:D], b.H1[:, i, :], ACT.Square,
                                         accum_out=b.ss2[:, i:i + 1]).then_inc(*K.step("scalar", f"h_square{i}"))
                    act.wait_ge(*K.last("scalar"))
                yield
                act.wait_ge(*K.ready("tensor", "h2T"))
                for k in range(KD):
                    nc.scalar.activation(b.AT[:, k, :], K.bank("h2T")[:, k * T:(k + 1) * T], ACT.Copy,
                                         scale=norm2[:, k:k + 1]).then_inc(*K.step("scalar", f"h2T{k}", frees="h2T"))
                yield
                for j in range(KG):
                    m = min(P, INTER - j * P)
                    act.wait_ge(*K.ready("tensor", f"gu{j}"))
                    if j >= 2:
                        act.wait_ge(*K.ready("vector", f"ma{j - 2}"))
                    nc.scalar.activation(b.MTH[0:m, j % 2, :], K.bank(f"gu{j}")[0:m, 0:T], ACT.Tanh,
                                         scale=0.5).then_inc(*K.step("scalar", f"thg{j}"))

            def rot_in(K, b):
                act.wait_ge(*K.ready("pool", "v_pad"))
                act.wait_ge(*K.ready("tensor", "xv"))
                for i in range(NT):
                    nc.scalar.copy(b.V1[:, i, :, 0:XD], K.bank("xv")[:, i * D:(i + 1) * D].rearrange(
                        "p (h d) -> p h d", d=XD)).then_inc(*K.step("scalar", f"v{i}", frees="xv"))
                yield
                for n, t in (("xkT", b.KT), ("xqT", b.QT)):
                    if n == "xqT":
                        turned(K, b, "xT")
                        yield
                        yield
                    for c in range(2):
                        act.wait_ge(*K.ready("tensor", f"{n}{c}"))
                        if c == 0:
                            nc.scalar.copy(t[0:SHIFT, 0:2, :].rearrange("p f t -> p (f t)"),
                                           K.bank(f"{n}0")[0:SHIFT, :]).then_inc(
                                               *K.step("scalar", f"{n}0", frees=f"{n}0"))
                        else:
                            m = D - 2 * SHIFT
                            nc.scalar.copy(t[0:m, 2, :], K.bank(f"{n}1")[0:m, 0:T]).then_inc(
                                *K.step("scalar", f"{n}1", frees=f"{n}1"))

            def masked_pair(K, b, p, out, name):
                for e in range(2):
                    h = 2 * p + e
                    nc.scalar.activation(out[0:SHIFT, e, :], b.QT[:, h // HT, :], ACT.Copy,
                                         scale=head12[:, h % HT:h % HT + 1]).then_inc(
                                             *K.step("scalar", (name, p) if e else None))

            def rot_max(K, b):
                act.wait_ge(s_const, CONSTS)
                act.wait_ge(*K.last("scalar"))
                act.wait_ge(*K.ready("pool", "k_pad"))
                masked_pair(K, b, 0, b.QMB[0], "q_low")
                for p in range(1, NPAIR):
                    if p >= 2:
                        act.wait_ge(*K.ready("tensor", ("xs", p - 2)))
                    masked_pair(K, b, p, b.QMB[p % 2], "q_low")
                    yield

            def rot_heads(K, b):
                for p in range(QSLOTS - 1):
                    masked_pair(K, b, p, b.QM[p], "q_masked")
                for p in range(NPAIR):
                    if p + QSLOTS - 1 < NPAIR:
                        if p >= 1:
                            act.wait_ge(*K.ready("tensor", ("xt", p - 1, NT - 1)))
                        masked_pair(K, b, p + QSLOTS - 1, b.QM[(p + QSLOTS - 1) % QSLOTS], "q_masked")
                    if p >= 3:
                        act.wait_ge(*K.ready("tensor", ("weighed", p - 3)))
                    for k in range(NT):
                        act.wait_ge(*K.ready("tensor", ("xt", p, k)))
                        nc.scalar.activation(b.PT[p % 3][:, k, :, :].rearrange("p e t -> p (e t)"),
                                             K.bank(("xt", p, k)), ACT.Exp, scale=XD ** -0.5).then_inc(
                                                 *K.step("scalar", ("weights", p, k), frees=("xt", p, k)))
                    if p >= 4 and p % 4 == 0:
                        rot_values(K, b, p // 4 - 1)
                    yield
                rot_values(K, b, NPAIR // 4 - 1)

            def rot_out(K, b):
                turned(K, b, "xoF")
                yield

            def rot_values(K, b, g):
                act.wait_ge(*K.ready("tensor", ("xo", g)))
                if g >= 2:
                    act.wait_ge(*K.ready("tensor", ("xoT", g - 2)))
                nc.scalar.copy(b.OT[g % 2][:, :, :].rearrange("p e t -> p (e t)"), K.bank(("xo", g))).then_inc(
                    *K.step("scalar", ("oT", g), frees=("xo", g)))

            def low_rank(K, b):
                for i in range(NT):
                    act.wait_ge(*K.ready("vector", f"xn3{i}"))
                    nc.scalar.activation(b.SQF[:, :], b.XN[:, i, :], ACT.Square,
                                         accum_out=b.ss[:, i:i + 1]).then_inc(*K.step("scalar", f"x_square{i}"))
                    act.wait_ge(*K.last("scalar"))
                yield
                turned(K, b, "fT")
                for j in range(FE // 2):
                    yield
                    act.wait_ge(*K.ready("tensor", ("fa", j)))
                    if j >= 2:
                        act.wait_ge(*K.ready("tensor", ("fb", 2 * j - 3)))
                    nc.scalar.copy(b.FH[j % 2][:, :, :].rearrange("p e t -> p (e t)"), K.bank(("fa", j))).then_inc(
                        *K.step("scalar", ("fh", j), frees=("fa", j)))
                    if j == 1:
                        act.wait_ge(*K.ready("vector", "f_shifted"))
                        nc.scalar.activation(b.f[2], b.f[1], ACT.Exp).then_inc(*K.step("scalar", "f_exp"))

            def mom_in(K, b):
                yield
                turned(K, b, "aT")
                yield
                for n, t in (("aq", b.AQ), ("ak", b.AK)):
                    act.wait_ge(*K.ready("tensor", n))
                    nc.scalar.copy(t[:, :, :].rearrange("p k t -> p (k t)"), K.bank(n)).then_inc(
                        *K.step("scalar", n, frees=n))
                act.wait_ge(*K.ready("vector", "a_shifted"))
                nc.scalar.activation(b.r2d[1], b.r2d[0], ACT.Exp).then_inc(*K.step("scalar", "a_exp"))
                for i in range(NT):
                    act.wait_ge(*K.ready("tensor", f"av{i}"))
                    nc.scalar.copy(b.AV[:, i, :, 0:AV], K.bank(f"av{i}").rearrange("p (h d) -> p h d", d=AV)).then_inc(
                        *K.step("scalar", f"av{i}", frees=f"av{i}"))
                yield
                act.wait_ge(*K.ready("tensor", "amT"))
                nc.scalar.copy(b.MKT[:, :], K.bank("amT")[0:AH * AR, 0:T]).then_inc(
                    *K.step("scalar", "mask_rows", frees="amT"))

            def mom_masks(K, b, h):
                act.wait_ge(*K.ready("tensor", ("aem", h)))
                if h >= 1:
                    act.wait_ge(*K.ready("vector", ("ke", h - 1)))
                nc.scalar.copy(b.MB[:, :, :].rearrange("p e t -> p (e t)"), K.bank(("aem", h))[0:RH * AD, :]).then_inc(
                    *K.step("scalar", ("masks", h), frees=("aem", h)))

            def mom_queries(K, b, h, g):
                if g == 0:
                    act.wait_ge(*K.ready("tensor", ("aeq", h)))
                    if h >= 2:
                        act.wait_ge(*K.ready("tensor", ("at", h - 2, AR - 1)))
                nc.scalar.activation(b.QE[h % 2][0:RH * AD, :, g, :], K.bank(("aeq", h))[0:RH * AD, :].rearrange(
                    "p (e t) -> p e t", e=2), ACT.Copy, scale=mem3[:, g:g + 1]).then_inc(
                        *K.step("scalar", ("qe", h) if g == RH - 1 else None, frees=("aeq", h)))

            def mom_weights(K, b, h, q):
                n = h * AR + q
                act.wait_ge(*K.ready("tensor", ("at", h, q)))
                if n >= 2:
                    act.wait_ge(*K.ready("tensor", ("weighed_a", n - 2)))
                nc.scalar.activation(b.APT[n % 2][:, :, :].rearrange("p k t -> p (k t)"),
                                     K.bank(("at", h, q)), ACT.Exp, scale=AD ** -0.5).then_inc(
                                         *K.step("scalar", ("weights_a", n), frees=("at", h, q)))

            def mom_heads(K2):
                for n in range(-3, UNITS + 1):
                    now, after = 0 <= n < UNITS, n + 3 < UNITS
                    for q in range(AR):
                        if now:
                            mom_weights(*units(K2, n), q)
                        if q == 1 and after:
                            mom_masks(*units(K2, n + 3))
                        if q in (2, 3, 4) and after:
                            mom_queries(*units(K2, n + 3), q - 2)
                        if q in (3, 5) and now:
                            mom_values(*units(K2, n), q // 2 - 1)
                    if now:
                        mom_values(*units(K2, n), AR // 2 - 1)

            def mom_values(K, b, h, j):
                act.wait_ge(*K.ready("tensor", ("ao", h, j)))
                if h >= 1 and j == 0:
                    act.wait_ge(*K.ready("tensor", ("aoT", h - 1, NT - 1)))
                nc.scalar.copy(b.AOT[:, 2 * j:2 * j + 2, :].rearrange("p r t -> p (r t)"),
                               K.bank(("ao", h, j))[0:VW, :]).then_inc(
                                   *K.step("scalar", ("aoT", h, j), frees=("ao", h, j)))

            def mom_out(K, b):
                for i in range(NT):
                    act.wait_ge(*K.ready("tensor", f"ag{i}"))
                    nc.scalar.activation(b.AG[:, i, :], K.bank(f"ag{i}"), ACT.Tanh, scale=0.5).then_inc(
                        *K.step("scalar", f"thag{i}"))
                yield
                for j in range(2):
                    act.wait_ge(*K.ready("tensor", f"aoF{j}"))
                    nc.scalar.activation(b.AYT[:, 2 * j:2 * j + 2, :].rearrange("p k t -> p (k t)"),
                                         K.bank(f"aoF{j}"), ACT.Copy, scale=0.5).then_inc(
                                             *K.step("scalar", f"ayT{j}", frees=f"aoF{j}"))

            def feat(K, b):
                act.wait_ge(w_loaded["feat"], 16 * N_FEAT)
                for n, t, bias in (("tq", b.TQ, bq), ("tk", b.TK, bk)):
                    act.wait_ge(*K.ready("tensor", n))
                    nc.scalar.activation(t[:, :], K.bank(n)[:, 0:T], ACT.Identity, bias=bias[:, 0:1]).then_inc(
                        *K.step("scalar", n, frees=n))
                yield
                act.wait_ge(*K.ready("vector", "t_max"))
                for i in range(NT):
                    nc.scalar.activation(b.TP[:, i, :], K.bank("te")[:, i * T:(i + 1) * T], ACT.Exp,
                                         bias=b.ts[1][:, i:i + 1], accum_out=b.ts[2][:, i:i + 1]).then_inc(
                                             *K.step("scalar", f"t_exp{i}", frees="te"))
                yield
                act.wait_ge(*K.ready("tensor", "tpT"))
                nc.scalar.copy(b.TPT[:, :, :].rearrange("p k t -> p (k t)"), K.bank("tpT")).then_inc(
                    *K.step("scalar", "tpT", frees="tpT"))
                yield
                turned(K, b, "tT")

            act.wait_ge(w_loaded["small"], 16 * N_SMALL)
            act.wait_ge(s_half, 2)
            with act.Fori(0, PAIRS) as turn:
                K2 = keys(turn)
                run(BEFORE_MOM, K2, mamba_in=mamba_in, mamba_ssd=mamba_ssd, mamba_out=mamba_out, rot_in=rot_in,
                    rot_max=rot_max, rot_heads=rot_heads, rot_out=rot_out, low_rank=low_rank, mom_in=mom_in)
                mom_heads(K2)
                run(AFTER_MOM, K2, mom_out=mom_out, feat=feat)
                turn_end(act, turn)
                act.wait_ge(started, turn + 1)

        @block.tensor
        def _(pe):
            def take(K, name, banks=(0, 1, 2, 3)):
                ps, wait = K.take(name, banks)
                if wait is not None:
                    pe.wait_ge(*wait)
                return ps

            def mm(out, lhsT, rhs, first, last):
                return nc.tensor.matmul(out, lhsT, rhs, start=first, stop=last)

            def turn_tiles(K, name, src, cols=KD, banks=(0, 1, 2, 3), c0=0):
                ps = take(K, name, banks)
                for k in range(cols):
                    for i in range(NT):
                        last = nc.tensor.transpose(ps[:, k * T + i * P:k * T + (i + 1) * P],
                                                   src[:, i, (c0 + k) * P:(c0 + k + 1) * P], ident[:, :])
                last.then_inc(*K.step("tensor", name))

            def mamba_in(K, b):
                yield
                yield
                pe.wait_ge(*K.ready("vector", "h_scaled"))
                turn_tiles(K, "hT", b.H)
                yield
                pe.wait_ge(*K.ready("scalar", "hT1"))
                pe.wait_ge(w_loaded["in"], 16 * N_IN)
                for j in range(NCH // 2):
                    ps = take(K, f"xbc{j}")
                    for c in (2 * j, 2 * j + 1):
                        for k in range(KD):
                            last = mm(ps[:, (c % 2) * T:(c % 2 + 1) * T], w_in[:, k, DI + c * P:DI + (c + 1) * P],
                                      b.AT[:, k, :], k == 0, k == KD - 1)
                    last.then_inc(*K.step("tensor", f"xbc{j}"))
                ps = take(K, "dt")
                for i in range(NT):
                    for k in range(KD):
                        last = mm(ps[:, i * MH:(i + 1) * MH], b.AT[:, k, i * P:(i + 1) * P],
                                  w_in[:, k, DI + NCH * P:DI + NCH * P + MH], k == 0, k == KD - 1)
                last.then_inc(*K.step("tensor", "dt"))
                yield
                for i in range(NT):
                    ps = take(K, f"z{i}")
                    for k in range(KD):
                        last = mm(ps, b.AT[:, k, i * P:(i + 1) * P], w_in[:, k, 0:DI], k == 0, k == KD - 1)
                    last.then_inc(*K.step("tensor", f"z{i}"))

            def mamba_ssd(K, b):
                pe.wait_ge(*K.ready("vector", "xbc2"))
                ps = take(K, "cb")
                for i in range(NT):
                    last = mm(ps[:, i * P:(i + 1) * P], b.XBC[:, KI, i * P:(i + 1) * P],
                              b.XBC[:, KI + 1, i * P:(i + 1) * P], True, True)
                last.then_inc(*K.step("tensor", "cb"))
                ps = take(K, "bT")
                nc.tensor.transpose(ps[:, 0:NS], b.XBC[:, KI, 0:P], ident[:, :]).then_inc(*K.step("tensor", "bT"))
                pe.wait_ge(*K.ready("vector", "xbc1"))
                for i in range(NT):
                    ps = take(K, f"xsT{i}")
                    for c in range(KI):
                        last = nc.tensor.transpose(ps[:, c * P:(c + 1) * P], b.XBC[:, c, i * P:(i + 1) * P],
                                                   ident[:, :])
                    last.then_inc(*K.step("tensor", f"xsT{i}"))
                yield
                pe.wait_ge(*K.ready("vector", "dA"))
                pe.wait_ge(s_const, CONSTS)
                ps = take(K, "cum")
                mm(ps[:, 0:MH], gt[:, :], b.dA[:, 0, :], True, True)
                mm(ps[:, MH:2 * MH], le[:, :], b.dA[:, 1, :], True, True).then_inc(*K.step("tensor", "cum"))
                for i in range(NT):
                    pe.wait_ge(*K.ready("pool", f"dA_rows{i}"))
                    for j in range(2):
                        ps = take(K, f"seg{i}{j}")
                        mm(ps, gt[:, :], b.E[i][:, 4 * j:4 * j + 4, :].rearrange("p h l -> p (h l)"),
                           True, True).then_inc(*K.step("tensor", f"seg{i}{j}"))
                yield
                pe.wait_ge(*K.ready("pool", "x_decayed"))
                pe.wait_ge(*K.ready("scalar", "bT"))
                mm(take(K, "state"), b.BT[:, :], b.XDEC[:, :], True, True).then_inc(*K.step("tensor", "state"))
                for i in range(NT):
                    pe.wait_ge(*K.ready("vector", f"M{i}"))
                    ps = take(K, f"y{i}")
                    for h in range(MH):
                        last = mm(ps[:, h * MP:(h + 1) * MP], b.E[i][:, h, :], b.XDT[:, i, h * MP:(h + 1) * MP],
                                  True, True)
                    last.then_inc(*K.step("tensor", f"y{i}"))
                yield
                pe.wait_ge(*K.ready("scalar", "state"))
                mm(take(K, "yoff"), b.XBC[:, KI + 1, P:2 * P], b.ST[:, :], True, True).then_inc(
                    *K.step("tensor", "yoff"))

            def mamba_out(K, b):
                yield
                pe.wait_ge(*K.ready("vector", "gated1"))
                for j in range(2):
                    turn_tiles(K, f"ynT{j}", b.XT, c0=2 * j)
                yield
                pe.wait_ge(*K.ready("scalar", "yT3"))
                pe.wait_ge(w_loaded["mamba"], 16 * N_MAMBA)
                ps = take(K, "mo")
                for i in range(NT):
                    for k in range(KI):
                        last = mm(ps[:, i * D:(i + 1) * D], b.YT[:, k, i * P:(i + 1) * P], w_mo[:, k, :],
                                  k == 0, k == KI - 1)
                last.then_inc(*K.step("tensor", "mo"))
                yield
                pe.wait_ge(*K.ready("vector", "h2"))
                turn_tiles(K, "h2T", b.H)
                yield
                pe.wait_ge(*K.ready("scalar", "h2T1"))
                for j in range(KG):
                    m = min(P, INTER - j * P)
                    ps = take(K, f"gu{j}")
                    for n, w in enumerate((w_gate, w_up)):
                        for k in range(KD):
                            last = mm(ps[0:m, n * T:(n + 1) * T], w[:, k, j * P:j * P + m], b.AT[:, k, :],
                                      k == 0, k == KD - 1)
                    last.then_inc(*K.step("tensor", f"gu{j}"))
                yield
                pe.wait_ge(*K.ready("vector", f"ma{KG - 1}"))
                ps = take(K, "down")
                for i in range(NT):
                    for j in range(KG):
                        m = min(P, INTER - j * P)
                        last = mm(ps[:, i * D:(i + 1) * D], b.MA[0:m, j, i * P:(i + 1) * P], w_down[0:m, j, :],
                                  j == 0, j == KG - 1)
                last.then_inc(*K.step("tensor", "down"))

            def turn_heads(K, name, src):
                for c in range(2):
                    ps = take(K, f"{name}{c}")
                    for n in range(2 if c == 0 else 1):
                        c0 = (2 * c + n) * SHIFT
                        m = min(SHIFT, D - c0)
                        for i in range(NT):
                            last = nc.tensor.transpose(ps[0:m, n * T + i * P:n * T + (i + 1) * P],
                                                       src[:, i, c0:c0 + m], ident[:, :])
                    last.then_inc(*K.step("tensor", f"{name}{c}"))

            def rot_in(K, b):
                pe.wait_ge(loaded[K.s], 16)
                pe.wait_ge(w_loaded["rot"], 16 * N_ROT)
                for n, c in (("xk", 0), ("xv", D)):
                    ps = take(K, n)
                    for i in range(NT):
                        last = mm(ps[:, i * D:(i + 1) * D], b.CT[:, i * P:(i + 1) * P], w_xkv[:, c:c + D], True, True)
                    last.then_inc(*K.step("tensor", n))
                yield
                pe.wait_ge(*K.ready("vector", "k_turned"))
                turn_heads(K, "xkT", b.KR)
                pe.wait_ge(*K.ready("vector", "xn21"))
                turn_tiles(K, "xT", b.XN)
                yield
                pe.wait_ge(*K.ready("scalar", "xT"))
                ps = take(K, "xq")
                for i in range(NT):
                    for k in range(KD):
                        last = mm(ps[:, i * D:(i + 1) * D], b.AT[:, k, i * P:(i + 1) * P], w_xq[:, k, :],
                                  k == 0, k == KD - 1)
                last.then_inc(*K.step("tensor", "xq"))
                yield
                pe.wait_ge(*K.ready("vector", "q_turned"))
                turn_heads(K, "xqT", b.QR)

            def rot_max(K, b):
                pe.wait_ge(*K.ready("pool", "k_low"))
                for p in range(NPAIR):
                    pe.wait_ge(*K.ready("scalar", ("q_low", p)))
                    for i in range(NT):
                        ps = take(K, ("xs", p, i), (0, 1, 2))
                        for e in range(2):
                            last = mm(ps[:, e * T:(e + 1) * T], b.QMB[p % 2][:, e, i * P:(i + 1) * P],
                                      b.KTB[:, (2 * p + e) // HT, :], True, True)
                        last.then_inc(*K.step("tensor", ("xs", p, i)))
                    K.name_last("tensor", ("xs", p))
                    yield
                pe.wait_ge(*K.ready("vector", "x_max"))
                ps = take(K, "xm", (0, 1, 2))
                for i in range(NT):
                    last = nc.tensor.transpose(ps[0:XH, i * P:(i + 1) * P], b.MX[:, i, :], ident[:, :])
                last.then_inc(*K.step("tensor", "xm"))

            def rot_heads(K, b):
                for p in range(NPAIR + 1):
                    if p < NPAIR:
                        pe.wait_ge(*K.ready("scalar", ("q_masked", p)))
                        pe.wait_ge(slot_rows[K.s][p % QSLOTS], 16 * (p // QSLOTS + 1))
                        for k in range(NT):
                            ps = take(K, ("xt", p, k), (0, 1, 2))
                            mm(ps, b.KT[:, 2 * p // HT, k * P:(k + 1) * P],
                               b.QM[p % QSLOTS][:, :, :].rearrange("p e t -> p (e t)"), True, True).then_inc(
                                   *K.step("tensor", ("xt", p, k)))
                    if p >= 1:
                        weigh(K, b, p - 1)
                    if p > 1 and p % 4 == 1:
                        turn_values(K, b, p // 4 - 1)
                    yield
                turn_values(K, b, NPAIR // 4 - 1)

            def weigh(K, b, p):
                g = p % 4
                if p % 4 == 0:
                    take(K, ("xo", p // 4), (3,))
                ps = K.bank(("xo", p // 4))
                pe.wait_ge(*K.ready("scalar", ("weights", p, 1)))
                for e in range(2):
                    for k in range(NT):
                        last = mm(ps[32 * g:32 * g + 32, e * T:(e + 1) * T], b.V1[:, k, 2 * p + e, :],
                                  b.PT[p % 3][:, k, e, :], k == 0, k == NT - 1)
                last.then_inc(*K.step("tensor", ("weighed", p)))
                if p % 4 == 3:
                    K.name_last("tensor", ("xo", p // 4))

            def turn_values(K, b, g4):
                pe.wait_ge(*K.ready("scalar", ("oT", g4)))
                ps = take(K, ("xoT", g4), (0, 1, 2))
                for e in range(2):
                    for i in range(NT):
                        last = nc.tensor.transpose(ps[:, (2 * e + i) * P:(2 * e + i + 1) * P],
                                                   b.OT[g4 % 2][:, e, i * P:(i + 1) * P], ident[:, :])
                last.then_inc(*K.step("tensor", ("xoT", g4)))

            def rot_out(K, b):
                pe.wait_ge(*K.ready("vector", "x_heads3"))
                turn_tiles(K, "xoF", b.O)
                yield
                pe.wait_ge(*K.ready("scalar", "xoF"))
                ps = take(K, "xout")
                for i in range(NT):
                    for k in range(KD):
                        last = mm(ps[:, i * D:(i + 1) * D], b.AT[:, k, i * P:(i + 1) * P], w_xo[:, k, :],
                                  k == 0, k == KD - 1)
                last.then_inc(*K.step("tensor", "xout"))

            def low_rank(K, b):
                yield
                pe.wait_ge(*K.ready("vector", "xn31"))
                turn_tiles(K, "fT", b.XN)
                yield
                pe.wait_ge(*K.ready("scalar", "fT"))
                pe.wait_ge(w_loaded["fexp"], 16 * N_FEXP)
                ps = take(K, "fr")
                for i in range(NT):
                    for k in range(KD):
                        last = mm(ps[:, i * FE:(i + 1) * FE], b.AT[:, k, i * P:(i + 1) * P], w_fr[:, k, :],
                                  k == 0, k == KD - 1)
                last.then_inc(*K.step("tensor", "fr"))
                for j in range(FE // 2 + 1):
                    if j >= 1:
                        yield
                    if j < FE // 2:
                        ps = take(K, ("fa", j))
                        for e in range(2):
                            for k in range(KD):
                                last = mm(ps[:, e * T:(e + 1) * T], w_fa[:, 2 * j + e, k, :], b.AT[:, k, :],
                                          k == 0, k == KD - 1)
                        last.then_inc(*K.step("tensor", ("fa", j)))
                    if j >= 1:
                        pe.wait_ge(*K.ready("scalar", ("fh", j - 1)))
                        for e in range(2):
                            x = 2 * (j - 1) + e
                            ps = take(K, ("fb", x))
                            for i in range(NT):
                                last = mm(ps[:, i * D:(i + 1) * D], b.FH[(j - 1) % 2][:, e, i * P:(i + 1) * P],
                                          w_fb[:, x, :], True, True)
                            last.then_inc(*K.step("tensor", ("fb", x)))

            def mom_in(K, b):
                yield
                pe.wait_ge(*K.ready("vector", "xn41"))
                turn_tiles(K, "aT", b.XN)
                yield
                pe.wait_ge(*K.ready("scalar", "aT"))
                pe.wait_ge(w_loaded["mom"], 16 * N_MOM)
                for n, w in (("aq", w_aq), ("ak", w_ak)):
                    ps = take(K, n)
                    for m in range(KD):
                        for k in range(KD):
                            last = mm(ps[:, m * T:(m + 1) * T], w[:, k, m * P:(m + 1) * P], b.AT[:, k, :],
                                      k == 0, k == KD - 1)
                    last.then_inc(*K.step("tensor", n))
                pe.wait_ge(*K.ready("scalar", "aq"))
                ps = take(K, "al")
                for i in range(NT):
                    for k in range(KD):
                        c = 32 * i + 16 * k
                        last = mm(ps[:, c:c + 16], b.AQ[:, k, i * P:(i + 1) * P],
                                  w_al[:, :, :].rearrange("p a n -> p (a n)"), True, True)
                last.then_inc(*K.step("tensor", "al"))
                for i in range(NT):
                    ps = take(K, f"av{i}")
                    for k in range(KD):
                        last = mm(ps, b.AT[:, k, i * P:(i + 1) * P], w_av[:, k, :], k == 0, k == KD - 1)
                    last.then_inc(*K.step("tensor", f"av{i}"))
                yield
                pe.wait_ge(*K.ready("vector", "a_mask"))
                ps = take(K, "amT")
                for i in range(NT):
                    last = nc.tensor.transpose(ps[0:AH * AR, i * P:(i + 1) * P],
                                               b.MK[:, i, :, :].rearrange("p h r -> p (h r)"), ident[:, :])
                last.then_inc(*K.step("tensor", "amT"))

            def mom_project(K, b, h):
                a, kk, m = h % 4, h // 4, RH * AD
                r = slice(32 * a, 32 * a + 32)
                for n, w, src in (("aeq", w_aeq, b.AQ), ("aek", w_aek, b.AK)):
                    pe.wait_ge(*K.ready("scalar", "ak"))
                    ps = take(K, (n, h), (2,) if n == "aeq" else (3,))
                    for rh in range(2):
                        last = mm(ps[0:m, rh * T:(rh + 1) * T], w[r, kk, rh * m:(rh + 1) * m], src[r, kk, :],
                                  True, True)
                    last.then_inc(*K.step("tensor", (n, h)))
                pe.wait_ge(*K.ready("scalar", "mask_rows"))
                ps = take(K, ("aem", h), (0, 1))
                for rh in range(2):
                    last = mm(ps[0:m, rh * T:(rh + 1) * T], spread[:, 2 * h + rh, :], b.MKT[:, :], True, True)
                last.then_inc(*K.step("tensor", ("aem", h)))

            def mom_max(K, b, h, q):
                if q == 0:
                    pe.wait_ge(*K.ready("pool", ("ke_low", h)))
                ps = take(K, ("as", h, q), (0, 1))
                for i in range(NT):
                    last = mm(ps[:, i * T:(i + 1) * T], b.QEB[:, q // RH, q % RH, i * P:(i + 1) * P],
                              b.KEB[:, q // RH, :], True, True)
                last.then_inc(*K.step("tensor", ("as", h, q)))

            def mom_turn_max(K, b, h):
                pe.wait_ge(*K.ready("vector", ("a_max", h)))
                ps = take(K, ("am", h), (0, 1))
                for i in range(NT):
                    last = nc.tensor.transpose(ps[0:AR, i * P:(i + 1) * P], b.AMX[:, i, :], ident[:, :])
                last.then_inc(*K.step("tensor", ("am", h)))

            def mom_scores(K, b, h, q):
                if q == 0:
                    pe.wait_ge(rowed[K.s], 16 * (h + 1))
                ps = take(K, ("at", h, q), (0, 1))
                for k in range(NT):
                    last = mm(ps[:, k * T:(k + 1) * T], b.KE[h % 2][:, q // RH, k * P:(k + 1) * P],
                              b.QE[h % 2][:, q // RH, q % RH, :], True, True)
                last.then_inc(*K.step("tensor", ("at", h, q)))

            def mom_turn_values(K, b, h):
                pe.wait_ge(*K.ready("scalar", ("aoT", h, AR // 2 - 1)))
                for i in range(NT):
                    ps = take(K, ("aoT", h, i), (2 + i,))
                    for q in range(AR):
                        last = nc.tensor.transpose(ps[:, q * VW:(q + 1) * VW], b.AOT[:, q, i * P:(i + 1) * P],
                                                   ident[0:VW, 0:VW])
                    last.then_inc(*K.step("tensor", ("aoT", h, i)))

            def mom_heads(K2):
                for n in range(-3, UNITS + 1):
                    now, after = 0 <= n < UNITS, 0 <= n + 1 < UNITS
                    for q in range(AR):
                        if q == 0 and n + 3 < UNITS:
                            mom_project(*units(K2, n + 3))
                        if now and q + 2 < AR:
                            mom_scores(*units(K2, n), q + 2)
                        if after and q < AR // 2:
                            mom_max(*units(K2, n + 1), 2 * q)
                            if q > 0:
                                mom_max(*units(K2, n + 1), 2 * q + 1)
                        if after and q == AR // 2:
                            mom_turn_max(*units(K2, n + 1))
                        if q == AR - 1 and n >= 1:
                            mom_turn_values(*units(K2, n - 1))
                        if now:
                            mom_weigh(*units(K2, n), q)
                        if after and q == 0:
                            mom_max(*units(K2, n + 1), 1)
                    if after:
                        mom_scores(*units(K2, n + 1), 0)
                        mom_scores(*units(K2, n + 1), 1)

            def mom_weigh(K, b, h, q):
                n = h * AR + q
                if q % 2 == 0:
                    take(K, ("ao", h, q // 2), (2 + (q // 2) % 2,))
                ps = K.bank(("ao", h, q // 2))
                if q == 2:
                    pe.wait_ge(*K.ready("vector", ("vm", h)))
                pe.wait_ge(*K.ready("scalar", ("weights_a", n)))
                for k in range(NT):
                    v = b.AV[:, k, h, :] if q < AS else b.VM[h % 2][:, k, q - AS, :]
                    last = mm(ps[0:VW, (q % 2) * T:(q % 2 + 1) * T], v, b.APT[n % 2][:, k, :], k == 0, k == NT - 1)
                last.then_inc(*K.step("tensor", ("weighed_a", n)))
                if q % 2 == 1:
                    K.name_last("tensor", ("ao", h, q // 2))

            def mom_out(K, b):
                for i in range(NT):
                    ps = take(K, f"ag{i}")
                    for k in range(KD):
                        last = mm(ps, b.AT[:, k, i * P:(i + 1) * P], w_ag[:, k, :], k == 0, k == KD - 1)
                    last.then_inc(*K.step("tensor", f"ag{i}"))
                yield
                pe.wait_ge(*K.ready("vector", "a_gated1"))
                for j in range(2):
                    turn_tiles(K, f"aoF{j}", b.AO, c0=2 * j)
                yield
                pe.wait_ge(*K.ready("scalar", "ayT1"))
                ps = take(K, "aout")
                for i in range(NT):
                    for k in range(AH * AV // P):
                        last = mm(ps[:, i * D:(i + 1) * D], b.AYT[:, k, i * P:(i + 1) * P], w_ao[:, k, :],
                                  k == 0, k == AH * AV // P - 1)
                last.then_inc(*K.step("tensor", "aout"))

            def feat(K, b):
                pe.wait_ge(w_loaded["feat"], 16 * N_FEAT)
                for n, w in (("tq", w_tq), ("tk", w_tk)):
                    mm(take(K, n)[:, 0:T], w[:, :], b.CT[:, :], True, True).then_inc(*K.step("tensor", n))
                yield
                pe.wait_ge(*K.ready("scalar", "tk"))
                ps = take(K, "te")
                for i in range(NT):
                    last = mm(ps[:, i * T:(i + 1) * T], b.TQ[:, i * P:(i + 1) * P], b.TK[:, :], True, True)
                last.then_inc(*K.step("tensor", "te"))
                yield
                pe.wait_ge(*K.ready("vector", "t_norm1"))
                turn_tiles(K, "tpT", b.TP)
                yield
                pe.wait_ge(*K.ready("vector", "xn51"))
                turn_tiles(K, "tT", b.XN)
                yield
                pe.wait_ge(*K.ready("scalar", "tT"))
                ps = take(K, "tout")
                for i in range(NT):
                    for k in range(KD):
                        last = mm(ps[:, i * D:(i + 1) * D], b.AT[:, k, i * P:(i + 1) * P], b.TPT[:, k, :],
                                  k == 0, k == KD - 1)
                last.then_inc(*K.step("tensor", "tout"))

            pe.wait_ge(s_ident, 1)
            with pe.Fori(0, PAIRS) as turn:
                K2 = keys(turn)
                run(BEFORE_MOM, K2, mamba_in=mamba_in, mamba_ssd=mamba_ssd, mamba_out=mamba_out, rot_in=rot_in,
                    rot_max=rot_max, rot_heads=rot_heads, rot_out=rot_out, low_rank=low_rank, mom_in=mom_in)
                mom_heads(K2)
                run(AFTER_MOM, K2, mom_out=mom_out, feat=feat)
                turn_end(pe, turn)
                pe.wait_ge(started, turn + 1)

        @block.vector
        def _(dve):
            def statistics(K, b, q):
                for i in range(NT):
                    nc.vector.bn_stats(b.bst[:, i, :], b.X[:, i, :]).then_inc(*K.step("vector"))
                dve.wait_ge(*K.last("vector"))
                for i in range(NT):
                    nc.vector.bn_aggr(b.mv[:, i, :], b.bst[:, i, :]).then_inc(*K.step("vector", f"stat{q}{i}"))

            def normalised(K, b, q, known=False):
                if not known:
                    statistics(K, b, q)
                dve.wait_ge(*K.last("vector"))
                dve.wait_ge(*K.ready("pool", f"rstd{q}"))
                for i in range(NT):
                    nc.vector.tensor_scalar(b.XN[:, i, :], b.X[:, i, :], b.mv[:, i, 0:1], b.rstd[:, i:i + 1],
                                            ALU.subtract, ALU.mult).then_inc(*K.step("vector", f"xn{q}{i}"))

            def heads_in(t, n):
                return t.unsqueeze(2).broadcast_to([P, MH, n])

            def mamba_in(K, b):
                dve.wait_ge(*K.ready("scalar", "x_in"))
                statistics(K, b, 1)
                yield
                normalised(K, b, 1, known=True)
                dve.wait_ge(*K.ready("pool", "h_scale"))
                for i in range(NT):
                    nc.vector.tensor_scalar(b.H[:, i, :], b.X[:, i, :], b.mv[:, i, 0:1], b.rh[:, i:i + 1],
                                            ALU.subtract, ALU.mult).then_inc(*K.step("vector"))
                K.name_last("vector", "h_scaled")
                yield
                yield
                for j in range(NCH // 2):
                    ps = K.bank(f"xbc{j}")
                    dve.wait_ge(*K.ready("tensor", f"xbc{j}"))
                    for n in range(1, 4):
                        for c in (2 * j, 2 * j + 1):
                            if n == 1:
                                dve.wait_ge(*K.ready("scalar", f"tap{2 * j + 1}"))
                            elif c == 2 * j:
                                dve.wait_ge(*K.last("vector"))
                            t0 = (c % 2) * T
                            nc.vector.scalar_tensor_tensor(
                                out=b.XBC[:, c, n:T], in0=ps[:, t0:t0 + T - n], scalar=cw[:, c, 3 - n:4 - n],
                                in1=b.XBC[:, c, n:T], op0=ALU.mult, op1=ALU.add).then_inc(
                                    *K.step("vector", f"conv{j}" if (n, c) == (3, 2 * j + 1) else None,
                                            frees=f"xbc{j}" if (n, c) == (3, 2 * j + 1) else None))
                yield
                dve.wait_ge(*K.ready("tensor", "dt"))
                nc.vector.tensor_tensor(b.raw, K.bank("dt")[:, 0:NT * MH].rearrange("p (i h) -> p i h", i=NT),
                                        dtb[:, :].unsqueeze(1).broadcast_to([P, NT, MH]), ALU.add).then_inc(
                                            *K.step("vector", frees="dt"))
                dve.wait_ge(*K.last("vector"))
                nc.vector.scalar_tensor_tensor(out=b.nab, in0=b.raw, scalar=-1.0, in1=b.raw, op0=ALU.mult,
                                               op1=ALU.min).then_inc(*K.step("vector", "dt_low"))
                for j in (2, 0, 1):
                    dve.wait_ge(*K.ready("scalar", f"th{j}"))
                    nc.vector.scalar_tensor_tensor(out=b.XBC[:, 2 * j:2 * j + 2, :], in0=b.TH[:, 2 * j:2 * j + 2, :],
                                                   scalar=1.0, in1=b.XBC[:, 2 * j:2 * j + 2, :], op0=ALU.add,
                                                   op1=ALU.mult).then_inc(*K.step("vector", f"xbc{j}"))
                    if j < 2:
                        dve.wait_ge(*K.ready("scalar", f"thz{j}"))
                        nc.vector.scalar_tensor_tensor(out=b.G[:, j, :], in0=b.G[:, j, :], scalar=1.0,
                                                       in1=K.bank(f"z{j}"), op0=ALU.add, op1=ALU.mult).then_inc(
                                                           *K.step("vector", f"z_gate{j}", frees=f"z{j}"))
                dve.wait_ge(*K.ready("scalar", "dt_exp"))
                nc.vector.tensor_scalar(b.z2, b.u, 2.0, None, ALU.add).then_inc(*K.step("vector"))
                dve.wait_ge(*K.last("vector"))
                nc.vector.reciprocal(b.z, b.z2).then_inc(*K.step("vector"))
                dve.wait_ge(*K.last("vector"))
                nc.vector.tensor_tensor(b.z, b.z, b.u, ALU.mult).then_inc(*K.step("vector"))
                dve.wait_ge(*K.last("vector"))
                nc.vector.tensor_tensor(b.z2, b.z, b.z, ALU.mult).then_inc(*K.step("vector"))
                dve.wait_ge(*K.last("vector"))
                nc.vector.tensor_scalar(b.ser, b.z2, 1.0 / 17, None, ALU.mult).then_inc(*K.step("vector"))
                for n in range(15, 1, -2):
                    dve.wait_ge(*K.last("vector"))
                    nc.vector.scalar_tensor_tensor(out=b.ser, in0=b.ser, scalar=1.0 / n, in1=b.z2, op0=ALU.add,
                                                   op1=ALU.mult).then_inc(*K.step("vector"))
                dve.wait_ge(*K.last("vector"))
                nc.vector.scalar_tensor_tensor(out=b.ser, in0=b.ser, scalar=1.0, in1=b.z, op0=ALU.add,
                                               op1=ALU.mult).then_inc(*K.step("vector"))
                nc.vector.tensor_scalar(b.raw, b.raw, 0.0, None, ALU.max).then_inc(*K.step("vector"))
                dve.wait_ge(*K.last("vector"))
                nc.vector.scalar_tensor_tensor(out=b.dt, in0=b.ser, scalar=2.0, in1=b.raw, op0=ALU.mult,
                                               op1=ALU.add).then_inc(*K.step("vector"))
                dve.wait_ge(*K.last("vector"))
                nc.vector.tensor_tensor(b.dA, b.dt, aneg[:, :].unsqueeze(1).broadcast_to([P, NT, MH]),
                                        ALU.mult).then_inc(*K.step("vector", "dA"))

            def mamba_ssd(K, b):
                dve.wait_ge(s_const, CONSTS)
                dve.wait_ge(*K.ready("tensor", "cb"))
                for i in range(NT):
                    nc.vector.tensor_tensor(b.CB[:, i, :], K.bank("cb")[:, i * P:(i + 1) * P], le[:, :],
                                            ALU.mult).then_inc(*K.step("vector", frees="cb"))
                for i in range(NT):
                    dve.wait_ge(*K.ready("scalar", f"xs{i}"))
                    nc.vector.tensor_tensor(b.XDT[:, i, :].rearrange("p (h d) -> p h d", h=MH),
                                            K.bank(f"xsT{i}").rearrange("p (h d) -> p h d", h=MH),
                                            heads_in(b.dt[:, i, :], MP), ALU.mult).then_inc(
                                                *K.step("vector", f"x_dt{i}", frees=f"xsT{i}"))
                yield
                for i in range(NT):
                    dve.wait_ge(*K.ready("scalar", f"L{i}1"))
                    nc.vector.tensor_tensor(b.E[i][:, :, :], b.E[i][:, :, :],
                                            b.CB[:, i, :].unsqueeze(1).broadcast_to([P, MH, P]), ALU.mult).then_inc(
                                                *K.step("vector", f"M{i}"))
                yield

            def mamba_out(K, b):
                dve.wait_ge(*K.ready("tensor", "yoff"))
                nc.vector.tensor_tensor(b.YO[:, :].rearrange("p (h d) -> p h d", h=MH),
                                        K.bank("yoff").rearrange("p (h d) -> p h d", h=MH),
                                        heads_in(b.dcy[:, MH:2 * MH], MP), ALU.mult).then_inc(
                                            *K.step("vector", frees="yoff"))
                for i in range(NT):
                    dve.wait_ge(*K.ready("pool", f"x_skip{i}"))
                    dve.wait_ge(*K.ready("tensor", f"y{i}"))
                    nc.vector.tensor_tensor(b.XT[:, i, :], K.bank(f"y{i}"), b.XT[:, i, :], ALU.add).then_inc(
                        *K.step("vector", frees=f"y{i}"))
                dve.wait_ge(*K.last("vector"))
                nc.vector.tensor_tensor(b.XT[:, 1, :], b.XT[:, 1, :], b.YO[:, :], ALU.add).then_inc(*K.step("vector"))
                dve.wait_ge(*K.last("vector"))
                for i in range(NT):
                    nc.vector.tensor_tensor(b.XT[:, i, :], b.XT[:, i, :], b.G[:, i, :], ALU.mult).then_inc(
                        *K.step("vector", f"gated{i}"))
                yield
                yield
                dve.wait_ge(*K.ready("tensor", "mo"))
                dve.wait_ge(*K.ready("pool", "y_scale"))
                for i in range(NT):
                    nc.vector.scalar_tensor_tensor(out=b.H1[:, i, :], in0=K.bank("mo")[:, i * D:(i + 1) * D],
                                                   scalar=b.rs[:, i:i + 1], in1=b.XN[:, i, :], op0=ALU.mult,
                                                   op1=ALU.add).then_inc(*K.step("vector", f"h1{i}", frees="mo"))
                dve.wait_ge(*K.ready("pool", "h1_scale"))
                for i in range(NT):
                    nc.vector.tensor_scalar(b.H[:, i, :], b.H1[:, i, :], b.rs2[:, i:i + 1], None, ALU.mult).then_inc(
                        *K.step("vector"))
                K.name_last("vector", "h2")
                yield
                yield
                for j in range(KG):
                    m = min(P, INTER - j * P)
                    ps = K.bank(f"gu{j}")
                    dve.wait_ge(*K.ready("scalar", f"thg{j}"))
                    nc.vector.scalar_tensor_tensor(out=b.MA[0:m, j, :], in0=b.MTH[0:m, j % 2, :], scalar=1.0,
                                                   in1=ps[0:m, 0:T], op0=ALU.add, op1=ALU.mult).then_inc(
                                                       *K.step("vector"))
                    dve.wait_ge(*K.last("vector"))
                    nc.vector.tensor_tensor(b.MA[0:m, j, :], b.MA[0:m, j, :], ps[0:m, T:2 * T], ALU.mult).then_inc(
                        *K.step("vector", f"ma{j}", frees=f"gu{j}"))
                yield
                dve.wait_ge(*K.ready("tensor", "down"))
                dve.wait_ge(*K.ready("pool", "x_h1"))
                for i in range(NT):
                    nc.vector.scalar_tensor_tensor(out=b.X[:, i, :], in0=K.bank("down")[:, i * D:(i + 1) * D],
                                                   scalar=0.5, in1=b.X[:, i, :], op0=ALU.mult,
                                                   op1=ALU.add).then_inc(*K.step("vector", frees="down"))
                dve.wait_ge(*K.last("vector"))

            def rotate(K, b, group, out, name):
                ps = K.bank(group)
                sc = b.sc
                dve.wait_ge(*K.ready("tensor", group))
                for i in range(NT):
                    x = ps[:, i * D:(i + 1) * D].rearrange("p (h f e) -> p h f e", f=4, e=2)
                    for t, c in ((b.QS, 0), (b.QC, 4)):
                        for e in range(2):
                            nc.vector.tensor_tensor(
                                t[:, i, :].rearrange("p (h f e) -> p h f e", f=4, e=2)[:, :, :, e], x[:, :, :, e],
                                sc[:, i, c:c + 4].unsqueeze(1).broadcast_to([P, XH, 4]), ALU.mult).then_inc(
                                    *K.step("vector", frees=group))
                dve.wait_ge(*K.last("vector"))
                qs, qc, o = (t[:, :, :].rearrange("p i (n e) -> p i n e", e=2) for t in (b.QS, b.QC, out))
                nc.vector.tensor_tensor(o[:, :, :, 0], qc[:, :, :, 0], qs[:, :, :, 1], ALU.subtract).then_inc(
                    *K.step("vector"))
                nc.vector.tensor_tensor(o[:, :, :, 1], qs[:, :, :, 0], qc[:, :, :, 1], ALU.add).then_inc(
                    *K.step("vector", name))
                dve.wait_ge(*K.last("vector"))

            def rot_in(K, b):
                dve.wait_ge(s_sin, 1)
                nc.vector.tensor_copy(b.sc.rearrange("p i c -> p (i c)"), sincos[:, K.turn, K.s, :]).then_inc(
                    *K.step("vector"))
                dve.wait_ge(*K.last("vector"))
                statistics(K, b, 2)
                rotate(K, b, "xk", b.KR, "k_turned")
                normalised(K, b, 2, known=True)
                yield
                yield
                rotate(K, b, "xq", b.QR, "q_turned")
                yield

            def rot_max(K, b):
                for p in range(NPAIR):
                    h0 = 2 * p
                    for i in range(NT):
                        dve.wait_ge(*K.ready("tensor", ("xs", p, i)))
                        nc.vector.tensor_reduce(b.MX[:, i, h0:h0 + 2],
                                                K.bank(("xs", p, i)).rearrange("p (e t) -> p e t", e=2), AX.X, ALU.max,
                                                ).then_inc(*K.step("vector", frees=("xs", p, i)))
                    yield
                dve.wait_ge(*K.last("vector"))
                nc.vector.tensor_scalar(b.MX[:, :, :], b.MX[:, :, :], -1.0, None, ALU.mult).then_inc(
                    *K.step("vector", "x_max"))
                dve.wait_ge(*K.ready("tensor", "xm"))
                nc.vector.tensor_copy(b.NMT[:, :], K.bank("xm")[0:XH, 0:T]).then_inc(
                    *K.step("vector", "xnm", frees="xm"))

            def rot_heads(K, b):
                yield
                for g4 in range(NPAIR // 4):
                    for _ in range(4):
                        yield
                    dve.wait_ge(*K.ready("tensor", ("xoT", g4)))
                    ps = K.bank(("xoT", g4)).rearrange("p (n c d) -> p n c d", n=4, d=32)
                    if g4:
                        dve.wait_ge(*K.last("vector"))
                    nc.vector.reciprocal(b.RD[:, :, :], ps[:, :, :, XD]).then_inc(*K.step("vector"))
                    dve.wait_ge(*K.last("vector"))
                    for e in range(2):
                        for i in range(NT):
                            o = b.O[:, i, :].rearrange("p (h d) -> p h d", d=XD)[:, 8 * g4 + e:8 * g4 + 8:2, :]
                            nc.vector.tensor_tensor(o, ps[:, 2 * e + i, :, 0:XD],
                                                    b.RD[:, 2 * e + i, :].unsqueeze(2).broadcast_to([P, 4, XD]),
                                                    ALU.mult).then_inc(*K.step("vector", frees=("xoT", g4)))
                    K.name_last("vector", f"x_heads{g4}")

            def add_block(K, b, name):
                dve.wait_ge(*K.ready("tensor", name))
                nc.vector.tensor_tensor(b.X[:, :, :].rearrange("p i d -> p (i d)"), K.bank(name),
                                        b.X[:, :, :].rearrange("p i d -> p (i d)"), ALU.add).then_inc(
                                            *K.step("vector", frees=name))
                dve.wait_ge(*K.last("vector"))

            def rot_out(K, b):
                yield
                dve.wait_ge(*K.ready("pool", "x_bias"))
                add_block(K, b, "xout")

            def low_rank(K, b):
                normalised(K, b, 3)
                yield
                yield
                lg, lo, ex, v8, gt_, eq, cum, sel = b.f[0], b.f[1], b.f[2], b.f[3], b.f[4], b.f[5], b.f[6], b.f[7]
                comb = b.f[8]
                need, tot = b.fs[0], b.fs[1]
                dve.wait_ge(*K.ready("tensor", "fr"))
                dve.wait_ge(*K.ready("pool", "f_inverse"))
                for i in range(NT):
                    nc.vector.tensor_scalar(lg[:, i, :], K.bank("fr")[:, i * FE:(i + 1) * FE], b.rs[:, i:i + 1], None,
                                            ALU.mult).then_inc(*K.step("vector", frees="fr"))
                dve.wait_ge(*K.last("vector"))
                for i in range(NT):
                    nc.vector.max(v8[:, i, :], lg[:, i, :]).then_inc(*K.step("vector"))
                dve.wait_ge(*K.last("vector"))
                nc.vector.tensor_tensor(lo, lg, v8[:, :, 0:1].broadcast_to([P, NT, FE]), ALU.subtract).then_inc(
                    *K.step("vector", "f_shifted"))
                second = v8[:, :, 1:2].broadcast_to([P, NT, FE])
                nc.vector.tensor_tensor(gt_, lg, second, ALU.is_gt).then_inc(*K.step("vector"))
                nc.vector.tensor_tensor(eq, lg, second, ALU.is_equal).then_inc(*K.step("vector"))
                dve.wait_ge(*K.last("vector"))
                nc.vector.tensor_reduce(need, gt_, AX.X, ALU.add).then_inc(*K.step("vector"))
                for i in range(NT):
                    nc.vector.tensor_tensor_scan(cum[:, i, :], eq[:, i, :], eq[:, i, :], 0.0, ALU.add,
                                                 ALU.max).then_inc(*K.step("vector"))
                dve.wait_ge(*K.last("vector"))
                nc.vector.tensor_tensor(cum, cum, need.unsqueeze(2).broadcast_to([P, NT, FE]), ALU.add).then_inc(
                    *K.step("vector"))
                dve.wait_ge(*K.last("vector"))
                nc.vector.scalar_tensor_tensor(out=eq, in0=cum, scalar=2.5, in1=eq, op0=ALU.is_lt,
                                               op1=ALU.mult).then_inc(*K.step("vector"))
                dve.wait_ge(*K.last("vector"))
                nc.vector.tensor_tensor(sel, gt_, eq, ALU.add).then_inc(*K.step("vector"))
                dve.wait_ge(*K.last("vector"))
                yield
                dve.wait_ge(*K.ready("scalar", "f_exp"))
                nc.vector.tensor_tensor(sel, sel, ex, ALU.mult).then_inc(*K.step("vector"))
                dve.wait_ge(*K.last("vector"))
                nc.vector.tensor_reduce(tot, sel, AX.X, ALU.add).then_inc(*K.step("vector"))
                dve.wait_ge(*K.last("vector"))
                nc.vector.reciprocal(need, tot).then_inc(*K.step("vector"))
                dve.wait_ge(*K.last("vector"))
                nc.vector.tensor_tensor(comb, sel, need.unsqueeze(2).broadcast_to([P, NT, FE]), ALU.mult).then_inc(
                    *K.step("vector"))
                dve.wait_ge(*K.last("vector"))
                for e in range(FE):
                    if e >= 2 and e % 2 == 0:
                        yield
                    dve.wait_ge(*K.ready("tensor", ("fb", e)))
                    for i in range(NT):
                        nc.vector.scalar_tensor_tensor(out=b.X[:, i, :], in0=K.bank(("fb", e))[:, i * D:(i + 1) * D],
                                                       scalar=comb[:, i, e:e + 1], in1=b.X[:, i, :], op0=ALU.mult,
                                                       op1=ALU.add).then_inc(*K.step("vector", frees=("fb", e)))
                    dve.wait_ge(*K.last("vector"))

            def mom_in(K, b):
                normalised(K, b, 4)
                G = NT * AH
                for i in range(NT):
                    nc.vector.memset(b.AV[:, i, :, AV:VW], 1.0).then_inc(*K.step("vector"))
                yield
                yield
                lo, pr, sel, rk = b.r2d[0], b.r2d[1], b.r2d[2], b.r2d[3]
                mx, tot, inv = b.r1
                above, same, _ = b.r3
                dve.wait_ge(*K.ready("tensor", "al"))
                lg = K.bank("al")[:, 0:4 * G].rearrange("p (g n) -> p g n", n=4)
                nc.vector.tensor_reduce(mx, lg, AX.X, ALU.max).then_inc(*K.step("vector"))
                dve.wait_ge(*K.last("vector"))
                nc.vector.tensor_tensor(lo, lg, mx.unsqueeze(2).broadcast_to([P, G, 4]), ALU.subtract).then_inc(
                    *K.step("vector", "a_shifted", frees="al"))
                dve.wait_ge(*K.ready("scalar", "a_exp"))
                mine = pr.unsqueeze(3).broadcast_to([P, G, 4, 4])
                other = pr.unsqueeze(2).broadcast_to([P, G, 4, 4])
                nc.vector.tensor_tensor(above, other, mine, ALU.is_gt).then_inc(*K.step("vector"))
                nc.vector.tensor_tensor(same, other, mine, ALU.is_equal).then_inc(*K.step("vector"))
                dve.wait_ge(*K.last("vector"))
                nc.vector.tensor_tensor(same.rearrange("p g a b -> p g (a b)"), same.rearrange("p g a b -> p g (a b)"),
                                        below[:, :, :].rearrange("p a b -> p (a b)").unsqueeze(1).broadcast_to(
                                            [P, G, 16]), ALU.mult).then_inc(*K.step("vector"))
                dve.wait_ge(*K.last("vector"))
                nc.vector.tensor_tensor(above, above, same, ALU.add).then_inc(*K.step("vector"))
                dve.wait_ge(*K.last("vector"))
                nc.vector.tensor_reduce(rk, above, AX.X, ALU.add).then_inc(*K.step("vector"))
                dve.wait_ge(*K.last("vector"))
                nc.vector.scalar_tensor_tensor(out=sel, in0=rk, scalar=1.5, in1=pr, op0=ALU.is_lt,
                                               op1=ALU.mult).then_inc(*K.step("vector"))
                dve.wait_ge(*K.last("vector"))
                nc.vector.tensor_reduce(tot, sel, AX.X, ALU.add).then_inc(*K.step("vector"))
                dve.wait_ge(*K.last("vector"))
                nc.vector.reciprocal(inv, tot).then_inc(*K.step("vector"))
                dve.wait_ge(*K.last("vector"))
                nc.vector.tensor_tensor(sel, sel, inv.unsqueeze(2).broadcast_to([P, G, 4]), ALU.mult).then_inc(
                    *K.step("vector"))
                dve.wait_ge(*K.last("vector"))
                nc.vector.tensor_reduce(tot, sel, AX.X, ALU.add).then_inc(*K.step("vector"))
                dve.wait_ge(*K.last("vector"))
                nc.vector.tensor_scalar(tot, tot, 1.0, None, ALU.add).then_inc(*K.step("vector"))
                dve.wait_ge(*K.last("vector"))
                nc.vector.reciprocal(inv, tot).then_inc(*K.step("vector"))
                dve.wait_ge(*K.last("vector"))
                rw = b.RW[:, :, :, :].rearrange("p i h r -> p (i h) r")
                mk = b.MK[:, :, :, :].rearrange("p i h r -> p (i h) r")
                nc.vector.tensor_tensor(rw[:, :, AS:AR], sel, inv.unsqueeze(2).broadcast_to([P, G, AR - AS]),
                                        ALU.mult).then_inc(*K.step("vector"))
                nc.vector.tensor_scalar(rw[:, :, 0:AS], inv.unsqueeze(2).broadcast_to([P, G, AS]), 1.0 / AS, None,
                                        ALU.mult).then_inc(*K.step("vector"))
                dve.wait_ge(*K.last("vector"))
                nc.vector.tensor_scalar(mk, rw, 0.0, None, ALU.not_equal).then_inc(*K.step("vector", "a_mask"))
                yield

            def mom_keys(K, b, h):
                m = RH * AD
                dve.wait_ge(*K.ready("tensor", ("aek", h)))
                dve.wait_ge(*K.ready("scalar", ("masks", h)))
                if h >= 2:
                    dve.wait_ge(*K.ready("tensor", ("at", h - 2, AR - 1)))
                nc.vector.tensor_tensor(b.KE[h % 2][0:m, :, :].rearrange("p e t -> p (e t)"), K.bank(("aek", h))[0:m, :],
                                        b.MB[:, :, :].rearrange("p e t -> p (e t)"), ALU.mult).then_inc(
                                            *K.step("vector", ("ke", h), frees=("aek", h)))

            def mom_max(K, b, h):
                for q in range(AR):
                    dve.wait_ge(*K.ready("tensor", ("as", h, q)))
                    nc.vector.tensor_reduce(b.AMX[:, :, q:q + 1], K.bank(("as", h, q)).rearrange(
                        "p (i t) -> p i t", i=NT), AX.X, ALU.max).then_inc(*K.step("vector", frees=("as", h, q)))
                dve.wait_ge(*K.last("vector"))
                nc.vector.tensor_scalar(b.AMX[:, :, :], b.AMX[:, :, :], -1.0, None, ALU.mult).then_inc(
                    *K.step("vector", ("a_max", h)))

            def mom_rows_out(K, b, h):
                dve.wait_ge(*K.ready("tensor", ("am", h)))
                nc.vector.tensor_copy(b.ANT[:, :], K.bank(("am", h))[0:AR, 0:T]).then_inc(
                    *K.step("vector", f"anm{h}", frees=("am", h)))

            def mom_values(K, b, h):
                if h == 0:
                    dve.wait_ge(*K.ready("scalar", "av1"))
                if h >= 2:
                    dve.wait_ge(*K.ready("tensor", ("weighed_a", (h - 1) * AR - 1)))
                for k in range(NT):
                    nc.vector.tensor_tensor(b.VM[h % 2][:, k, :, 0:AV],
                                            b.AV[:, k, h, 0:AV].unsqueeze(1).broadcast_to([P, AR - AS, AV]),
                                            b.MK[:, k, h, AS:AR].unsqueeze(2).broadcast_to([P, AR - AS, AV]),
                                            ALU.mult).then_inc(*K.step("vector"))
                    nc.vector.memset(b.VM[h % 2][:, k, :, AV:VW], 1.0).then_inc(*K.step("vector"))
                K.name_last("vector", ("vm", h))

            def mom_combine(K, b, h):
                for i in range(NT):
                    dve.wait_ge(*K.ready("tensor", ("aoT", h, i)))
                    ps = K.bank(("aoT", h, i))[:, 0:AR * VW].rearrange("p (r c) -> p r c", r=AR)
                    nc.vector.reciprocal(b.CO[:, :], ps[:, :, AV]).then_inc(*K.step("vector"))
                    dve.wait_ge(*K.last("vector"))
                    nc.vector.tensor_tensor(b.CO[:, :], b.CO[:, :], b.RW[:, i, h, :], ALU.mult).then_inc(
                        *K.step("vector"))
                    dve.wait_ge(*K.last("vector"))
                    nc.vector.tensor_tensor(b.TMP[:, :, :], ps[:, :, 0:AV],
                                            b.CO[:, :].unsqueeze(2).broadcast_to([P, AR, AV]), ALU.mult).then_inc(
                                                *K.step("vector", frees=("aoT", h, i)))
                    dve.wait_ge(*K.last("vector"))
                    nc.vector.tensor_reduce(b.AO[:, i, h * AV:(h + 1) * AV],
                                            b.TMP[:, :, :].rearrange("p r c -> p c r"), AX.X, ALU.add).then_inc(
                                                *K.step("vector"))

            def mom_heads(K2):
                for n in range(-3, UNITS + 1):
                    if n + 3 < UNITS:
                        mom_keys(*units(K2, n + 3))
                    if 0 <= n + 1 < UNITS:
                        mom_max(*units(K2, n + 1))
                        mom_rows_out(*units(K2, n + 1))
                        mom_values(*units(K2, n + 1))
                    if n >= 1:
                        mom_combine(*units(K2, n - 1))

            def mom_out(K, b):
                for i in range(NT):
                    dve.wait_ge(*K.ready("scalar", f"thag{i}"))
                    nc.vector.scalar_tensor_tensor(out=b.AG[:, i, :], in0=b.AG[:, i, :], scalar=1.0,
                                                   in1=K.bank(f"ag{i}"), op0=ALU.add, op1=ALU.mult).then_inc(
                                                       *K.step("vector", frees=f"ag{i}"))
                dve.wait_ge(*K.last("vector"))
                for i in range(NT):
                    nc.vector.tensor_tensor(b.AO[:, i, :], b.AO[:, i, :], b.AG[:, i, :], ALU.mult).then_inc(
                        *K.step("vector", f"a_gated{i}"))
                yield
                yield
                add_block(K, b, "aout")
                dve.wait_ge(*K.last("vector"))
                normalised(K, b, 5)

            def feat(K, b):
                mx, neg, tot, inv = b.ts[0:4]
                yield
                dve.wait_ge(*K.ready("tensor", "te"))
                nc.vector.tensor_reduce(mx, K.bank("te").rearrange("p (i t) -> p i t", i=NT), AX.X, ALU.max).then_inc(
                    *K.step("vector"))
                dve.wait_ge(*K.last("vector"))
                nc.vector.tensor_scalar(neg, mx, -1.0, None, ALU.mult).then_inc(*K.step("vector", "t_max"))
                dve.wait_ge(*K.ready("scalar", "t_exp1"))
                nc.vector.reciprocal(inv, tot).then_inc(*K.step("vector"))
                dve.wait_ge(*K.last("vector"))
                for i in range(NT):
                    nc.vector.tensor_scalar(b.TP[:, i, :], b.TP[:, i, :], inv[:, i:i + 1], None, ALU.mult).then_inc(
                        *K.step("vector", f"t_norm{i}"))
                yield
                yield
                yield
                dve.wait_ge(*K.ready("tensor", "tout"))
                nc.vector.tensor_tensor(xall[:, K.turn, K.s, :], K.bank("tout"),
                                        b.X[:, :, :].rearrange("p i d -> p (i d)"), ALU.add).then_inc(
                                            *K.step("vector", frees="tout"))

            dve.wait_ge(w_loaded["small"], 16 * N_SMALL)
            for f in range(2):
                nc.vector.tensor_scalar(ang[:, :, f:4:2], posn[:, :, :], [1.0, 0.01][f], None, ALU.mult).then_inc(
                    s_half, 1)
            dve.wait_ge(s_half, 2)
            nc.vector.tensor_scalar(ang[:, :, 4:8], ang[:, :, 0:4], HALF_PI, None, ALU.add).then_inc(s_ang, 1)
            nc.vector.tensor_scalar(cw[:, :, :], cw[:, :, :], 0.5, None, ALU.mult).then_inc(s_half, 1)
            nc.vector.tensor_scalar(cb[:, :], cb[:, :], 0.5, None, ALU.mult).then_inc(s_half, 1)
            dve.wait_ge(s_exp, 1)
            nc.vector.tensor_scalar(aneg[:, :], aneg[:, :], -1.0, None, ALU.mult).then_inc(s_half, 1)
            dve.wait_ge(s_half, 5)
            with dve.Fori(0, PAIRS) as turn:
                K2 = keys(turn)
                run(BEFORE_MOM, K2, mamba_in=mamba_in, mamba_ssd=mamba_ssd, mamba_out=mamba_out, rot_in=rot_in,
                    rot_max=rot_max, rot_heads=rot_heads, rot_out=rot_out, low_rank=low_rank, mom_in=mom_in)
                mom_heads(K2)
                run(AFTER_MOM, K2, mom_out=mom_out, feat=feat)
                turn_end(dve, turn)
                dve.wait_ge(started, turn + 1)

        @block.gpsimd
        def _(pool):
            def power(K, out, base, name):
                pool.wait_ge(*K.last("pool"))
                nc.gpsimd.tensor_tensor(out, base, pw[:, :], ALU.pow).then_inc(*K.step("pool", name))

            def inverse_deviation(K, b, q):
                pool.wait_ge(*K.ready("vector", f"stat{q}1"))
                if K.taken.get("pool"):
                    pool.wait_ge(*K.last("pool"))
                nc.gpsimd.tensor_scalar(b.ve, b.mv[:, :, 1], 1e-5, None, ALU.add).then_inc(*K.step("pool"))
                power(K, b.rstd, b.ve, f"rstd{q}")

            def mamba_in(K, b):
                inverse_deviation(K, b, 1)
                pool.wait_ge(*K.last("pool"))
                nc.gpsimd.tensor_tensor(b.r2, b.rstd, b.rstd, ALU.mult).then_inc(*K.step("pool"))
                pool.wait_ge(*K.last("pool"))
                nc.gpsimd.tensor_tensor(b.r2, b.r2, b.mv[:, :, 1], ALU.mult).then_inc(*K.step("pool"))
                pool.wait_ge(*K.last("pool"))
                nc.gpsimd.tensor_scalar(b.r2, b.r2, 1e-6, None, ALU.add).then_inc(*K.step("pool"))
                power(K, b.rh, b.r2, None)
                pool.wait_ge(*K.last("pool"))
                nc.gpsimd.tensor_tensor(b.rh, b.rh, b.rstd, ALU.mult).then_inc(*K.step("pool", "h_scale"))
                yield
                yield
                yield
                yield

            def mamba_ssd(K, b):
                pool.wait_ge(*K.ready("vector", "dA"))
                for i in range(NT):
                    nc.gpsimd.tensor_tensor(b.E[i][:, :, :], le[:, :].unsqueeze(1).broadcast_to([P, MH, P]),
                                            b.dA[:, i, :].unsqueeze(2).broadcast_to([P, MH, P]), ALU.mult).then_inc(
                                                *K.step("pool", f"dA_rows{i}"))
                yield
                pool.wait_ge(*K.ready("scalar", "decay"))
                pool.wait_ge(*K.ready("vector", "x_dt0"))
                nc.gpsimd.tensor_tensor(b.XDEC[:, :].rearrange("p (h d) -> p h d", h=MH),
                                        b.XDT[:, 0, :].rearrange("p (h d) -> p h d", h=MH),
                                        b.dcy[:, 0:MH].unsqueeze(2).broadcast_to([P, MH, MP]), ALU.mult).then_inc(
                                            *K.step("pool", "x_decayed"))
                for i in range(NT):
                    pool.wait_ge(*K.ready("scalar", f"xs{i}"))
                    nc.gpsimd.tensor_tensor(b.XT[:, i, :].rearrange("p (h d) -> p h d", h=MH),
                                            b.XT[:, i, :].rearrange("p (h d) -> p h d", h=MH),
                                            dpar[:, :].unsqueeze(2).broadcast_to([P, MH, MP]), ALU.mult).then_inc(
                                                *K.step("pool", f"x_skip{i}"))
                yield

            def mamba_out(K, b):
                pool.wait_ge(*K.ready("scalar", "y_square1"))
                nc.gpsimd.tensor_scalar(b.ss, b.ss, 1.0 / DI, 4e-6, ALU.mult, ALU.add).then_inc(*K.step("pool"))
                power(K, b.rs, b.ss, "y_scale")
                yield
                yield
                pool.wait_ge(*K.ready("scalar", "h_square1"))
                nc.gpsimd.tensor_scalar(b.ss2, b.ss2, 1.0 / D, 1e-6, ALU.mult, ALU.add).then_inc(*K.step("pool"))
                power(K, b.rs2, b.ss2, "h1_scale")
                nc.gpsimd.tensor_tensor(b.X[:, :, :], b.X[:, :, :], b.H1[:, :, :], ALU.add).then_inc(
                    *K.step("pool", "x_h1"))
                yield
                yield
                yield

            def rot_in(K, b):
                inverse_deviation(K, b, 2)
                pool.wait_ge(*K.ready("tensor", "down"))
                nc.gpsimd.memset(b.V1[:, :, :, :].rearrange("p i h d -> p (i h) d")[:, :, XD:XD + 1], 1.0).then_inc(
                    *K.step("pool"))
                nc.gpsimd.memset(b.V1[:, :, :, :].rearrange("p i h d -> p (i h) d")[:, :, XD + 1:32], 0.0).then_inc(
                    *K.step("pool", "v_pad"))
                m = D - 2 * SHIFT
                pool.wait_ge(*K.last("pool"))
                nc.gpsimd.memset(b.QT[m:SHIFT, 2, :], 0.0).then_inc(*K.step("pool"))
                nc.gpsimd.memset(b.KT[m:SHIFT, 2, :], 0.0).then_inc(*K.step("pool"))
                pool.wait_ge(*K.last("pool"))
                nc.gpsimd.memset(b.KT[SHIFT:SHIFT + 1, :, :], 1.0).then_inc(*K.step("pool", "k_pad"))
                pool.wait_ge(*K.last("pool"))
                yield
                pool.wait_ge(*K.ready("scalar", "xkT1"))
                nc.gpsimd.tensor_copy(b.KTB[:, :, :], b.KT[0:SHIFT, :, :]).then_inc(*K.step("pool", "k_low"))
                pool.wait_ge(*K.last("pool"))
                yield
                yield

            def rot_out(K, b):
                pool.wait_ge(*K.ready("vector", "xn21"))
                pool.wait_ge(*K.last("pool"))
                nc.gpsimd.tensor_tensor(b.X[:, :, :], b.X[:, :, :],
                                        bout[:, :].unsqueeze(1).broadcast_to([P, NT, D]), ALU.add).then_inc(
                                            *K.step("pool", "x_bias"))
                yield

            def low_rank(K, b):
                inverse_deviation(K, b, 3)
                pool.wait_ge(*K.ready("scalar", "x_square1"))
                power(K, b.rs, b.ss, None)
                pool.wait_ge(*K.last("pool"))
                nc.gpsimd.tensor_scalar(b.rs, b.rs, 1e12, None, ALU.min).then_inc(*K.step("pool", "f_inverse"))
                yield

            def mom_in(K, b):
                inverse_deviation(K, b, 4)
                pool.wait_ge(*K.last("pool"))
                for k in range(2):
                    nc.gpsimd.memset(b.KE[k][SHIFT:SHIFT + 1, :, :], 1.0).then_inc(*K.step("pool"))
                pool.wait_ge(*K.last("pool"))
                yield

            def mom_low(K, b, h):
                pool.wait_ge(*K.ready("vector", ("ke", h)))
                if h >= 1:
                    pool.wait_ge(*K.ready("tensor", ("as", h - 1, AR - 1)))
                nc.gpsimd.tensor_copy(b.KEB[:, :, :], b.KE[h % 2][0:SHIFT, :, :]).then_inc(*K.step("pool"))
                pool.wait_ge(*K.ready("scalar", ("qe", h)))
                nc.gpsimd.tensor_copy(b.QEB[:, :, :, :].rearrange("p a g t -> p (a g t)"),
                                      b.QE[h % 2][0:SHIFT, :, :, :].rearrange("p a g t -> p (a g t)")).then_inc(
                                          *K.step("pool", ("ke_low", h)))

            def mom_heads(K2):
                for n in range(UNITS):
                    mom_low(*units(K2, n))
                for K in K2:
                    pool.wait_ge(*K.last("pool"))

            def mom_out(K, b):
                yield
                yield
                inverse_deviation(K, b, 5)

            s_c, n = s_pool, 0
            for t, v in ((ident, 0.0), (le, 1.0), (gt, 1.0), (head12, 1.0), (mem3, 1.0), (below, 1.0), (pw, -0.5)):
                nc.gpsimd.memset(t[tuple(slice(None) for _ in t.shape)], v).then_inc(s_c, 1)
                n += 1
            nc.gpsimd.memset(spread[:, :, :], 0.0).then_inc(s_c, 1)
            nc.gpsimd.memset(w_al[:, :, :], 0.0).then_inc(s_fill, 1)
            pool.wait_ge(s_c, n + 1)
            nc.gpsimd.affine_select(out=ident[:, :], in_=ident[:, :], compare_op=ALU.not_equal, fill=1.0, base=0,
                                    pattern=[[-1, P]], channel_multiplier=1).then_inc(s_ident, 1)
            nc.gpsimd.affine_select(out=le[:, :], in_=le[:, :], compare_op=ALU.is_ge, fill=0.0, base=0,
                                    pattern=[[1, P]], channel_multiplier=-1).then_inc(s_c, 1)
            nc.gpsimd.affine_select(out=gt[:, :], in_=gt[:, :], compare_op=ALU.is_gt, fill=0.0, base=0,
                                    pattern=[[-1, P]], channel_multiplier=1).then_inc(s_const, 1)
            nc.gpsimd.affine_select(out=below[:, :, :], in_=below[:, :, :], compare_op=ALU.is_gt, fill=0.0, base=0,
                                    pattern=[[1, 4], [-1, 4]], channel_multiplier=0).then_inc(s_const, 1)
            nc.gpsimd.affine_select(out=spread[:, :, :], in_=spread[:, :, :], compare_op=ALU.not_equal, fill=1.0,
                                    base=0, pattern=[[-3, 2 * AH], [-1, RH], [0, AD]],
                                    channel_multiplier=1).then_inc(s_const, 1)
            for t, m, c in ((head12, XD, HT), (mem3, AD, RH)):
                nc.gpsimd.affine_select(out=t[:, :], in_=t[:, :], compare_op=ALU.is_ge, fill=0.0, base=0,
                                        pattern=[[-m, c]], channel_multiplier=1).then_inc(s_c, 1)
            pool.wait_ge(s_c, n + 4)
            for t, m, c in ((head12, XD, HT), (mem3, AD, RH)):
                nc.gpsimd.affine_select(out=t[:, :], in_=t[:, :], compare_op=ALU.is_ge, fill=0.0, base=m - 1,
                                        pattern=[[m, c]], channel_multiplier=-1).then_inc(s_const, 1)
            pool.wait_ge(w_loaded["small"], 16 * N_SMALL)
            pool.wait_ge(s_const, CONSTS)
            with pool.Fori(0, PAIRS) as turn:
                K2 = keys(turn)
                run(BEFORE_MOM, K2, mamba_in=mamba_in, mamba_ssd=mamba_ssd, mamba_out=mamba_out, rot_in=rot_in,
                    rot_out=rot_out, low_rank=low_rank, mom_in=mom_in)
                mom_heads(K2)
                run(AFTER_MOM, K2, mom_out=mom_out)
                turn_end(pool, turn)
                pool.wait_ge(started, turn + 1)


def grouped_experts(nc, io, out, xall, ident):
    TT = B * NT
    CH = 512
    GS = ME // MG
    SLOTS = 4
    TURNS = ME // SLOTS
    with ExitStack() as ctx:
        def sb(name, shape, dt=F32):
            return ctx.enter_context(nc.sbuf_tensor(name, shape, dt))

        def sem(name):
            return ctx.enter_context(nc.semaphore(name))

        X = xall[:, :, :, :].rearrange("p a b (i d) -> p (a b i) d", d=D)
        XN = sb("g_xn", [P, TT, D])
        XT = sb("g_xT", [P, KD, B * T])
        wr = sb("g_wr", [P, KD, ME])
        rbias = sb("g_rbias", [P, ME])
        wg = sb("g_wg", [P, SLOTS, KD, MI])
        wu = sb("g_wu", [P, SLOTS, KD, MI])
        wd = sb("g_wd", [P, SLOTS, D])
        TH = sb("g_th", [P, 2, CH])
        HH = sb("g_hh", [P, 2, CH])
        bst = sb("g_bst", [P, TT, 6])
        mv = sb("g_mv", [P, TT, 2])
        rstd = sb("g_rstd", [P, TT])
        pw8 = sb("g_pw8", [P, TT])
        sc = sb("g_sc", [P, TT, ME])
        bi = sb("g_bi", [P, TT, ME])
        ta = sb("g_ta", [P, TT, ME])
        tb = sb("g_tb", [P, TT, ME])
        td = sb("g_td", [P, TT, ME])
        comb = sb("g_comb", [P, TT, ME])
        g4 = [sb(f"g_g{n}", [P, TT * MG]) for n in range(6)]
        ga = sb("g_ga", [P, TT, MG, MG])
        gb = sb("g_gb", [P, TT, MG, MG])
        lower = sb("g_lower", [P, MG, MG])
        v8 = sb("g_v8", [P, TT, 8])
        need = sb("g_need", [P, TT])
        tot = sb("g_tot", [P, TT])
        share = sb("g_share", [P, SLOTS, TT])
        psum = ctx.enter_context(nc.psum_tensor("g_psum", [P, 8, 512], F32))

        s_router = sem("g_router_in")
        s_slot = [sem(f"g_slot{j}") for j in range(SLOTS)]
        s_lower = sem("g_lower_made")
        s_stat = sem("g_stat")
        s_rstd = sem("g_rstd_made")
        s_xn = sem("g_xn_made")
        s_turn = sem("g_turned")
        s_xT = sem("g_xT_made")
        s_logit = sem("g_logits")
        s_sig = sem("g_exp")
        s_seq = sem("g_vector_seq")
        s_comb = sem("g_comb_made")
        s_gu = sem("g_gate_up")
        s_th = sem("g_tanh")
        s_half = sem("g_half")
        s_hh = sem("g_hidden")
        s_down = sem("g_down")
        s_acc = sem("g_added")
        s_out = sem("g_out")

        block = ctx.enter_context(nc.Block())


        @block.sync
        def _(sp):
            sp.dma_start(wr[:, :, :], io["L1_ffn_router_w"].rearrange("(k p) n -> p k n", p=P)).then_inc(s_router, 16)
            sp.dma_start(rbias[:, :], io["L1_ffn_router_bias"].partition_broadcast(P)).then_inc(s_router, 16)
            for m in range(MSH):
                j = SLOTS - MSH + m
                c = slice(m * MI, (m + 1) * MI)
                sp.dma_start(wg[:, j, :, :], io["L1_ffn_sw_gate"][:, c].rearrange("(k p) n -> p k n", p=P)).then_inc(
                    s_slot[j], 16)
                sp.dma_start(wu[:, j, :, :], io["L1_ffn_sw_up"][:, c].rearrange("(k p) n -> p k n", p=P)).then_inc(
                    s_slot[j], 16)
                sp.dma_start(wd[:, j, :], io["L1_ffn_sw_down"][c, :]).then_inc(s_slot[j], 16)

            def load(e, j):
                sp.dma_start(wg[:, j, :, :], io["w_gate_tiles"][e]).then_inc(s_slot[j], 16)
                sp.dma_start(wu[:, j, :, :], io["w_up_tiles"][e]).then_inc(s_slot[j], 16)
                sp.dma_start(wd[:, j, :], io["L1_ffn_w_down"][e]).then_inc(s_slot[j], 16)

            for j in range(SLOTS):
                if j >= SLOTS - MSH:
                    sp.wait_ge(s_down, 4 * (MSH + j - SLOTS + 1))
                load(j, j)
            with sp.Fori(1, TURNS) as turn:
                for j in range(SLOTS):
                    sp.wait_ge(s_down, turn * 4 * SLOTS + 4 * (MSH + j - SLOTS + 1))
                    load(turn * SLOTS + j, j)
            sp.wait_ge(s_acc, 4 * (MSH + ME))
            for b in range(B):
                sp.dma_start(out[b].rearrange("(i p) d -> p i d", p=P), X[:, NT * b:NT * (b + 1), :]).then_inc(
                    s_out, 16)
            sp.wait_ge(s_out, 16 * B)

        def program(turn):
            return [(j, turn * 2 * SLOTS + 2 * (MSH + j)) for j in range(SLOTS)]

        SHARED = [(SLOTS - MSH + m, 2 * m) for m in range(MSH)]

        @block.scalar
        def _(act):
            for q in range(TT // 2):
                act.wait_ge(s_turn, q + 1)
                nc.scalar.copy(XT[:, :, 2 * P * q:2 * P * (q + 1)], psum[:, q, :].rearrange("p (k t) -> p k t", k=KD)
                               ).then_inc(s_xT, 1)
            act.wait_ge(s_logit, 1)
            nc.scalar.activation(sc[:, :, :].rearrange("p t e -> p (t e)"), psum[:, 4, 0:TT * ME], ACT.Exp,
                                 scale=-1.0).then_inc(s_sig, 1)

            def tanh(n, c, first=False):
                act.wait_ge(s_gu, n + 1)
                if not first:
                    act.wait_ge(s_hh, n - 1)
                nc.scalar.activation(TH[:, c, :], psum[:, 2 * c, :], ACT.Tanh, scale=0.5).then_inc(s_th, 1)

            for j, n in SHARED:
                for c in range(2):
                    tanh(n + c, c, n == 0)
            with act.Fori(0, TURNS) as turn:
                for j, n in program(turn):
                    for c in range(2):
                        tanh(n + c, c)

        @block.tensor
        def _(pe):
            for q in range(TT // 2):
                pe.wait_ge(s_xn, 2 * q + 2)
                for k in range(KD):
                    for i in range(2):
                        last = nc.tensor.transpose(psum[:, q, (2 * k + i) * P:(2 * k + i + 1) * P],
                                                   XN[:, 2 * q + i, k * P:(k + 1) * P], ident[:, :])
                last.then_inc(s_turn, 1)
            pe.wait_ge(s_router, 32)
            pe.wait_ge(s_xT, TT // 2)
            for t in range(TT):
                for k in range(KD):
                    last = nc.tensor.matmul(psum[:, 4, t * ME:(t + 1) * ME], XT[:, k, t * P:(t + 1) * P], wr[:, k, :],
                                            start=(k == 0), stop=(k == KD - 1))
            last.then_inc(s_logit, 1)
            pe.wait_ge(s_sig, 1)

            def gate_up(j, n, c, first=False):
                if not first:
                    pe.wait_ge(s_hh, n - 1)
                for bank, w in ((2 * c, wg), (2 * c + 1, wu)):
                    for k in range(KD):
                        last = nc.tensor.matmul(psum[:, bank, :], w[:, j, k, :], XT[:, k, c * CH:(c + 1) * CH],
                                                start=(k == 0), stop=(k == KD - 1))
                last.then_inc(s_gu, 1)

            def down(j, n, c, first=False):
                pe.wait_ge(s_hh, n + 1)
                for q in range(2):
                    if not first:
                        pe.wait_ge(s_acc, 2 * n - 3 + q)
                    for i in range(2):
                        t = 2 * q + i
                        last = nc.tensor.matmul(psum[:, 4 + 2 * c + q, i * D:(i + 1) * D],
                                                HH[:, c, t * P:(t + 1) * P], wd[:, j, :], start=True, stop=True)
                    last.then_inc(s_down, 1)

            for j, n in SHARED:
                pe.wait_ge(s_slot[j], 48)
                gate_up(j, n, 0, n == 0)
                if n > 0:
                    down(j - 1, n - 1, 1, n - 1 == 1)
                gate_up(j, n + 1, 1, n == 0)
                down(j, n, 0, n == 0)
            with pe.Fori(0, TURNS) as turn:
                for j, n in program(turn):
                    pe.wait_ge(s_slot[j], turn * 48 + (96 if j >= SLOTS - MSH else 48))
                    gate_up(j, n, 0)
                    down((j - 1) % SLOTS, n - 1, 1)
                    gate_up(j, n + 1, 1)
                    down(j, n, 0)
            down(SLOTS - 1, 2 * (MSH + ME) - 1, 1)

        @block.gpsimd
        def _(pool):
            nc.gpsimd.memset(lower[:, :, :], 1.0).then_inc(s_lower, 1)
            nc.gpsimd.memset(pw8[:, :], -0.5).then_inc(s_lower, 1)
            pool.wait_ge(s_lower, 2)
            nc.gpsimd.affine_select(out=lower[:, :, :], in_=lower[:, :, :], compare_op=ALU.is_gt, fill=0.0, base=0,
                                    pattern=[[1, MG], [-1, MG]], channel_multiplier=0).then_inc(s_lower, 1)
            pool.wait_ge(s_stat, TT)
            nc.gpsimd.tensor_scalar(rstd[:, :], mv[:, :, 1], 1e-5, None, ALU.add).then_inc(s_rstd, 1)
            pool.wait_ge(s_rstd, 1)
            nc.gpsimd.tensor_tensor(rstd[:, :], rstd[:, :], pw8[:, :], ALU.pow).then_inc(s_rstd, 1)

        @block.vector
        def _(dve):
            seq = [0]

            def chain(instruction):
                seq[0] += 1
                instruction.then_inc(s_seq, 1)
                dve.wait_ge(s_seq, seq[0])

            def hidden(n, c, first=False):
                dve.wait_ge(s_th, n + 1)
                if not first:
                    dve.wait_ge(s_down, 2 * n - 2)
                nc.vector.scalar_tensor_tensor(out=HH[:, c, :], in0=TH[:, c, :], scalar=1.0, in1=psum[:, 2 * c, :],
                                               op0=ALU.add, op1=ALU.mult).then_inc(s_half, 1)
                dve.wait_ge(s_half, n + 1)
                nc.vector.tensor_tensor(HH[:, c, :], HH[:, c, :], psum[:, 2 * c + 1, :], ALU.mult).then_inc(s_hh, 1)

            for t in range(TT):
                nc.vector.bn_stats(bst[:, t, :], X[:, t, :]).then_inc(s_seq, 1)
                seq[0] += 1
            dve.wait_ge(s_seq, seq[0])
            for t in range(TT):
                nc.vector.bn_aggr(mv[:, t, :], bst[:, t, :]).then_inc(s_stat, 1)
            dve.wait_ge(s_stat, TT)
            dve.wait_ge(s_rstd, 2)
            for t in range(TT):
                nc.vector.tensor_scalar(XN[:, t, :], X[:, t, :], mv[:, t, 0:1], rstd[:, t:t + 1], ALU.subtract,
                                        ALU.mult).then_inc(s_xn, 1)
            dve.wait_ge(s_sig, 1)
            chain(nc.vector.tensor_scalar(sc[:, :, :], sc[:, :, :], 1.0, None, ALU.add))
            chain(nc.vector.reciprocal(sc[:, :, :], sc[:, :, :]))
            dve.wait_ge(s_router, 32)
            chain(nc.vector.tensor_tensor(bi[:, :, :], sc[:, :, :], rbias[:, :].unsqueeze(1).broadcast_to([P, TT, ME]),
                                          ALU.add))
            q = bi[:, :, :].rearrange("p t (g n) -> p (t g) n", n=GS)
            hi1, lo1, hi2, lo2, top, nxt = g4
            nc.vector.tensor_tensor(hi1[:, :], q[:, :, 0], q[:, :, 1], ALU.max)
            nc.vector.tensor_tensor(lo1[:, :], q[:, :, 0], q[:, :, 1], ALU.min)
            nc.vector.tensor_tensor(hi2[:, :], q[:, :, 2], q[:, :, 3], ALU.max)
            chain(nc.vector.tensor_tensor(lo2[:, :], q[:, :, 2], q[:, :, 3], ALU.min))
            nc.vector.tensor_tensor(top[:, :], hi1[:, :], hi2[:, :], ALU.max)
            nc.vector.tensor_tensor(nxt[:, :], hi1[:, :], hi2[:, :], ALU.min)
            chain(nc.vector.tensor_tensor(lo1[:, :], lo1[:, :], lo2[:, :], ALU.max))
            chain(nc.vector.tensor_tensor(nxt[:, :], nxt[:, :], lo1[:, :], ALU.max))
            chain(nc.vector.tensor_tensor(top[:, :], top[:, :], nxt[:, :], ALU.add))
            hidden(0, 0, first=True)
            dve.wait_ge(s_lower, 3)
            score = top[:, :].rearrange("p (t g) -> p t g", g=MG)
            mine = score.unsqueeze(3).broadcast_to([P, TT, MG, MG])
            other = score.unsqueeze(2).broadcast_to([P, TT, MG, MG])
            nc.vector.tensor_tensor(ga[:, :, :, :], other, mine, ALU.is_gt)
            chain(nc.vector.tensor_tensor(gb[:, :, :, :], other, mine, ALU.is_equal))
            chain(nc.vector.tensor_tensor(gb[:, :, :, :].rearrange("p t a b -> p t (a b)"),
                                          gb[:, :, :, :].rearrange("p t a b -> p t (a b)"),
                                          lower[:, :, :].rearrange("p a b -> p (a b)").unsqueeze(1).broadcast_to(
                                              [P, TT, MG * MG]), ALU.mult))
            chain(nc.vector.tensor_tensor(ga[:, :, :, :], ga[:, :, :, :], gb[:, :, :, :], ALU.add))
            chain(nc.vector.tensor_reduce(hi1[:, :].rearrange("p (t g) -> p t g", g=MG), ga[:, :, :, :], AX.X, ALU.add))
            chain(nc.vector.tensor_scalar(hi1[:, :], hi1[:, :], MTG - 0.5, None, ALU.is_lt))
            chain(nc.vector.tensor_tensor(q, q, hi1[:, :].unsqueeze(2).broadcast_to([P, TT * MG, GS]), ALU.mult))
            for t in range(TT):
                nc.vector.max(v8[:, t, :], bi[:, t, :]).then_inc(s_seq, 1)
                seq[0] += 1
            dve.wait_ge(s_seq, seq[0])
            hidden(1, 1, first=True)
            eighth = v8[:, :, 7:8].broadcast_to([P, TT, ME])
            nc.vector.tensor_tensor(ta[:, :, :], bi[:, :, :], eighth, ALU.is_gt)
            chain(nc.vector.tensor_tensor(tb[:, :, :], bi[:, :, :], eighth, ALU.is_equal))
            nc.vector.tensor_reduce(need[:, :], ta[:, :, :], AX.X, ALU.add).then_inc(s_seq, 1)
            seq[0] += 1
            for t in range(TT):
                nc.vector.tensor_tensor_scan(td[:, t, :], tb[:, t, :], tb[:, t, :], 0.0, ALU.add,
                                             ALU.max).then_inc(s_seq, 1)
                seq[0] += 1
            dve.wait_ge(s_seq, seq[0])
            chain(nc.vector.tensor_tensor(td[:, :, :], td[:, :, :], need[:, :].unsqueeze(2).broadcast_to([P, TT, ME]),
                                          ALU.add))
            chain(nc.vector.scalar_tensor_tensor(out=tb[:, :, :], in0=td[:, :, :], scalar=MTK + 0.5, in1=tb[:, :, :],
                                                 op0=ALU.is_lt, op1=ALU.mult))
            chain(nc.vector.tensor_tensor(ta[:, :, :], ta[:, :, :], tb[:, :, :], ALU.add))
            chain(nc.vector.tensor_tensor(ta[:, :, :], ta[:, :, :], sc[:, :, :], ALU.mult))
            chain(nc.vector.tensor_reduce(tot[:, :], ta[:, :, :], AX.X, ALU.add))
            chain(nc.vector.reciprocal(tot[:, :], tot[:, :]))
            chain(nc.vector.tensor_scalar(tot[:, :], tot[:, :], 0.5 * ROUTED_SCALE, None, ALU.mult))
            chain(nc.vector.tensor_tensor(comb[:, :, :], ta[:, :, :], tot[:, :].unsqueeze(2).broadcast_to([P, TT, ME]),
                                          ALU.mult))

            def add(n, c, scale):
                for q in range(2):
                    dve.wait_ge(s_down, 2 * n + 1 + q)
                    for i in range(2):
                        t = 4 * c + 2 * q + i
                        last = nc.vector.scalar_tensor_tensor(
                            out=X[:, t, :], in0=psum[:, 4 + 2 * c + q, i * D:(i + 1) * D],
                            scalar=0.5 if scale is None else share[:, scale, t:t + 1], in1=X[:, t, :], op0=ALU.mult,
                            op1=ALU.add)
                    last.then_inc(s_acc, 1)

            def shares(turn, j):
                nc.vector.tensor_copy(share[:, j, :], comb[:, :, turn * SLOTS + j])

            for j, n in SHARED:
                if n > 0:
                    hidden(n, 0)
                    add(n - 1, 1, None)
                    hidden(n + 1, 1)
                add(n, 0, None)
            nc.vector.memset(share[:, SLOTS - 1, :], 0.5)
            with dve.Fori(0, TURNS) as turn:
                for j, n in program(turn):
                    hidden(n, 0)
                    add(n - 1, 1, (j - 1) % SLOTS)
                    shares(turn, j)
                    hidden(n + 1, 1)
                    add(n, 0, j)
            add(2 * (MSH + ME) - 1, 1, SLOTS - 1)


def views(a):
    io = dict(a)
    io["x"] = a["x"].rearrange("(t s) (i p) d -> s t p i d", s=STREAMS, p=P)
    io["ctx"] = a["ctx_t"].rearrange("(t s) c n -> s t c n", s=STREAMS)
    io["pos"] = a["fside_BxSx2_0"].rearrange("b (i p) c -> p (b i) c", p=P)
    for n, m in (("wq_exp", "L1_attn_Wq_exp"), ("wk_exp", "L1_attn_Wk_exp")):
        io[n] = a[m].rearrange("(k a) d e -> k (a d) e", k=KD)
    for n, m in (("w_gate_tiles", "L1_ffn_w_gate"), ("w_up_tiles", "L1_ffn_w_up")):
        io[n] = a[m].rearrange("e (k p) n -> e p k n", p=P)
    return io


def declare(nc, shapes):
    a = {n: nc.dram_tensor(f"in_{n}_dram", s, F32, kind="ExternalInput").ap() for n, s in shapes.items()}
    return views(a), nc.dram_tensor("out_0_dram", (B, T, D), F32, kind="ExternalOutput").ap()


def program(nc, trial, shapes):
    plan = Plan()
    build(trial, plan, *declare(trial, shapes))
    plan.final = True
    build(nc, plan, *declare(nc, shapes))


def kernel(**inputs):
    import numpy as np
    import concourse.bacc as bacc
    from concourse.bass_utils import run_bass_kernel_spmd

    def columns(v, *rest):
        n = v.shape[0] // P
        return np.ascontiguousarray(np.moveaxis(v.reshape(n, P, *rest), 0, 1))

    a = {n: np.ascontiguousarray(v) for n, v in inputs.items()}
    a["ctx_t"] = np.ascontiguousarray(np.transpose(a.pop("ctx_1024"), (0, 2, 1)))
    a["norm1"] = columns(a.pop("L0_attn_norm1_w"))
    a["norm2"] = columns(a.pop("L0_attn_norm2_w"))
    a["mixn"] = columns(a.pop("L0_attn_mixer_norm_w"))
    a["conv_w"] = columns(a.pop("L0_attn_conv_w"), 4)
    a["conv_b"] = columns(a.pop("L0_attn_conv_b"))
    a["wq_t"] = np.ascontiguousarray(a.pop("L1_xattn_Wq").T)
    a["wk_t"] = np.ascontiguousarray(a.pop("L1_xattn_Wk").T)
    a["bq"] = a.pop("L1_xattn_bq").reshape(P, 1)
    a["bk"] = a.pop("L1_xattn_bk").reshape(P, 1)
    nc, trial = (bacc.Bacc("TRN2", target_bir_lowering=False, num_devices=1) for _ in range(2))
    program(nc, trial, {n: v.shape for n, v in a.items()})
    r = run_bass_kernel_spmd(nc, [{f"in_{n}_dram": v for n, v in a.items()}], core_ids=[0])
    return r.results[0]["out_0_dram"]
```
